# Optimizing a Trainium2 kernel written in Bass

```python
import numpy as np
import jax
import jax.numpy as jnp

def _softmax(x, axis=-1):
    return jax.nn.softmax(x, axis=axis)

def _gelu(x):
    return jax.nn.gelu(x, approximate=True)

def _silu(x):
    return jax.nn.silu(x)

def _sigmoid(x):
    return jax.nn.sigmoid(x)

def _layernorm(x, axis=-1, eps=1e-05):
    m = jnp.mean(x, axis=axis, keepdims=True)
    v = jnp.var(x, axis=axis, keepdims=True)
    return (x - m) / jnp.sqrt(v + eps)

def _scatter_add(tgt, idx, src, axis=0):
    return tgt.at[idx].add(src)

def _segment_sum(src, seg, n):
    return jax.ops.segment_sum(src, seg, n)
kernel_name = 'mk_gps_d1_gnn_r8_efec53'

def setup_inputs(seed: int=0):
    np.random.seed(seed)
    _w = jnp.asarray

    def _rec_inputs():
        import jax
        import jax.numpy as jnp
        _gk = jax.random.key(seed)
        x = -0.0003019 + 1 * jax.random.normal(jax.random.fold_in(_gk, 1), (1250, 1024), jnp.float32)
        src = jax.random.randint(jax.random.fold_in(_gk, 2), (20000,), 0, 1250, jnp.int32)
        dst = jnp.minimum((1250 * jax.random.uniform(jax.random.fold_in(_gk, 3), (20000,)) ** 2.0).astype(jnp.int32), 9999)
        _o = jnp.argsort(dst, stable=True)
        src = src[_o]
        dst = dst[_o]
        return (x, src, dst)
    x, src, dst = _rec_inputs()

    def _L0_gnn_setup():
        import jax, jax.numpy as jnp
        import numpy as np
        N = 2500
        E = 40000
        D_IN = 1024
        D_OUT = 1024
        key = jax.random.key(seed)
        k1, k2, k3, k4 = jax.random.split(key, 4)
        x = jax.random.normal(k1, (N, D_IN), dtype=jnp.float32)
        edge_index = jax.random.randint(k2, (2, E), 0, N, dtype=jnp.int64)
        W = jax.random.normal(k3, (D_OUT, D_IN), dtype=jnp.float32) * (1.0 / np.sqrt(D_IN))
        b = jax.random.normal(k4, (D_OUT,), dtype=jnp.float32) * 0.01
        return {'x': x, 'edge_index': edge_index, 'W': W, 'b': b}
    _L0_gnn_all = _L0_gnn_setup()
    _L0_gnn_in = {k: v for k, v in _L0_gnn_all.items() if k in ('W', 'b')}
    del _L0_gnn_all

    def _L0_mix_setup():
        import jax, jax.numpy as jnp
        import numpy as np
        import math
        DIM = 1024
        H = 16
        HD = DIM // H
        M = 64
        B, S = (4, 512)

        def _feature_map(t, P):
            proj = jnp.einsum('bhsd,hmd->bhsm', t, P)
            return jax.nn.relu(proj) * (1.0 / math.sqrt(P.shape[1]))
        key = jax.random.key(seed)
        ks = jax.random.split(key, 10)
        sc = 1.0 / math.sqrt(DIM)
        return {'x': jax.random.normal(ks[0], (B, S, DIM), dtype=jnp.float32), 'Wq': jax.random.normal(ks[1], (DIM, DIM), dtype=jnp.float32) * sc, 'bq': jax.random.normal(ks[2], (DIM,), dtype=jnp.float32) * 0.01, 'Wk': jax.random.normal(ks[3], (DIM, DIM), dtype=jnp.float32) * sc, 'bk': jax.random.normal(ks[4], (DIM,), dtype=jnp.float32) * 0.01, 'Wv': jax.random.normal(ks[5], (DIM, DIM), dtype=jnp.float32) * sc, 'bv': jax.random.normal(ks[6], (DIM,), dtype=jnp.float32) * 0.01, 'Wo': jax.random.normal(ks[7], (DIM, DIM), dtype=jnp.float32) * sc, 'bo': jax.random.normal(ks[8], (DIM,), dtype=jnp.float32) * 0.01, 'P': jax.random.normal(ks[9], (H, M, HD), dtype=jnp.float32)}
    _L0_mix_all = _L0_mix_setup()
    _L0_mix_in = {k: v for k, v in _L0_mix_all.items() if k in ('Wq', 'bq', 'Wk', 'bk', 'Wv', 'bv', 'Wo', 'bo', 'P')}
    del _L0_mix_all

    def _L0_ffn_setup():
        import jax, jax.numpy as jnp
        import numpy as np
        import math
        GOLDEN_CENTER = 1.0 / math.e
        GOLDEN_LOWER = 0.5 - math.log(4.0 / 3.0)
        GOLDEN_UPPER = 0.5
        B, T, D = (4, 256, 1024)
        E = 8
        I = 512 // (E // 2)

        def _routing_weights(x, Wr, temperature):
            inh = jax.nn.sigmoid(x @ Wr / temperature)
            in_zone = (inh >= GOLDEN_LOWER) & (inh <= GOLDEN_UPPER)
            dist = jnp.abs(inh - GOLDEN_CENTER)
            w = jnp.exp(-dist / 0.1) * in_zone.astype(x.dtype)
            wsum = w.sum(axis=-1, keepdims=True)
            no_expert = wsum < 1e-08
            fb = jnp.exp(-dist / 0.3)
            _, top2 = jax.lax.top_k(fb, 2)
            fb_mask = jax.nn.one_hot(top2, E, dtype=x.dtype).sum(axis=-2)
            fb_w = fb * fb_mask
            fb_w = fb_w / jnp.clip(fb_w.sum(axis=-1, keepdims=True), 1e-08)
            w = jnp.where(no_expert, fb_w, w)
            wsum = w.sum(axis=-1, keepdims=True)
            return w / jnp.clip(wsum, 1e-08)
        key = jax.random.key(seed)
        k = jax.random.split(key, 6)
        s_d = 1.0 / math.sqrt(D)
        s_i = 1.0 / math.sqrt(I)
        return {'x': jax.random.normal(k[0], (B, T, D), jnp.float32), 'Wg': jax.random.normal(k[1], (E, D, I), jnp.float32) * s_d, 'Wu': jax.random.normal(k[2], (E, D, I), jnp.float32) * s_d, 'Wd': jax.random.normal(k[3], (E, I, D), jnp.float32) * s_i, 'Wr': jax.random.normal(k[4], (D, E), jnp.float32) * s_d, 'temperature': jnp.ones((1,), jnp.float32)}
    _L0_ffn_all = _L0_ffn_setup()
    _L0_ffn_in = {k: v for k, v in _L0_ffn_all.items() if k in ('Wg', 'Wu', 'Wd', 'Wr', 'temperature')}
    del _L0_ffn_all
    return {'x': x, 'src': src, 'dst': dst, 'L0_gnn_W': _L0_gnn_in['W'], 'L0_gnn_b': _L0_gnn_in['b'], 'L0_mix_Wq': _L0_mix_in['Wq'], 'L0_mix_bq': _L0_mix_in['bq'], 'L0_mix_Wk': _L0_mix_in['Wk'], 'L0_mix_bk': _L0_mix_in['bk'], 'L0_mix_Wv': _L0_mix_in['Wv'], 'L0_mix_bv': _L0_mix_in['bv'], 'L0_mix_Wo': _L0_mix_in['Wo'], 'L0_mix_bo': _L0_mix_in['bo'], 'L0_mix_P': _L0_mix_in['P'], 'L0_ffn_Wg': _L0_ffn_in['Wg'], 'L0_ffn_Wu': _L0_ffn_in['Wu'], 'L0_ffn_Wd': _L0_ffn_in['Wd'], 'L0_ffn_Wr': _L0_ffn_in['Wr'], 'L0_ffn_temperature': _L0_ffn_in['temperature']}

def reference(x, src, dst, L0_gnn_W, L0_gnn_b, L0_mix_Wq, L0_mix_bq, L0_mix_Wk, L0_mix_bk, L0_mix_Wv, L0_mix_bv, L0_mix_Wo, L0_mix_bo, L0_mix_P, L0_ffn_Wg, L0_ffn_Wu, L0_ffn_Wd, L0_ffn_Wr, L0_ffn_temperature):
    import jax
    import jax.numpy as jnp

    def _L0_gnn_ref(x, edge_index, W, b):
        import jax, jax.numpy as jnp
        import numpy as np
        N = 2500
        E = 40000
        D_IN = 1024
        D_OUT = 1024
        num_nodes = x.shape[0]
        self_idx = jnp.arange(num_nodes, dtype=edge_index.dtype)
        ei = jnp.concatenate([edge_index, jnp.stack([self_idx, self_idx], axis=0)], axis=1)
        row, col = (ei[0], ei[1])
        h = jnp.einsum('nd,od->no', x, W) + b
        deg = jnp.zeros((num_nodes,), dtype=h.dtype).at[row].add(1.0)
        deg_inv_sqrt = deg ** (-0.5)
        norm = deg_inv_sqrt[row] * deg_inv_sqrt[col]
        msg = norm[:, None] * h[col]
        out = jax.ops.segment_sum(msg, row, num_segments=num_nodes)
        return out

    def _L0_mix_ref(x, Wq, bq, Wk, bk, Wv, bv, Wo, bo, P):
        import jax, jax.numpy as jnp
        import numpy as np
        import math
        DIM = 1024
        H = 16
        HD = DIM // H
        M = 64
        B, S = (4, 512)

        def _feature_map(t, P):
            proj = jnp.einsum('bhsd,hmd->bhsm', t, P)
            return jax.nn.relu(proj) * (1.0 / math.sqrt(P.shape[1]))
        b, s, dim = x.shape
        h, m, hd = P.shape

        def split_heads(y):
            return y.reshape(b, s, h, hd).transpose(0, 2, 1, 3)
        q = split_heads(x @ Wq.T + bq)
        k = split_heads(x @ Wk.T + bk)
        v = split_heads(x @ Wv.T + bv)
        q_prime = _feature_map(q, P)
        k_prime = _feature_map(k, P)
        kv = jnp.einsum('bhsm,bhsd->bhmd', k_prime, v)
        attn = jnp.einsum('bhsm,bhmd->bhsd', q_prime, kv)
        attn = attn.transpose(0, 2, 1, 3).reshape(b, s, dim)
        return attn @ Wo.T + bo

    def _L0_ffn_ref(x, Wg, Wu, Wd, Wr, temperature):
        import jax, jax.numpy as jnp
        import numpy as np
        import math
        GOLDEN_CENTER = 1.0 / math.e
        GOLDEN_LOWER = 0.5 - math.log(4.0 / 3.0)
        GOLDEN_UPPER = 0.5
        B, T, D = (4, 256, 1024)
        E = 8
        I = 512 // (E // 2)

        def _routing_weights(x, Wr, temperature):
            inh = jax.nn.sigmoid(x @ Wr / temperature)
            in_zone = (inh >= GOLDEN_LOWER) & (inh <= GOLDEN_UPPER)
            dist = jnp.abs(inh - GOLDEN_CENTER)
            w = jnp.exp(-dist / 0.1) * in_zone.astype(x.dtype)
            wsum = w.sum(axis=-1, keepdims=True)
            no_expert = wsum < 1e-08
            fb = jnp.exp(-dist / 0.3)
            _, top2 = jax.lax.top_k(fb, 2)
            fb_mask = jax.nn.one_hot(top2, E, dtype=x.dtype).sum(axis=-2)
            fb_w = fb * fb_mask
            fb_w = fb_w / jnp.clip(fb_w.sum(axis=-1, keepdims=True), 1e-08)
            w = jnp.where(no_expert, fb_w, w)
            wsum = w.sum(axis=-1, keepdims=True)
            return w / jnp.clip(wsum, 1e-08)
        weights = _routing_weights(x, Wr, temperature)
        gate = jnp.einsum('btd,edi->beti', x, Wg)
        up = jnp.einsum('btd,edi->beti', x, Wu)
        h = jax.nn.silu(gate) * up
        e_out = jnp.einsum('beti,eid->betd', h, Wd)
        out = jnp.einsum('bte,betd->btd', weights, e_out)
        return out
    edge_index = jnp.stack([src, dst])
    xn = _layernorm(x, axis=-1)
    x = x + _L0_gnn_ref(xn, edge_index, L0_gnn_W, L0_gnn_b) + _L0_mix_ref(xn[None], L0_mix_Wq, L0_mix_bq, L0_mix_Wk, L0_mix_bk, L0_mix_Wv, L0_mix_bv, L0_mix_Wo, L0_mix_bo, L0_mix_P)[0]
    x = x + _L0_ffn_ref(_layernorm(x, axis=-1)[None], L0_ffn_Wg, L0_ffn_Wu, L0_ffn_Wd, L0_ffn_Wr, L0_ffn_temperature)[0]
    return x

_drawn_inputs = setup_inputs


def setup_inputs(seed=0):
    import zlib

    import numpy as np

    out = dict(_drawn_inputs(seed))
    spreads = {}
    factors = {'L0_gnn_W': 8.0,
     'L0_gnn_b': 46.612,
     'L0_mix_bq': 8.0,
     'L0_mix_bk': 8.0,
     'L0_mix_bo': 54.088,
     'L0_ffn_Wg': 8.0,
     'L0_ffn_Wu': 8.0,
     'L0_ffn_Wd': 8.0,
     'L0_ffn_Wr': 8.0}
    for name, (base, spread) in spreads.items():
        noise = np.random.default_rng([zlib.crc32(name.encode()), seed]).standard_normal(out[name].shape)
        drawn = base * np.exp(spread * noise) if base else spread * noise
        out[name] = jnp.asarray(drawn.astype(out[name].dtype))
    for name, factor in factors.items():
        out[name] = (out[name] * factor).astype(out[name].dtype)
    return out
```

```python
from contextlib import ExitStack

import concourse.bass as bass
from concourse import mybir

F32 = mybir.dt.float32
F32R = mybir.dt.float32r
F16 = mybir.dt.float16
I32 = mybir.dt.int32
ALU = mybir.AluOpType
ACT = mybir.ActivationFunctionType
AX_X = mybir.AxisListType.X
RMAX = bass.bass_isa.ReduceOp.max

P = 128
N = 1250
D = 1024
NT = (N + P - 1) // P
NP = NT * P
NL = NT // 2
KC = D // P
W = D // 2
BANK = 512
HD = 64
E_EDGES = 20000
NPAIR = (E_EDGES + 2 * P - 1) // (2 * P)
NCH = 2 * NPAIR
NEXP = 8
XH = NEXP // 2
WIDE = 2 * NP - P
EPS = 1e-5
PIECE = 1024
NPIECE = 2 * KC * W // PIECE
EXACT_COUNT = 2048
ZONE_LOW = -1.31100973754
ZONE_HIGH = 1.1e-7
CENTER = 0.36787944117144233

KB = 1024
BASE = 16512
OFF_A = BASE
OFF_B = OFF_A + 80 * KB
OFF_E = OFF_A + 64 * KB
OFF_AF = OFF_B + 64 * KB
OFF_AH = OFF_AF + 8 * KB
OFF_AL = OFF_AH + 8 * KB
OFF_TA = OFF_AL + 8 * KB
OFF_TB = OFF_TA + 8 * KB
OFF_OT = OFF_TB + 8 * KB
OFF_BIAS = OFF_OT + 8 * KB
OFF_STG = OFF_BIAS + 4 * KB
OFF_SM = OFF_STG + 10 * KB


def gps_layer(nc, x, src, dst, wk_nat, wq_nat, pbd, bk_col, bq_col, wv_pan, bv, wh_pan, bh, wo_t, bo,
              wgu_pan, wd_pan, wr_t, temp, out):
    ctx = ExitStack()
    with ctx:
        def at(name, shape, dt, off):
            return nc.alloc_sbuf_tensor_at(name, shape, dt, offset=off)

        def sem(name):
            return ctx.enter_context(nc.semaphore(name))

        def dram(name, shape, dt=F32):
            return nc.dram_tensor(name, shape, dt, kind="Internal").ap()

        xnT_d = dram("xnT_d", [NT, P, D])
        qT_d = dram("qT_d", [NT, P, D])
        x1_d = dram("x1_d", [NT, P, D])
        x2T_d = dram("x2T_d", [NT, P, D])
        hT_d = dram("hT_d", [NT, P, D])
        kfold_d = dram("kfold_d", [2, P, KC, W])
        qfold_d = dram("qfold_d", [2, P, KC, W])
        m_d = dram("m_d", [2, P, KC, W])
        fbias_d = dram("fbias_d", [2, D])
        chi_d = dram("chi_d", [NT, P, NP])
        clo_d = dram("clo_d", [NT, P, NP])

        panA = [at("panA_hi", [P, 2, KC, W], F32R, OFF_A), at("panA_lo", [P, 2, KC, W], F32R, OFF_A + 32 * KB)]
        panB = [at("panB_hi", [P, 2, KC, W], F32R, OFF_B), at("panB_lo", [P, 2, KC, W], F32R, OFF_B + 32 * KB)]
        hp = [at("hp_hi", [P, NT, D], F32R, OFF_A), at("hp_lo", [P, NT, D], F32R, OFF_A + 40 * KB)]
        actF = at("actF", [P, 2, D], F32, OFF_AF)
        actH = at("actH", [P, 2, D], F32R, OFF_AH)
        actL = at("actL", [P, 2, D], F32R, OFF_AL)
        tokA = at("tokA", [P, 2, D], F32, OFF_TA)
        tokB = at("tokB", [P, 2, D], F32, OFF_TB)
        outT = at("outT", [P, 2, D], F32, OFF_OT)
        woP = at("woP", [P, 2, D], F32, OFF_OT)
        bias = at("bias", [P, D], F32, OFF_BIAS)
        stage = at("stage", [P, 2, PIECE], F32, OFF_STG)
        cHi = at("cHi", [P, 2, NT, P], F32R, OFF_STG)
        cLo = at("cLo", [P, NT, P], F32R, OFF_TB + 4 * KB)
        small = [OFF_SM]

        def sm(name, cols, dt=F32, size=4):
            off = small[0]
            small[0] += (cols * size + 31) // 32 * 32
            return at(name, [P, cols], dt, off)

        ident = sm("ident", P)
        wr = sm("wr", KC * NEXP)
        zlog = sm("zlog", NT * NEXP)
        wexp = sm("wexp", NT * NEXP)
        dis = sm("dis", NT)
        vscale = sm("vscale", NT)
        tmp_t = sm("tmp_t", 2)
        st6 = sm("st6", 12)
        mv = sm("mv", 2)
        nrm = sm("nrm", 8)
        degi = sm("degi", 2)
        flag = sm("flag", 1, I32)
        assert small[0] <= 229368

        wk_s = at("wk_s", [P, KC, D], F32, OFF_A)
        wq_s = at("wq_s", [P, KC, D], F32, OFF_A + 32 * KB)
        kvT = at("kvT", [P, 4, P], F32, OFF_TB + 2 * KB)
        o = OFF_B
        ph0 = {}
        for name, shape, dt, size in (
                ("pbd_s", [P, KC, P], F32, 4), ("fold", [P, 2, W], F32, 4),
                ("bkq", [P, 2 * KC], F32, 4), ("frow", [P, 2 * D], F32, 4),
                ("srcI", [P, NCH], I32, 4), ("dstI", [P, NCH], I32, 4), ("srcF", [P, NCH], F32, 4),
                ("dstF", [P, NCH], F32, 4), ("iota", [P, NP], F16, 2), ("rowid", [P, NT], F32, 4),
                ("ge", [P, NT + 1, NCH], F16, 2), ("inT", [P, NT, NCH], F16, 2), ("ones16", [P, 2], F16, 2),
                ("id16", [P, P], F16, 2), ("wide", [P, WIDE], F16, 2), ("pres", [1, NT, NPAIR], F32, 4), ("up", [1, NT, NPAIR], F32, 4),
                ("down", [1, NT, NPAIR], F32, 4), ("prod", [1, NT, NPAIR], F32, 4),
                ("rngF", [1, NT, 2], F32, 4), ("rng", [1, NT, 2], I32, 4),
                ("srcHot", [P, 2, NP], F16, 2), ("dstHot", [P, 2, P], F16, 2),
                ("cA", [P, 2, NP], F16, 2), ("cB", [P, 2, NP], F16, 2)):
            cols = 1
            for s in shape[1:]:
                cols *= s
            ph0[name] = at(name, shape, dt, o)
            o += (cols * size + 31) // 32 * 32
        assert o <= OFF_B + 64 * KB, o - OFF_B
        pbd_s, fold, bkq, frow, srcI, dstI, srcF, dstF, iota, rowid, ge, inT, ones16, id16, wide, pres, up, down, prod, \
            rngF, rng, srcHot, dstHot, cA, cB = (ph0[k] for k in (
                "pbd_s", "fold", "bkq", "frow", "srcI", "dstI", "srcF", "dstF", "iota", "rowid", "ge", "inT",
                "ones16", "id16", "wide", "pres", "up", "down", "prod", "rngF", "rng", "srcHot", "dstHot", "cA", "cB"))
        c0 = at("c0", [P, 2, NP], F32R, OFF_E)
        c1 = at("c1", [P, NP], F32R, OFF_E + 10 * KB)
        dtmp = at("dtmp", [P, 4, NT], F32, OFF_TB + 4 * KB)
        route_t = at("route_t", [P, 9, NT * NEXP], F32, OFF_TB + 4 * KB)
        r_inh, r_dist, r_zone, r_w, r_fb, r_c, r_eq, r_rank, r_mask = (route_t[:, k, :] for k in range(9))
        route_s = at("route_s", [P, 2, NT], F32, OFF_TB + 7 * KB)
        r_s, r_none = (route_s[:, k, :] for k in range(2))

        ps = nc.alloc_psum_tensor("ps", [P, 8 * BANK], F32)

        def bank(b, n=BANK):
            return ps[:, b * BANK:b * BANK + n]

        in_x = [sem(f"in_x{p}") for p in range(2)]
        in_fold = sem("in_fold")
        in_edges = sem("in_edges")
        in_small = sem("in_small")
        consts = sem("consts")
        fold_mm = sem("fold_mm")
        fold_out = sem("fold_out")
        fold_st = [sem(f"fold_st{p}") for p in range(2)]
        fb_mm = sem("fb_mm")
        fb_out = sem("fb_out")
        fb_st = sem("fb_st")
        ln_step = sem("ln_step")
        ln_sqrt = sem("ln_sqrt")
        xn_ready = sem("xn_ready")
        tp_ready = sem("tp_ready")
        tp_out = sem("tp_out")
        tr_st = [sem(f"tr_st{p}") for p in range(2)]
        edge_step = sem("edge_step")
        pres_mm = sem("pres_mm")
        hot_ready = sem("hot_ready")
        hot_used = sem("hot_used")
        cnt_ready = sem("cnt_ready")
        ca_ready = sem("ca_ready")
        cb_ready = sem("cb_ready")
        deg_used = sem("deg_used")
        deg_done = sem("deg_done")
        chi_out = sem("chi_out")
        clo_out = sem("clo_out")
        chi_st = [sem(f"chi_st{p}") for p in range(2)]
        clo_st = sem("clo_st")
        dg = sem("dg")
        dg_sqrt = sem("dg_sqrt")
        dg_max = sem("dg_max")
        act_in = [sem(f"act_in{p}") for p in range(2)]
        act_hi = sem("act_hi")
        act_lo = sem("act_lo")
        act_used = sem("act_used")
        stg_in = [sem(f"stg_in{p}") for p in range(2)]
        pan_hi = sem("pan_hi")
        pan_lo = sem("pan_lo")
        bias_in = sem("bias_in")
        out_ready = sem("out_ready")
        out_free = sem("out_free")
        kb_ready = sem("kb_ready")
        k_ready = sem("k_ready")
        kv_used = sem("kv_used")
        kv_mm = sem("kv_mm")
        kvT_step = sem("kvT_step")
        wo_in = [sem(f"wo_in{p}") for p in range(2)]
        m_st = [sem(f"m_st{p}") for p in range(2)]
        qb_ready = sem("qb_ready")
        q_relu = sem("q_relu")
        hb_ready = sem("hb_ready")
        hhi_ready = sem("hhi_ready")
        hlo_ready = sem("hlo_ready")
        xt_in = [sem(f"xt_in{p}") for p in range(2)]
        chi_in = [sem(f"chi_in{p}") for p in range(2)]
        clo_in = sem("clo_in")
        c_ready = sem("c_ready")
        c_free = sem("c_free")
        x1s = sem("x1s")
        x1_sqrt = sem("x1_sqrt")
        x1_st = [sem(f"x1_st{p}") for p in range(2)]
        x2_ready = sem("x2_ready")
        z_ready = sem("z_ready")
        z_read = sem("z_read")
        rt = sem("rt")
        rt_act = sem("rt_act")
        silu_ready = sem("silu_ready")
        x1b_in = [sem(f"x1b_in{p}") for p in range(2)]
        o_st = [sem(f"o_st{p}") for p in range(2)]

        U = {"kv0": 0, "kv1": NT, "q": 2 * NT, "h": 3 * NT, "x": 4 * NT, "gu0": 5 * NT, "gu1": 6 * NT,
             "d": 7 * NT}
        V = {"kv0": 0, "m0": NT, "kv1": NT + 4, "m1": 2 * NT + 4, "q": 2 * NT + 8, "h": 3 * NT + 8,
             "x": 4 * NT + 8, "gu0": 5 * NT + 8, "gu1": 6 * NT + 8, "d": 7 * NT + 8}
        T = {"ln": 0, "q": 2 * NT, "x": 4 * NT, "gu0": 6 * NT, "gu1": 7 * NT}
        PAIR = {"kv0": 0, "kv1": 1, "q": 2, "h": 3, "x": 4, "gu0": 5, "gu1": 6, "d": 7}
        PANELS = {"kv0": panA, "kv1": panB, "q": panA, "h": panB, "x": panB, "gu0": panB, "gu1": panA,
                  "d": panB}
        LN_STEPS = 10
        X_STEPS = LN_STEPS + 3
        FOLD_BANK = (3, 7)
        PRES_BANK = (1, 2, 4, 5)
        EDGE_STEPS = 2 + (NT + 1) + 1 + 1 + len(PRES_BANK) + 1 + 4 + 4

        block = ctx.enter_context(nc.Block())

        def tiles(eng, first=0, last=NL):
            with eng.Fori(first, last) as i:
                for p in range(2):
                    yield 2 * i + p, p, i

        def pair_range(eng, t):
            at_t = rng[:].rearrange("a t c -> a (t c)")
            return (eng.value_load(at_t[0:1, bass.ds(2 * t, 1)], min_val=0, max_val=NPAIR - 1),
                    eng.value_load(at_t[0:1, bass.ds(2 * t + 1, 1)], min_val=1, max_val=NPAIR))

        def staggered(eng, front, back, extra=None):
            front(0, 0, 0)
            for t, p, i in tiles(eng, 0, NL - 1):
                front(t + 1, 1 - p, i + p)
                back(t, p, i)
                if extra:
                    extra(t, p)
            front(NT - 1, 1, NL - 1)
            back(NT - 2, 0, NL - 1)
            back(NT - 1, 1, NL - 1)

        @block.sync
        def _(sp):
            for p in range(2):
                sp.sem_inc(tr_st[p], 16)
                sp.sem_inc(chi_st[p], 16)
            sp.sem_inc(clo_st, 16)

            def load_act(source, t, u, p):
                sp.wait_ge(act_lo, u - 1)
                sp.dma_start(actF[:, p, :], source[t]).then_inc(act_in[p], 16)

            def load_bias(parts, v_before):
                if v_before:
                    sp.wait_ge(out_free, v_before + 2)
                n = D // len(parts)
                for k, part in enumerate(parts):
                    sp.dma_start(bias[:, k * n:(k + 1) * n], part.to_broadcast([P, n])).then_inc(bias_in, 16)

            for p in range(2):
                sp.dma_start(tokA[:, p, :], x[p]).then_inc(in_x[p], 16)
            sp.dma_start(srcI[:], src).then_inc(in_edges, 16)
            sp.dma_start(dstI[:], dst).then_inc(in_edges, 16)
            sp.dma_start(wr[:], wr_t).then_inc(in_small, 16)
            sp.dma_start(tmp_t[:, 0:1], temp.to_broadcast([P, 1])).then_inc(in_small, 16)
            for t, p, i in tiles(sp, 0, NL - 1):
                sp.wait_ge(xn_ready, t + 1)
                sp.dma_start(tokA[:, p, :], x[t + 2]).then_inc(in_x[p], 16)
                sp.wait_ge(tp_out, 2 * t + 4)
                sp.dma_start(xnT_d[t], outT[:, p, :]).then_inc(tr_st[p], 16)
            for t in (NT - 2, NT - 1):
                sp.wait_ge(tp_out, 2 * t + 4)
                sp.dma_start(xnT_d[t], outT[:, t % 2, :]).then_inc(tr_st[t % 2], 16)
            for p in range(2):
                sp.wait_ge(tr_st[p], 16 * (1 + NL))
            for p in range(2):
                sp.dma_start(actF[:, p, :], xnT_d[p]).then_inc(act_in[p], 16)
            for t, p, i in tiles(sp):
                sp.wait_ge(chi_out, t + 1)
                sp.dma_start(chi_d[t], c0[:, p, :].bitcast(F32)).then_inc(chi_st[p], 16)
                sp.wait_ge(clo_out, t + 3)
                sp.dma_start(clo_d[t], c1[:].bitcast(F32)).then_inc(clo_st, 16)
            sp.wait_ge(fb_st, 16)

            for hf in range(2):
                u0, vm = U[f"kv{hf}"], V[f"m{hf}"]
                load_bias([fbias_d[0:1, hf * W:(hf + 1) * W], bv[:, hf * W:(hf + 1) * W]], V["kv1"] if hf else 0)
                for t, p, i in tiles(sp, 0, NL - 1):
                    load_act(xnT_d, t + 2, t + u0 + 2, p)
                for t in range(2):
                    load_act(xnT_d, t, u0 + NT + t, t)
                for g in range(4 + 1):
                    if g < 4:
                        if g >= 2:
                            sp.wait_ge(out_ready, 2 * (vm + g - 1))
                        elif hf:
                            sp.wait_ge(out_ready, 2 * (V["m0"] + 4))
                        sp.dma_start(woP[:, g % 2, :], wo_t[4 * hf + g]).then_inc(wo_in[g % 2], 16)
                    if g >= 1:
                        k = g - 1
                        sp.wait_ge(out_free, vm + k + 3)
                        sp.dma_start(m_d[:, :, 4 * hf + k, :].rearrange("h q n -> q h n"),
                                     tokA[:, k % 2, :].rearrange("q (h n) -> q h n", h=2))\
                          .then_inc(m_st[k % 2], 16)

            load_bias([fbias_d[1:2, :]], V["q"])
            for t, p, i in tiles(sp, 0, NL - 1):
                load_act(xnT_d, t + 2, t + U["q"] + 2, p)
                sp.wait_ge(tp_out, 2 * t + T["q"] + 4)
                sp.dma_start(qT_d[t], outT[:, p, :]).then_inc(tr_st[p], 16)
            for t in range(2):
                load_act(xnT_d, t, U["h"] + t, t)
            for t in (NT - 2, NT - 1):
                sp.wait_ge(tp_out, 2 * t + T["q"] + 4)
                sp.dma_start(qT_d[t], outT[:, t % 2, :]).then_inc(tr_st[t % 2], 16)
            load_bias([bh], V["h"])
            for t, p, i in tiles(sp, 0, NL - 1):
                load_act(xnT_d, t + 2, t + U["h"] + 2, p)
            for p in range(2):
                sp.wait_ge(tr_st[p], 16 * (1 + 2 * NL))
            for t in range(2):
                load_act(qT_d, t, U["x"] + t, t)

            load_bias([bo], V["x"])
            sp.wait_ge(hlo_ready, NT)
            for p in range(2):
                sp.dma_start(tokA[:, p, :], x[p]).then_inc(xt_in[p], 16)
                sp.wait_ge(chi_st[p], 16 * (1 + NL))
            sp.wait_ge(clo_st, 16 * (1 + NT))
            sp.wait_ge(pan_lo, NPIECE * (PAIR["x"] + 1))

            def load_counts(t, p):
                sp.dma_start(cHi[:, p].bitcast(F32), chi_d[:, :, bass.ds(t * P, P)].rearrange("c q r -> q c r"))\
                  .then_inc(chi_in[p], 16)

            def load_rest(t):
                sp.dma_start(cLo[:].bitcast(F32), clo_d[:, :, bass.ds(t * P, P)].rearrange("c q r -> q c r"))\
                  .then_inc(clo_in, 16)

            load_counts(0, 0)
            load_rest(0)
            load_counts(1, 1)

            def store_x(t, p):
                sp.wait_ge(c_free, t + 2)
                sp.dma_start(x1_d[t], tokA[:, p, :]).then_inc(x1_st[p], 16)

            def store_x2(t):
                sp.wait_ge(tp_out, 2 * t + T["x"] + 4)
                sp.dma_start(x2T_d[t], outT[:, 1, :]).then_inc(tr_st[1], 16)

            for t, p, i in tiles(sp, 0, NL - 1):
                load_act(qT_d, t + 2, t + U["x"] + 2, p)
                sp.wait_ge(c_ready, 2 * t + 2)
                load_rest(t + 1)
                load_counts(t + 2, p)
                store_x(t, p)
                sp.wait_ge(x1_st[p], 16 * i + 16)
                sp.wait_ge(x2_ready, t + 1)
                sp.dma_start(tokA[:, p, :], x[t + 2]).then_inc(xt_in[p], 16)
                store_x2(t)
            for t in (NT - 2, NT - 1):
                p = t % 2
                if t < NT - 1:
                    sp.wait_ge(c_ready, 2 * t + 2)
                    load_rest(t + 1)
                sp.wait_ge(tr_st[1], 16 * (1 + 2 * NL + p + 1))
                load_act(x2T_d, p, U["gu0"] + p, p)
                store_x(t, p)
                store_x2(t)

            for hf in range(2):
                name = f"gu{hf}"

                def store_h(t, p):
                    sp.wait_ge(tp_out, t + T[name] + 3)
                    sp.dma_start(hT_d[t][:, hf * W:(hf + 1) * W], outT[:, p, 0:W]).then_inc(tr_st[p], 16)

                if hf == 0:
                    sp.wait_ge(tr_st[1], 16 * (1 + 2 * NL + NT))
                for t, p, i in tiles(sp, 0, NL - 1):
                    load_act(x2T_d, t + 2, t + U[name] + 2, p)
                    store_h(t, p)
                for t in range(2):
                    if hf:
                        sp.wait_ge(tr_st[t], 16 * (1 + 2 * NL + (NT if t else 0) + NL + 1))
                    load_act(hT_d if hf else x2T_d, t, U[name] + NT + t, t)
                for t in (NT - 2, NT - 1):
                    store_h(t, t % 2)

            sp.wait_ge(out_free, V["d"] + 2)
            for p in range(2):
                sp.wait_ge(x1_st[p], 16 * NL)
                sp.wait_ge(tr_st[p], 16 * (1 + 4 * NL + (NT if p else 0)))
            for p in range(2):
                sp.dma_start(tokA[:, p, :], x1_d[p]).then_inc(x1b_in[p], 16)
            for t, p, i in tiles(sp, 0, NL - 1):
                load_act(hT_d, t + 2, t + U["d"] + 2, p)
                sp.wait_ge(out_free, t + V["d"] + 3)
                sp.dma_start(out[t], tokA[:, p, :]).then_inc(o_st[p], 16)
                sp.wait_ge(o_st[p], 16 * i + 16)
                sp.dma_start(tokA[:, p, :], x1_d[t + 2]).then_inc(x1b_in[p], 16)
            for t in (NT - 2, NT - 1):
                sp.wait_ge(out_free, t + V["d"] + 3)
                sp.dma_start(out[t], tokA[:, t % 2, :]).then_inc(o_st[t % 2], 16)
            for p in range(2):
                sp.wait_ge(o_st[p], 16 * NL)

        @block.gpsimd
        def _(pool):
            pool.sem_inc(clo_out, 2)
            for m in (ident, id16, wide):
                pool.memset(m[:], 0.0).then_inc(consts, 1)
            pool.memset(ones16[:], 1.0).then_inc(consts, 1)
            for m, pattern, base, channel in ((iota, [[1, NP]], 0, 0), (rowid, [[P, NT]], 0, 1),
                                              (up, [[0, NT], [1, NPAIR]], 1, 0),
                                              (down, [[0, NT], [-1, NPAIR]], NPAIR, 0)):
                pool.iota(m[:], pattern, base=base, channel_multiplier=channel,
                          allow_small_or_imprecise_dtypes=True).then_inc(consts, 1)
            pool.wait_ge(consts, 8)
            for m, cols, base in ((ident, P, 0), (id16, P, 0), (wide, WIDE, NP - P)):
                pool.affine_select(out=m[:], in_=m[:], compare_op=ALU.not_equal, fill=1.0, base=base,
                                   pattern=[[-1, cols]], channel_multiplier=1).then_inc(consts, 1)

            def load_pair(name, first, second, between=None):
                n0 = NPIECE * PAIR[name]
                half = NPIECE // 2
                hi, lo = (m[:].rearrange("q a k n -> q (a k n)") for m in PANELS[name])

                def load(k, p):
                    source = first if k < half else second
                    at = k % half * PIECE
                    pool.dma_start(stage[:, p, :], source[:, at:at + PIECE]).then_inc(stg_in[p], 16)

                if n0:
                    pool.wait_ge(pan_lo, n0)
                for k in range(2):
                    load(k, k)
                for k in range(NPIECE):
                    p = k % 2
                    at = slice(k * PIECE, (k + 1) * PIECE)
                    if between:
                        between(k)
                    pool.wait_ge(pan_hi, n0 + k + 1)
                    pool.tensor_tensor(lo[:, at], stage[:, p, :], hi[:, at].bitcast(F32),
                                       ALU.subtract).then_inc(pan_lo, 1)
                    if k + 2 < NPIECE:
                        pool.wait_ge(pan_lo, n0 + k + 1)
                        load(k + 2, p)

            kf = kfold_d.rearrange("h q k n -> h q (k n)")
            qf = qfold_d.rearrange("h q k n -> h q (k n)")
            mf = m_d.rearrange("h q k n -> h q (k n)")

            def counts(t):
                pool.wait_ge(cb_ready, t + 3)
                pool.wait_ge(clo_st, 16 * t + 16)
                pool.tensor_copy(c1[:], cB[:, t % 2, :]).then_inc(clo_out, 1)

            counts(0)
            for p in range(2):
                pool.wait_ge(fold_st[p], 16 * 2 * KC)
            load_pair("kv0", kf[0], wv_pan[0], lambda k: counts(k + 1))
            counts(NT - 1)
            pool.wait_ge(dg_max, 1)
            pool.partition_all_reduce(degi[:, 1:2], degi[:, 0:1], P, RMAX).then_inc(dg_max, 1)
            pool.wait_ge(dg_max, 3)
            load_pair("kv1", kf[1], wv_pan[1])
            pool.wait_ge(out_ready, 2 * V["m0"])
            load_pair("q", qf[0], qf[1])
            pool.wait_ge(out_ready, 2 * V["m1"])
            load_pair("h", wh_pan[0], wh_pan[1])
            for p in range(2):
                pool.wait_ge(m_st[p], 16 * 4)
            pool.wait_ge(out_ready, 2 * V["x"])
            load_pair("x", mf[0], mf[1])
            pool.wait_ge(c_ready, 2 * NT)
            load_pair("gu0", wgu_pan[0, 0], wgu_pan[0, 1])
            load_pair("gu1", wgu_pan[1, 0], wgu_pan[1, 1])
            pool.wait_ge(out_ready, 2 * V["gu1"])
            load_pair("d", wd_pan[0], wd_pan[1])

        @block.scalar
        def _(act):
            act.sem_inc(tp_out, 2)
            act.dma_start(pbd_s[:], pbd).then_inc(in_fold, 16)
            act.dma_start(bkq[:, 0:KC], bk_col).then_inc(in_fold, 16)
            act.dma_start(bkq[:, KC:2 * KC], bq_col).then_inc(in_fold, 16)
            act.dma_start(wk_s[:], wk_nat).then_inc(in_fold, 16)
            act.dma_start(wq_s[:], wq_nat).then_inc(in_fold, 16)

            def to_outT(w, bank_no, p, col, k):
                act.wait_ge(tp_ready, w + 1)
                act.wait_ge(tr_st[p], 16 * k + 16)
                act.activation(outT[:, p, col:col + W], bank(6 + bank_no), ACT.Copy).then_inc(tp_out, 1)

            def fold_evac(n):
                act.wait_ge(fold_mm, n + 1)
                if n >= 2:
                    act.wait_ge(fold_st[n % 2], 16 * (n // 2))
                act.activation(fold[:, n % 2, :], bank(FOLD_BANK[n % 2]), ACT.Copy).then_inc(fold_out, 1)
                act.wait_ge(fold_out, n + 1)
                target = (kfold_d, qfold_d)[n // (2 * KC)][n % (2 * KC) // KC, :, n % KC, :]
                act.dma_start(target, fold[:, n % 2, :]).then_inc(fold_st[n % 2], 16)

            def split(u, p, k):
                act.wait_ge(act_in[p], 16 * k + 16)
                act.wait_ge(act_used, u + 1)
                act.activation(actH[:, p, :], actF[:, p, :], ACT.Copy).then_inc(act_hi, 1)

            def split_next(name, t, p, i):
                split(t + U[name] + 1, 1 - p, i + U[name] // 2 + p)

            def piece(name, k, p):
                n = NPIECE * PAIR[name]
                hi = PANELS[name][0][:].rearrange("q a k n -> q (a k n)")
                act.wait_ge(stg_in[p], 8 * k + 8 * (1 - p) + 8 * n + 8)
                act.activation(hi[:, bass.ds(k * PIECE, PIECE)], stage[:, p, :], ACT.Copy).then_inc(pan_hi, 1)

            for t, p, i in tiles(act):
                act.wait_ge(ln_step, LN_STEPS * t + 5)
                act.activation(nrm[:, 1:2], nrm[:, 0:1], ACT.Sqrt).then_inc(ln_sqrt, 1)
                for h in range(2):
                    to_outT(2 * t + h, h, p, h * W, i)
            for n in range(2 * KC):
                fold_evac(n)
            for n in range(4):
                act.wait_ge(fb_mm, n + 1)
                act.activation(frow[0:1, n * W:(n + 1) * W], bank(FOLD_BANK[n % 2])[0:1, :], ACT.Copy).then_inc(fb_out, 1)
            act.wait_ge(fb_out, 4)
            act.dma_start(fbias_d.rearrange("(a b) n -> a b n", a=1), frow[0:1, :].rearrange("a (b n) -> a b n", b=2)).then_inc(fb_st, 16)

            def counts(t, p, i):
                act.wait_ge(cnt_ready, t + 1)
                act.wait_ge(deg_used, t + 1)
                act.activation(cA[:, p, :], ps[:, 3 * p * BANK:3 * p * BANK + NP], ACT.Copy).then_inc(ca_ready, 1)
                act.wait_ge(ca_ready, t + 1)
                act.wait_ge(chi_st[p], 16 * i + 16)
                act.activation(c0[:, p, :], cA[:, p, :], ACT.Copy).then_inc(chi_out, 1)

            counts(0, 0, 0)
            for n in range(2 * KC, 4 * KC):
                fold_evac(n)
            with act.Fori(0, NL - 1) as i:
                counts(2 * i + 1, 1, i)
                piece("kv0", 2 * i, 0)
                counts(2 * i + 2, 0, i + 1)
                piece("kv0", 2 * i + 1, 1)
            counts(NT - 1, 1, NL - 1)
            act.wait_ge(dg, 1)
            act.activation(dtmp[:, 1, :], dtmp[:, 0, :], ACT.Sqrt).then_inc(dg_sqrt, 1)
            split(0, 0, 0)

            for hf in range(2):
                name, nxt = (f"kv{hf}", ("kv1", "q")[hf])

                def features(t, p):
                    act.wait_ge(kb_ready, t + hf * NT + 1)
                    act.activation(tokB[:, p, 0:W], tokA[:, p, 0:W], ACT.Relu,
                                   scale=vscale[:, bass.ds(t, 1)]).then_inc(k_ready, 1)

                for t, p, i in tiles(act, 0, NL - 1):
                    split_next(name, t, p, i)
                    features(t, p)
                    piece(nxt, t, p)
                for t in (NT - 2, NT - 1):
                    split_next(name, t, t % 2, t // 2)
                    features(t, t % 2)
                for g in range(4):
                    v, p = V[f"m{hf}"] + g, g % 2
                    if 2 * hf + g // 2:
                        act.wait_ge(m_st[p], 16 * (2 * hf + g // 2))
                    for h in range(2):
                        act.wait_ge(out_ready, 2 * v + h + 1)
                        last = act.activation(tokA[:, p, h * W:(h + 1) * W], bank(2 * p + h), ACT.Copy)
                    last.then_inc(out_free, 1)

            def q_tile(t, p, i):
                split_next("q", t, p, i)
                for h in range(2):
                    if h == 0:
                        act.wait_ge(qb_ready, t + 1)
                    else:
                        act.wait_ge(out_free, t + V["q"] + 3)
                    act.wait_ge(tp_ready, 2 * t + T["q"] - 3 + h)
                    act.activation(tokB[:, p, h * W:(h + 1) * W], tokA[:, p, h * W:(h + 1) * W], ACT.Relu,
                                   scale=1.0 / HD ** 0.5).then_inc(q_relu, 1)

            def q_transposed(t, p, i):
                for h in range(2):
                    to_outT(2 * t + T["q"] + h, h, p, h * W, i + NL)

            act.sem_inc(q_relu, 4)
            staggered(act, q_tile, q_transposed, lambda t, p: piece("h", t, p))

            for p in range(2):
                act.wait_ge(chi_st[p], 16 * (1 + NL))
            act.wait_ge(clo_st, 16 * (1 + NT))
            hp_hi = hp[0][:].rearrange("q t n -> q (t n)")
            for t, p, i in tiles(act):
                split_next("h", t, p, i)
                act.wait_ge(out_free, t + V["h"] + 3)
                act.activation(hp_hi[:, bass.ds(t * D, D)], tokA[:, p, :], ACT.Copy,
                               scale=dis[:, bass.ds(t, 1)]).then_inc(hhi_ready, 1)
            for k in range(NPIECE):
                piece("x", k, k % 2)

            def x_tile(t, p, i):
                split_next("x", t, p, i)

            def x_transposed(t, p, i):
                act.wait_ge(z_ready, t + 1)
                for h in range(2):
                    to_outT(2 * t + T["x"] + h, h, 1, h * W, t + 2 * NL)

            def x_sqrt(t):
                act.wait_ge(x1s, X_STEPS * t + 1 + 3 + 5)
                act.activation(nrm[:, 1:2], nrm[:, 0:1], ACT.Sqrt).then_inc(x1_sqrt, 1)

            x_tile(0, 0, 0)
            x_sqrt(0)
            for t, p, i in tiles(act, 0, NL - 1):
                x_tile(t + 1, 1 - p, i + p)
                x_transposed(t, p, i)
                x_sqrt(t + 1)
            x_tile(NT - 1, 1, NL - 1)
            x_transposed(NT - 2, 0, NL - 1)
            x_sqrt(NT - 1)
            x_transposed(NT - 1, 1, NL - 1)
            act.wait_ge(z_read, NT + 1)
            act.activation(r_inh, zlog[:], ACT.Sigmoid).then_inc(rt_act, 1)
            act.wait_ge(rt, 3)
            act.activation(r_w, r_dist, ACT.Exp, scale=-1.0 / 0.1).then_inc(rt_act, 1)
            act.activation(r_fb, r_dist, ACT.Exp, scale=-1.0 / 0.3).then_inc(rt_act, 1)
            for k in range(NPIECE):
                piece("gu0", k, k % 2)

            for p in range(2):
                act.wait_ge(x1_st[p], 16 * NL)
            for hf in range(2):
                name = f"gu{hf}"

                def gate(t, p, i):
                    split_next(name, t, p, i)
                    act.wait_ge(out_ready, 2 * t + 2 * V[name] + 1)
                    act.wait_ge(out_free, t + V[name] + 1)
                    act.activation(tokA[:, p, 0:W], bank(2 * p), ACT.Silu).then_inc(silu_ready, 1)

                def h_transposed(t, p, i):
                    to_outT(t + T[name], p, p, 0, i + (2 + hf) * NL + p * NT)

                staggered(act, gate, h_transposed, (lambda t, p: piece("gu1", t, p)) if hf == 0 else
                          (lambda t, p: piece("d", t, p)))

            for t, p, i in tiles(act, 0, NL - 1):
                split_next("d", t, p, i)
            split_next("d", NT - 2, 0, NL - 1)

        @block.vector
        def _(dve):
            dve.sem_inc(out_free, 2)
            dve.sem_inc(cb_ready, 2)
            dve.sem_inc(c_free, 1)
            dve.sem_inc(z_read, 1)

            def split(u, p, k):
                dve.wait_ge(act_in[p], 16 * k + 16)
                dve.wait_ge(act_hi, u + 1)
                dve.tensor_tensor(actL[:, p, :], actF[:, p, :], actH[:, p, :].bitcast(F32), ALU.subtract)\
                   .then_inc(act_lo, 1)

            def split_next(name, t, p, i):
                split(t + U[name] + 1, 1 - p, i + U[name] // 2 + p)

            def refine(value, y, t, out_y, step, s):
                dve.tensor_tensor(t, y, y, ALU.mult).then_inc(step, 1)
                dve.wait_ge(step, s + 1)
                dve.tensor_tensor(t, t, value, ALU.mult).then_inc(step, 1)
                dve.wait_ge(step, s + 2)
                dve.tensor_scalar(t, t, -0.5, 1.5, ALU.mult, ALU.add).then_inc(step, 1)
                dve.wait_ge(step, s + 3)
                dve.tensor_tensor(out_y, y, t, ALU.mult).then_inc(step, 1)
                dve.wait_ge(step, s + 4)

            def layernorm(xin, target, step, s, root, n, done, before_second=None):
                dve.bn_stats(st6[:, 0:6], xin[:, 0:W]).then_inc(step, 1)
                if before_second:
                    before_second()
                dve.bn_stats(st6[:, 6:12], xin[:, W:D]).then_inc(step, 1)
                dve.wait_ge(step, s + 2)
                dve.sem_inc(step, 1)
                dve.bn_aggr(mv[:], st6[:]).then_inc(step, 1)
                dve.wait_ge(step, s + 4)
                dve.tensor_scalar(nrm[:, 0:1], mv[:, 1:2], EPS, None, ALU.add).then_inc(step, 1)
                dve.wait_ge(root, n)
                dve.reciprocal(nrm[:, 2:3], nrm[:, 1:2]).then_inc(step, 1)
                dve.wait_ge(step, s + 6)
                refine(nrm[:, 0:1], nrm[:, 2:3], nrm[:, 3:4], nrm[:, 4:5], step, s + 6)
                dve.tensor_scalar(target, xin, mv[:, 0:1], nrm[:, 4:5], ALU.subtract, ALU.mult).then_inc(done, 1)

            es = [0]

            def edge(ins):
                ins.then_inc(edge_step, 1)
                es[0] += 1
                dve.wait_ge(edge_step, es[0])

            dve.wait_ge(in_edges, 32)
            edge(dve.tensor_copy(srcF[:], srcI[:]))
            edge(dve.tensor_copy(dstF[:], dstI[:]))
            for t in range(NT + 1):
                edge(dve.tensor_scalar(ge[:, t, :], dstF[:], float(P * t), None, ALU.is_ge))
            dve.tensor_tensor(inT[:], ge[:, 0:NT, :], ge[:, 1:NT + 1, :], ALU.subtract).then_inc(edge_step, 1)
            es[0] += 1
            dve.wait_ge(consts, 11)
            edge(dve.tensor_scalar(vscale[:], rowid[:], float(N), 1.0 / HD ** 0.5, ALU.is_lt, ALU.mult))
            dve.wait_ge(pres_mm, 4)
            for k, b in enumerate(PRES_BANK):
                n = min(3, NT - 3 * k)
                cols = bank(b)[0:1, 0:n * NCH].rearrange("a (t c k) -> a t c k", t=n, k=2)
                edge(dve.tensor_reduce(pres[:, 3 * k:3 * k + n, :], cols, AX_X, ALU.max))
            edge(dve.tensor_scalar(pres[:], pres[:], 1.0, None, ALU.min))
            for col, weight in ((1, up), (0, down)):
                edge(dve.tensor_tensor(prod[:], pres[:], weight[:], ALU.mult))
                edge(dve.tensor_reduce(rngF[:, :, col], prod[:], AX_X, ALU.max))
            edge(dve.tensor_scalar(rngF[:, :, 0], rngF[:, :, 0], -1.0, float(NPAIR), ALU.mult, ALU.add))
            edge(dve.tensor_scalar(rngF[:, :, 0], rngF[:, :, 0], float(NPAIR - 1), None, ALU.min))
            edge(dve.scalar_tensor_tensor(out=rngF[:, :, 1], in0=rngF[:, :, 0], scalar=1.0, in1=rngF[:, :, 1],
                                          op0=ALU.add, op1=ALU.max))
            edge(dve.tensor_copy(rng[:], rngF[:]))
            assert es[0] == EDGE_STEPS

            for t, p, i in tiles(dve):
                dve.wait_ge(in_x[p], 16 * i + 16)
                layernorm(tokA[:, p, :], tokB[:, p, :], ln_step, LN_STEPS * t, ln_sqrt, t + 1, xn_ready,
                          lambda: dve.wait_ge(tp_out, 2 * t + 1))

            seen = dve.alloc_register("pairs_seen")
            dve.reg_mov(seen, 0)

            def one_hots(t, p, i):
                first, last = pair_range(dve, t)
                with dve.Fori(first, last) as j:
                    n = dve.snap(seen)
                    for k in range(2):
                        dve.wait_ge(hot_used, 2 * n + k + 1)
                        dve.tensor_scalar(srcHot[:, k, :], iota[:], srcF[:, bass.ds(2 * j + k, 1)], None,
                                          ALU.is_equal)
                        dve.tensor_scalar(dstHot[:, k, :], iota[:, bass.ds(P * t, P)],
                                          dstF[:, bass.ds(2 * j + k, 1)], None, ALU.is_equal)\
                           .then_inc(hot_ready, 1)
                    dve.reg_add(seen, seen, 1)

            def counts_rest(t, p, i):
                dve.wait_ge(ca_ready, t + 1)
                dve.wait_ge(clo_out, t + 1)
                dve.tensor_tensor(cB[:, p, :], ps[:, 3 * p * BANK:3 * p * BANK + NP], cA[:, p, :],
                                  ALU.subtract).then_inc(cb_ready, 1)

            staggered(dve, one_hots, counts_rest)

            dve.wait_ge(deg_done, 1)
            dve.tensor_copy(dtmp[:, 0, :], bank(6, NT)).then_inc(dg, 1)
            dve.tensor_reduce(degi[:, 0:1], bank(6, NT), AX_X, ALU.max).then_inc(dg_max, 1)
            dve.wait_ge(dg_sqrt, 1)
            dve.reciprocal(dtmp[:, 2, :], dtmp[:, 1, :]).then_inc(dg, 1)
            dve.wait_ge(dg, 2)
            refine(dtmp[:, 0, :], dtmp[:, 2, :], dtmp[:, 3, :], dis[:], dg, 2)
            split(0, 0, 0)
            dve.wait_ge(dg_max, 2)
            dve.tensor_scalar(flag[:], degi[:, 1:2], float(EXACT_COUNT), None, ALU.is_gt).then_inc(dg_max, 1)

            dve.memset(kvT[:], 0.0).then_inc(kvT_step, 1)
            for hf in range(2):
                name = f"kv{hf}"
                dve.wait_ge(bias_in, 32 * (hf + 1))
                if hf:
                    for p in range(2):
                        dve.wait_ge(m_st[p], 32)
                for t, p, i in tiles(dve):
                    split_next(name, t, p, i)
                    dve.wait_ge(kv_used, t + hf * NT + 1)
                    dve.wait_ge(out_ready, 2 * t + 2 * V[name] + 1)
                    dve.tensor_tensor(tokA[:, p, 0:W], bank(2 * p), bias[:, 0:W], ALU.add).then_inc(kb_ready, 1)
                    dve.wait_ge(out_ready, 2 * t + 2 * V[name] + 2)
                    dve.tensor_tensor(tokA[:, p, W:D], bank(2 * p + 1), bias[:, W:D], ALU.add)\
                       .then_inc(out_free, 1)
                dve.wait_ge(kv_used, (hf + 1) * NT + 2)
                for k in range(2):
                    own = slice(k * HD, (k + 1) * HD)
                    dve.tensor_copy(kvT[own, :, own], bank(4).rearrange("q (g m) -> q g m", g=4)[own, :, own])\
                       .then_inc(kvT_step, 1)

            dve.wait_ge(bias_in, 80)
            for p in range(2):
                dve.wait_ge(m_st[p], 64)
            for t, p, i in tiles(dve):
                split_next("q", t, p, i)
                for h in range(2):
                    dve.wait_ge(q_relu, 2 * t + h + 1)
                    dve.wait_ge(out_ready, 2 * t + 2 * V["q"] + h + 1)
                    dve.tensor_tensor(tokA[:, p, h * W:(h + 1) * W], bank(2 * p + h),
                                      bias[:, h * W:(h + 1) * W], ALU.add)\
                       .then_inc(qb_ready if h == 0 else out_free, 1)

            dve.wait_ge(bias_in, 96)
            dve.wait_ge(q_relu, 2 * NT + 4)
            hp_hi, hp_lo = (m[:].rearrange("q t n -> q (t n)") for m in hp)
            for t, p, i in tiles(dve):
                split_next("h", t, p, i)
                for h in range(2):
                    dve.wait_ge(out_ready, 2 * t + 2 * V["h"] + h + 1)
                    last = dve.tensor_tensor(tokA[:, p, h * W:(h + 1) * W], bank(2 * p + h),
                                             bias[:, h * W:(h + 1) * W], ALU.add)
                last.then_inc(out_free, 1)
                dve.wait_ge(hhi_ready, t + 1)
                dve.scalar_tensor_tensor(out=hp_lo[:, bass.ds(t * D, D)], in0=tokA[:, p, :],
                                         scalar=dis[:, bass.ds(t, 1)],
                                         in1=hp_hi[:, bass.ds(t * D, D)].bitcast(F32),
                                         op0=ALU.mult, op1=ALU.subtract).then_inc(hlo_ready, 1)

            dve.wait_ge(bias_in, 112)

            def x_tile(t, p, i):
                xt, s, v = tokA[:, p, :], X_STEPS * t + 1, t + V["x"]
                split_next("x", t, p, i)
                dve.wait_ge(xt_in[p], 16 * i + 16)
                dve.tensor_tensor(xt, xt, bias[:], ALU.add).then_inc(x1s, 1)
                dve.wait_ge(x1s, s + 1)
                dve.wait_ge(out_ready, 2 * v + 1)
                dve.tensor_tensor(xt[:, 0:W], bank(2 * p), xt[:, 0:W], ALU.add).then_inc(x1s, 1)
                dve.wait_ge(out_ready, 2 * v + 2)
                dve.tensor_tensor(xt[:, W:D], bank(2 * p + 1), xt[:, W:D], ALU.add).then_inc(out_free, 1)
                dve.wait_ge(x1s, s + 2)
                dve.wait_ge(c_ready, 2 * t + 1)
                dve.scalar_tensor_tensor(out=xt[:, 0:W], in0=bank(4), scalar=dis[:, bass.ds(t, 1)],
                                         in1=xt[:, 0:W], op0=ALU.mult, op1=ALU.add).then_inc(x1s, 1)
                dve.wait_ge(out_free, v + 3)
                dve.wait_ge(c_ready, 2 * t + 2)
                dve.scalar_tensor_tensor(out=xt[:, W:D], in0=bank(5), scalar=dis[:, bass.ds(t, 1)],
                                         in1=xt[:, W:D], op0=ALU.mult, op1=ALU.add).then_inc(c_free, 1)
                dve.wait_ge(x1s, s + 3)

                def second_half():
                    dve.wait_ge(c_free, t + 2)
                    dve.wait_ge(tp_ready, 2 * t + T["x"])

                layernorm(xt, tokB[:, 0, :], x1s, s + 3, x1_sqrt, t + 1, x2_ready, second_half)

            def logits(t, p, i):
                dve.wait_ge(z_ready, t + 2)
                dve.tensor_scalar(zlog[:, bass.ds(NEXP * t, NEXP)], bank(7, NEXP), tmp_t[:, 1:2], None,
                                  ALU.mult).then_inc(z_read, 1)

            dve.wait_ge(in_small, 32)
            dve.reciprocal(tmp_t[:, 1:2], tmp_t[:, 0:1]).then_inc(x1s, 1)
            dve.wait_ge(x1s, 1)
            staggered(dve, x_tile, logits)

            rs = [0]

            def route(ins):
                ins.then_inc(rt, 1)
                rs[0] += 1
                dve.wait_ge(rt, rs[0])

            def by_tile(m):
                return m.rearrange("q (t e) -> q t e", e=NEXP)

            def spread(m):
                return m.unsqueeze(2).to_broadcast([P, NT, NEXP])

            dve.wait_ge(c_ready, 2 * NT)
            dve.wait_ge(rt_act, 1)
            route(dve.tensor_scalar(r_dist, r_inh, CENTER, None, ALU.subtract))
            route(dve.tensor_scalar(r_c, r_inh, -1.0, CENTER, ALU.mult, ALU.add))
            route(dve.tensor_tensor(r_dist, r_dist, r_c, ALU.max))
            route(dve.tensor_scalar(r_zone, zlog[:], ZONE_HIGH, None, ALU.is_le))
            route(dve.scalar_tensor_tensor(out=r_zone, in0=zlog[:], scalar=ZONE_LOW, in1=r_zone, op0=ALU.is_ge,
                                           op1=ALU.mult))
            dve.wait_ge(rt_act, 2)
            route(dve.tensor_tensor(r_w, r_w, r_zone, ALU.mult))
            route(dve.tensor_reduce(r_s, by_tile(r_w), AX_X, ALU.add))
            route(dve.tensor_scalar(r_none, r_s, 1e-8, None, ALU.is_lt))
            dve.wait_ge(rt_act, 3)
            route(dve.tensor_copy(r_c, r_fb))
            for e in range(NEXP):
                route(dve.memset(by_tile(r_rank)[:, :, e], float(NEXP - e)))
            for k in range(2):
                route(dve.tensor_reduce(r_s, by_tile(r_c), AX_X, ALU.max))
                route(dve.tensor_tensor(by_tile(r_eq), by_tile(r_c), spread(r_s), ALU.is_equal))
                route(dve.tensor_tensor(r_eq, r_eq, r_rank, ALU.mult))
                route(dve.tensor_reduce(r_s, by_tile(r_eq), AX_X, ALU.max))
                route(dve.tensor_tensor(by_tile(r_eq), by_tile(r_eq), spread(r_s), ALU.is_equal))
                if k == 0:
                    route(dve.tensor_copy(r_mask, r_eq))
                    route(dve.scalar_tensor_tensor(out=r_c, in0=r_eq, scalar=-2.0, in1=r_c, op0=ALU.mult,
                                                   op1=ALU.add))
            route(dve.tensor_tensor(r_mask, r_mask, r_eq, ALU.add))
            route(dve.tensor_tensor(r_fb, r_fb, r_mask, ALU.mult))

            def normalise(m):
                route(dve.tensor_reduce(r_s, by_tile(m), AX_X, ALU.add))
                route(dve.tensor_scalar(r_s, r_s, 1e-8, None, ALU.max))
                route(dve.reciprocal(r_s, r_s))
                route(dve.tensor_tensor(by_tile(m), by_tile(m), spread(r_s), ALU.mult))

            normalise(r_fb)
            route(dve.tensor_tensor(by_tile(r_fb), by_tile(r_fb), spread(r_none), ALU.mult))
            route(dve.tensor_scalar(r_none, r_none, -1.0, 1.0, ALU.mult, ALU.add))
            route(dve.tensor_tensor(by_tile(r_w), by_tile(r_w), spread(r_none), ALU.mult))
            route(dve.tensor_tensor(r_w, r_w, r_fb, ALU.add))
            normalise(r_w)
            route(dve.tensor_copy(wexp[:], r_w))

            for hf in range(2):
                name = f"gu{hf}"
                for t, p, i in tiles(dve):
                    split_next(name, t, p, i)
                    dve.wait_ge(silu_ready, t + hf * NT + 1)
                    dve.wait_ge(out_ready, 2 * t + 2 * V[name] + 2)
                    dve.wait_ge(tp_ready, t + T[name] - 1)
                    for e in range(XH):
                        cols = slice(e * P, (e + 1) * P)
                        last = dve.scalar_tensor_tensor(
                            out=tokB[:, p, cols], in0=tokA[:, p, cols],
                            scalar=wexp[:, bass.ds(NEXP * t + hf * XH + e, 1)], in1=bank(2 * p + 1)[:, cols],
                            op0=ALU.mult, op1=ALU.mult)
                    last.then_inc(out_free, 1)

            def d_tile(t, p, i):
                dve.wait_ge(x1b_in[p], 16 * i + 16)
                for h in range(2):
                    dve.wait_ge(out_ready, 2 * t + 2 * V["d"] + h + 1)
                    cols = slice(h * W, (h + 1) * W)
                    last = dve.tensor_tensor(tokA[:, p, cols], bank(2 * p + h), tokA[:, p, cols], ALU.add)
                last.then_inc(out_free, 1)

            for t, p, i in tiles(dve, 0, NL - 1):
                split_next("d", t, p, i)
                d_tile(t, p, i)
            split_next("d", NT - 2, 0, NL - 1)
            d_tile(NT - 2, 0, NL - 1)
            d_tile(NT - 1, 1, NL - 1)

        @block.tensor
        def _(pe):
            pe.sem_inc(hot_used, 2)
            pe.sem_inc(deg_used, 2)
            pe.sem_inc(act_used, 2)
            pe.sem_inc(kv_used, 2)
            pe.sem_inc(z_ready, 1)

            pe.wait_ge(edge_step, 2 + NT + 1 + 1)
            pe.wait_ge(consts, 11)
            for k, b in enumerate(PRES_BANK):
                n = min(3, NT - 3 * k)
                pe.matmul(bank(b)[0:1, 0:n * NCH], ones16[:, 0:1],
                          inT[:, 3 * k:3 * k + n, :].rearrange("q t c -> q (t c)"), start=True, stop=True)\
                  .then_inc(pres_mm, 1)

            def transposes(source, b):
                for k in range(4):
                    last = pe.transpose(bank(6 + b)[:, k * P:(k + 1) * P], source[:, k * P:(k + 1) * P], ident[:])
                last.then_inc(tp_ready, 1)

            for t, p, i in tiles(pe):
                pe.wait_ge(xn_ready, t + 1)
                for h in range(2):
                    pe.wait_ge(tp_out, 2 * t + h + 1)
                    transposes(tokB[:, p, h * W:(h + 1) * W], h)

            def fold(weight, n0):
                for n in range(2 * KC):
                    hf, kc = n // KC, n % KC
                    if n0 + n >= 2:
                        pe.wait_ge(fold_out, n0 + n - 1)
                    for g in range(4):
                        last = pe.matmul(bank(FOLD_BANK[n % 2])[:, g * P:(g + 1) * P],
                                         weight[:, 4 * hf + g, kc * P:(kc + 1) * P], pbd_s[:, 4 * hf + g, :],
                                         start=True, stop=True)
                    last.then_inc(fold_mm, 1)

            pe.wait_ge(tp_out, 2 * NT + 2)
            pe.wait_ge(in_fold, 16 * 5)
            fold(wk_s, 0)
            for n in range(4):
                pe.wait_ge(fold_out, 2 * KC)
                if n >= 2:
                    pe.wait_ge(fb_out, n - 1)
                for g in range(4):
                    c = 4 * n + g
                    last = pe.matmul(bank(FOLD_BANK[n % 2])[0:1, g * P:(g + 1) * P], bkq[:, c:c + 1],
                                     pbd_s[:, c % KC, :], start=True, stop=True)
                last.then_inc(fb_mm, 1)

            seen = pe.alloc_register("pairs_counted")
            pe.reg_mov(seen, 0)

            def count(t, p, i):
                blocks = [(slice(c, min(c + BANK, NP)), ps[:, 3 * p * BANK + c:3 * p * BANK + min(c + BANK, NP)])
                          for c in range(0, NP, BANK)]
                pe.wait_ge(cb_ready, t + 1)
                for cols, target in blocks:
                    pe.matmul(target, id16[:], wide[:, bass.ds(NP - P + cols.start - P * t, cols.stop - cols.start)],
                              start=True, stop=False)
                first, last = pair_range(pe, t)
                with pe.Fori(first, last):
                    n = pe.snap(seen)
                    for k in range(2):
                        pe.wait_ge(hot_ready, 2 * n + k + 1)
                        for cols, target in blocks:
                            mm = pe.matmul(target, dstHot[:, k, :], srcHot[:, k, cols], start=False, stop=False)
                        mm.then_inc(hot_used, 1)
                    pe.reg_add(seen, seen, 1)
                for cols, target in blocks:
                    mm = pe.matmul(target, id16[:], wide[:, NP:NP + cols.stop - cols.start], start=False, stop=True)
                mm.then_inc(cnt_ready, 1)

            def degrees(t, p, i):
                pe.wait_ge(cb_ready, t + 3)
                for rt_ in range(NT):
                    for m in (cA, cB):
                        mm = pe.matmul(bank(6)[:, rt_:rt_ + 1], m[:, p, rt_ * P:(rt_ + 1) * P], ones16[:, 0:1],
                                       start=False, stop=False)
                mm.then_inc(deg_used, 1)

            pe.wait_ge(edge_step, EDGE_STEPS)
            count(0, 0, 0)
            pe.wait_ge(fb_out, 4)
            fold(wq_s, 2 * KC)
            pe.wait_ge(fold_out, 4 * KC)
            pe.matmul(bank(6, NT), id16[:], wide[:, NP:NP + NT], start=True, stop=False)
            for t, p, i in tiles(pe, 0, NL - 1):
                count(t + 1, 1 - p, i + p)
                degrees(t, p, i)
            count(NT - 1, 1, NL - 1)
            degrees(NT - 2, 0, NL - 1)
            degrees(NT - 1, 1, NL - 1)
            pe.matmul(bank(6, NT), id16[:], wide[:, NP:NP + NT], start=False, stop=True).then_inc(deg_done, 1)

            def gemm(name, t, p):
                u, v = t + U[name], t + V[name]
                hi, lo = PANELS[name]
                pe.wait_ge(act_hi, u + 1)
                pe.wait_ge(act_lo, u + 1)
                pe.wait_ge(out_free, v + 1)
                for h in range(2):
                    target = bank(2 * p + h)
                    for kc in range(KC):
                        ah = actH[:, p, kc * P:(kc + 1) * P]
                        al = actL[:, p, kc * P:(kc + 1) * P]
                        pe.matmul(target, ah, hi[:, h, kc, :], start=(kc == 0), stop=False)
                        mm = pe.matmul(target, ah, lo[:, h, kc, :], start=False, stop=False)
                        if h == 1 and kc == KC - 1:
                            mm.then_inc(act_used, 1)
                        mm = pe.matmul(target, al, hi[:, h, kc, :], start=False, stop=(kc == KC - 1))
                    mm.then_inc(out_ready, 1)

            def panels(name):
                pe.wait_ge(pan_lo, NPIECE * (PAIR[name] + 1))
                pe.wait_ge(pan_hi, NPIECE * (PAIR[name] + 1))

            for hf in range(2):
                name = f"kv{hf}"

                def kv(t, p, first=False, last=False):
                    pe.wait_ge(k_ready, t + hf * NT + 1)
                    pe.wait_ge(out_free, t + V[name] + 3)
                    for g in range(4):
                        mm = pe.matmul(bank(4)[:, g * P:(g + 1) * P], tokA[:, p, W + g * P:W + (g + 1) * P],
                                       tokB[:, p, g * P:(g + 1) * P], start=first and g == 0,
                                       stop=last and g == 3)
                    mm.then_inc(kv_used, 1)

                panels(name)
                gemm(name, 0, 0)
                gemm(name, 1, 1)
                kv(0, 0, first=True)
                with pe.Fori(0, NL - 1) as i:
                    gemm(name, 2 * i + 2, 0)
                    kv(2 * i + 1, 1)
                    gemm(name, 2 * i + 3, 1)
                    kv(2 * i + 2, 0)
                kv(NT - 1, 1, last=True)
                pe.wait_ge(kvT_step, 1 + 2 * (hf + 1))
                for g in range(4):
                    v, p = V[f"m{hf}"] + g, g % 2
                    pe.wait_ge(wo_in[p], 16 * (2 * hf + g // 2 + 1))
                    pe.wait_ge(out_free, v + 1)
                    for h in range(2):
                        pe.matmul(bank(2 * p + h), kvT[:, g, :], woP[:, p, h * W:(h + 1) * W], start=True,
                                  stop=True).then_inc(out_ready, 1)

            def q_transposes(t, p, i):
                for h in range(2):
                    pe.wait_ge(q_relu, 4 + 2 * t + h + 1)
                    pe.wait_ge(tp_out, 2 * t + T["q"] + h + 1)
                    transposes(tokB[:, p, h * W:(h + 1) * W], h)

            panels("q")
            staggered(pe, lambda t, p, i: gemm("q", t, p), q_transposes)

            panels("h")
            for t, p, i in tiles(pe):
                gemm("h", t, p)

            panels("x")
            pe.wait_ge(hlo_ready, NT)
            pe.wait_ge(dg_max, 3)
            big = pe.value_load(flag[0:1, 0:1], min_val=0, max_val=1)

            def x_products(t, p, i):
                gemm("x", t, p)
                pe.wait_ge(chi_in[p], 16 * i + 16)
                pe.wait_ge(clo_in, 16 * t + 16)
                pe.wait_ge(c_free, t + 1)
                for h in range(2):
                    cols = slice(h * W, (h + 1) * W)
                    for c in range(NT):
                        pe.matmul(bank(4 + h), cHi[:, p, c, :], hp[0][:, c, cols], start=(c == 0), stop=False)
                    with pe.If(big != 0):
                        for c in range(NT):
                            pe.matmul(bank(4 + h), cLo[:, c, :], hp[0][:, c, cols], start=False, stop=False)
                    for c in range(NT):
                        mm = pe.matmul(bank(4 + h), cHi[:, p, c, :], hp[1][:, c, cols], start=False,
                                       stop=(c == NT - 1))
                    mm.then_inc(c_ready, 1)

            def x_transposes(t, p, i):
                pe.wait_ge(x2_ready, t + 1)
                pe.wait_ge(z_read, t + 1)
                for h in range(2):
                    pe.wait_ge(tp_out, 2 * t + T["x"] + h + 1)
                    transposes(tokB[:, 0, h * W:(h + 1) * W], h)
                pe.wait_ge(tp_out, 2 * t + T["x"] + 4)
                for kc in range(KC):
                    mm = pe.matmul(bank(7, NEXP), outT[:, 1, kc * P:(kc + 1) * P],
                                   wr[:, kc * NEXP:(kc + 1) * NEXP], start=(kc == 0), stop=(kc == KC - 1))
                mm.then_inc(z_ready, 1)

            pe.wait_ge(in_small, 32)
            staggered(pe, x_products, x_transposes)

            for hf in range(2):
                name = f"gu{hf}"

                def h_transposes(t, p, i):
                    pe.wait_ge(out_free, t + V[name] + 3)
                    pe.wait_ge(tp_out, t + T[name] + 1)
                    transposes(tokB[:, p, 0:W], p)

                panels(name)
                staggered(pe, lambda t, p, i: gemm(name, t, p), h_transposes)

            panels("d")
            for t, p, i in tiles(pe):
                gemm("d", t, p)


def _panels(w, np):
    return w.reshape(KC, P, 2, W).transpose(2, 1, 0, 3).reshape(2, P, KC * W)


def _layouts(np, x, src, dst, L0_gnn_W, L0_gnn_b, L0_mix_Wq, L0_mix_bq, L0_mix_Wk, L0_mix_bk, L0_mix_Wv, L0_mix_bv,
             L0_mix_Wo, L0_mix_bo, L0_mix_P, L0_ffn_Wg, L0_ffn_Wu, L0_ffn_Wd, L0_ffn_Wr, L0_ffn_temperature):
    def rows(w):
        return w.reshape(KC, P, -1).transpose(1, 0, 2)

    def edges(e):
        full = np.full(NCH * P, -1, dtype=e.dtype)
        full[:E_EDGES] = e
        return full.reshape(NCH, P).T

    xp = np.zeros((NP, D), dtype=x.dtype)
    xp[:N] = x
    pbd = np.zeros((P, KC, P), dtype=L0_mix_P.dtype)
    for h in range(2 * KC):
        k = h % 2 * HD
        pbd[k:k + HD, h // 2, k:k + HD] = L0_mix_P[h].T
    gate_up = np.stack([_panels(w.transpose(1, 0, 2).reshape(D, D), np) for w in (L0_ffn_Wg, L0_ffn_Wu)], axis=1)
    return [xp.reshape(NT, P, D), edges(src), edges(dst), rows(L0_mix_Wk), rows(L0_mix_Wq), pbd,
            L0_mix_bk.reshape(KC, P).T, L0_mix_bq.reshape(KC, P).T, _panels(L0_mix_Wv.T, np),
            L0_mix_bv.reshape(1, D), _panels(L0_gnn_W.T, np), L0_gnn_b.reshape(1, D),
            L0_mix_Wo.T.reshape(KC, P, D), L0_mix_bo.reshape(1, D), gate_up,
            _panels(L0_ffn_Wd.reshape(D, D), np), rows(L0_ffn_Wr).reshape(P, KC * NEXP),
            L0_ffn_temperature.reshape(1, 1)]


def kernel(**inputs):
    import numpy as np
    import concourse.bacc as bacc
    from concourse.bass_utils import run_bass_kernel_spmd

    nc = bacc.Bacc("TRN2", target_bir_lowering=False, num_devices=1)
    arrays, args = {}, []
    for k, a in enumerate(_layouts(np, **{name: np.asarray(a) for name, a in inputs.items()})):
        a = np.ascontiguousarray(a)
        arrays[f"in_{k}"] = a
        args.append(nc.dram_tensor(f"in_{k}", a.shape, mybir.dt.from_np(a.dtype), kind="ExternalInput").ap())
    args.append(nc.dram_tensor("out", (NT, P, D), F32, kind="ExternalOutput").ap())
    gps_layer(nc, *args)
    r = run_bass_kernel_spmd(nc, [arrays], core_ids=[0])
    return r.results[0]["out"].reshape(NP, D)[:N]
```

```python
from contextlib import ExitStack

import concourse.bass as bass
import numpy as np
from concourse import mybir

F32 = mybir.dt.float32
F32R = mybir.dt.float32r
F16 = mybir.dt.float16
I32 = mybir.dt.int32
ALU = mybir.AluOpType
ACT = mybir.ActivationFunctionType
AX_X = mybir.AxisListType.X
RMAX = bass.bass_isa.ReduceOp.max

P = 128
N = 1250
D = 1024
NT = (N + P - 1) // P
NP = NT * P
NL = NT // 2
KC = D // P
W = D // 2
BANK = 512
HD = 64
E_EDGES = 20000
NPAIR = (E_EDGES + 2 * P - 1) // (2 * P)
NCH = 2 * NPAIR
NEXP = 8
XH = NEXP // 2
EPS = 1e-5
PIECE = 1024
NPIECE = 2 * KC * W // PIECE
EXACT_COUNT = 4096
ZONE_LOW = -1.31100973754
ZONE_HIGH = 1.1e-7
LOGIT_MIN = -80.0
CENTER = 0.36787944117144233

KB = 1024
BASE = 16512
OFF_A = BASE
OFF_B = OFF_A + 80 * KB
OFF_E = OFF_A + 64 * KB
OFF_AF = OFF_B + 64 * KB
OFF_AH = OFF_AF + 8 * KB
OFF_AL = OFF_AH + 8 * KB
OFF_TA = OFF_AL + 8 * KB
OFF_TB = OFF_TA + 8 * KB
OFF_OT = OFF_TB + 8 * KB
OFF_BIAS = OFF_OT + 8 * KB
OFF_STG = OFF_BIAS + 4 * KB
OFF_SM = OFF_STG + 10 * KB


def gps_layer(nc, x, src, dst, wk_nat, wq_nat, pbd, bk_col, bq_col, wv_pan, bv, wh_pan, bh, wo_t, bo,
              wgu_pan, wd_pan, wr_t, temp, out):
    ctx = ExitStack()
    with ctx:
        def at(name, shape, dt, off):
            return nc.alloc_sbuf_tensor_at(name, shape, dt, offset=off)

        def sem(name):
            return ctx.enter_context(nc.semaphore(name))

        def dram(name, shape, dt=F32):
            return nc.dram_tensor(name, shape, dt, kind="Internal").ap()

        xnT_d = dram("xnT_d", [NT, P, D])
        qT_d = dram("qT_d", [NT, P, D])
        x1_d = dram("x1_d", [NT, P, D])
        x2T_d = dram("x2T_d", [NT, P, D])
        hT_d = dram("hT_d", [NT, P, D])
        qfold_d = dram("qfold_d", [2, P, KC, W])
        m_d = dram("m_d", [2, P, KC, W])
        fbias_d = dram("fbias_d", [2, D])
        chi_d = dram("chi_d", [NT, P, NP])
        clo_d = dram("clo_d", [NT, P, NP])

        panA = [at("panA_hi", [P, 2, KC, W], F32R, OFF_A), at("panA_lo", [P, 2, KC, W], F32R, OFF_A + 32 * KB)]
        panB = [at("panB_hi", [P, 2, KC, W], F32R, OFF_B), at("panB_lo", [P, 2, KC, W], F32R, OFF_B + 32 * KB)]
        hp = [at("hp_hi", [P, NT, D], F32R, OFF_A), at("hp_lo", [P, NT, D], F32R, OFF_A + 40 * KB)]
        actF = at("actF", [P, 2, D], F32, OFF_AF)
        actH = at("actH", [P, 2, D], F32R, OFF_AH)
        actL = at("actL", [P, 2, D], F32R, OFF_AL)
        tokA = at("tokA", [P, 2, D], F32, OFF_TA)
        tokB = at("tokB", [P, 2, D], F32, OFF_TB)
        outT = at("outT", [P, 2, D], F32, OFF_OT)
        woP = at("woP", [P, 2, D], F32, OFF_OT)
        bias = at("bias", [P, D], F32, OFF_BIAS)
        stage = at("stage", [P, 2, PIECE], F32, OFF_STG)
        cHi = at("cHi", [P, 2, NT, P], F32R, OFF_STG)
        cLo = at("cLo", [P, NT, P], F32R, OFF_TB + 4 * KB)
        small = [OFF_SM]

        def sm(name, cols, dt=F32, size=4):
            off = small[0]
            small[0] += (cols * size + 31) // 32 * 32
            return at(name, [P, cols], dt, off)

        ident = sm("ident", P)
        wr = sm("wr", KC * NEXP)
        zlog = sm("zlog", NT * NEXP)
        wexp = sm("wexp", NT * NEXP)
        dis = sm("dis", NT)
        vscale = sm("vscale", NT)
        tmp_t = sm("tmp_t", 2)
        st6 = sm("st6", 12)
        mv = sm("mv", 2)
        nrm = sm("nrm", 8)
        degi = sm("degi", 2)
        flag = sm("flag", 1, I32)
        ones = sm("ones", 1)
        assert small[0] <= 229368

        kvT = at("kvT", [P, 4, P], F32, OFF_TB + 2 * KB)
        w_s = [at(f"w_s{k}", [P, 4, D], F32, (OFF_A, OFF_B)[k // 2] + (16 + 32 * (k % 2)) * KB) for k in range(4)]
        pbd_s = at("pbd_s", [P, KC, P], F32, OFF_AL)
        fold = at("fold", [P, 2, W], F32, OFF_AL + 4 * KB)
        size = {F32: 4, I32: 4, F16: 2}

        def lay_out(items, start, stop):
            tensors = []
            for name, shape, dt in items:
                tensors.append(at(name, shape, dt, start))
                start += (int(np.prod(shape[1:])) * size[dt] + 31) // 32 * 32
            assert start <= stop
            return tensors

        srcI, dstI, ge, inT, ones16, pres, up, down, prod, rngF = lay_out((
            ("srcI", [P, NCH], I32), ("dstI", [P, NCH], I32), ("ge", [P, NT + 1, NCH], F16),
            ("inT", [P, NT, NCH], F16), ("ones16", [P, 2], F16), ("pres", [1, NT, NPAIR], F16),
            ("up", [1, NT, NPAIR], F16), ("down", [1, NT, NPAIR], F16), ("prod", [1, NT, NPAIR], F16),
            ("rngF", [1, NT, 2], F32)), OFF_AF, OFF_AL)
        srcHot, dstHot, iota, srcF, dstF, id16, zero16, acc, rowid, rng, bkq, dtmp = lay_out((
            ("srcHot", [P, 2, NP], F16), ("dstHot", [P, 2, P], F16), ("iota", [P, NP], F16),
            ("srcF", [P, NCH], F32), ("dstF", [P, NCH], F32), ("id16", [P, P], F16), ("zero16", [P, P], F16),
            ("acc", [P, NP], F32), ("rowid", [P, NT], F32), ("rng", [1, NT, 2], I32), ("bkq", [P, 2 * KC], F32),
            ("dtmp", [P, 4, NT], F32)), OFF_E, OFF_B)
        c0 = at("c0", [P, NP], F32R, OFF_TB + 6 * KB)
        c1 = at("c1", [P, NP], F32R, OFF_TB + 11 * KB)
        route_t = at("route_t", [P, 9, NT * NEXP], F32, OFF_TB + 4 * KB)
        r_inh, r_dist, r_zone, r_w, r_fb, r_c, r_eq, r_rank, r_mask = (route_t[:, k, :] for k in range(9))
        route_s = at("route_s", [P, 2, NT], F32, OFF_TB + 7 * KB)
        r_s, r_none = (route_s[:, k, :] for k in range(2))

        ps = nc.alloc_psum_tensor("ps", [P, 8 * BANK], F32)

        def bank(b, n=BANK):
            return ps[:, b * BANK:b * BANK + n]

        in_x = [sem(f"in_x{p}") for p in range(2)]
        in_fold = sem("in_fold")
        in_edges = sem("in_edges")
        in_small = sem("in_small")
        consts = sem("consts")
        fold_mm = sem("fold_mm")
        fold_out = sem("fold_out")
        fold_lo = sem("fold_lo")
        fold_st = [sem(f"fold_st{p}") for p in range(2)]
        ln_step = sem("ln_step")
        ln_sqrt = sem("ln_sqrt")
        xn_ready = sem("xn_ready")
        tp_ready = sem("tp_ready")
        tp_out = sem("tp_out")
        tr_st = [sem(f"tr_st{p}") for p in range(2)]
        in_w = [sem(f"in_w{k}") for k in range(4)]
        edge_step = sem("edge_step")
        pres_mm = sem("pres_mm")
        hot_ready = sem("hot_ready")
        hot_used = sem("hot_used")
        cnt_ready = sem("cnt_ready")
        cnt_free = sem("cnt_free")
        deg_done = sem("deg_done")
        chi_out = sem("chi_out")
        clo_out = sem("clo_out")
        chi_st = sem("chi_st")
        clo_st = sem("clo_st")
        dg = sem("dg")
        dg_sqrt = sem("dg_sqrt")
        dg_max = sem("dg_max")
        act_in = [sem(f"act_in{p}") for p in range(2)]
        act_hi = sem("act_hi")
        act_lo = sem("act_lo")
        act_used = sem("act_used")
        stg_in = [sem(f"stg_in{p}") for p in range(2)]
        stg_sp = [sem(f"stg_sp{p}") for p in range(2)]
        pan_hi = sem("pan_hi")
        pan_lo = sem("pan_lo")
        bias_in = sem("bias_in")
        out_ready = sem("out_ready")
        out_free = sem("out_free")
        kb_ready = sem("kb_ready")
        k_ready = sem("k_ready")
        kv_used = sem("kv_used")
        kv_mm = sem("kv_mm")
        kvT_step = sem("kvT_step")
        wo_in = [sem(f"wo_in{p}") for p in range(2)]
        m_st = [sem(f"m_st{p}") for p in range(2)]
        qb_ready = sem("qb_ready")
        q_relu = sem("q_relu")
        hb_ready = sem("hb_ready")
        hhi_ready = sem("hhi_ready")
        hlo_ready = sem("hlo_ready")
        xt_in = [sem(f"xt_in{p}") for p in range(2)]
        chi_in = [sem(f"chi_in{p}") for p in range(2)]
        clo_in = sem("clo_in")
        c_ready = sem("c_ready")
        c_free = sem("c_free")
        x1s = sem("x1s")
        x1_sqrt = sem("x1_sqrt")
        x1_st = [sem(f"x1_st{p}") for p in range(2)]
        x2_ready = sem("x2_ready")
        z_ready = sem("z_ready")
        z_read = sem("z_read")
        rt = sem("rt")
        rt_act = sem("rt_act")
        silu_ready = sem("silu_ready")
        x1b_in = [sem(f"x1b_in{p}") for p in range(2)]
        o_st = [sem(f"o_st{p}") for p in range(2)]

        U = {"kv0": 0, "kv1": NT, "q": 2 * NT, "h": 3 * NT, "x": 4 * NT, "gu0": 5 * NT, "gu1": 6 * NT,
             "d": 7 * NT}
        V = {"kv0": 0, "m0": NT, "kv1": NT + 4, "m1": 2 * NT + 4, "q": 2 * NT + 8, "h": 3 * NT + 8,
             "x": 4 * NT + 8, "gu0": 5 * NT + 8, "gu1": 6 * NT + 8, "d": 7 * NT + 8}
        T = {"ln": 0, "q": 2 * NT, "x": 4 * NT, "gu0": 6 * NT, "gu1": 7 * NT}
        FIRST = {"kv0": NPIECE // 2, "kv1": NPIECE // 2}
        JOBS = ("kv0", "kv1", "q", "h", "x", "gu0", "gu1", "d")
        SP_PAIRS = ("x", "gu0")
        POOL_PAIRS = ("kv0", "kv1", "q", "h", "gu1", "d")

        def before(name, names=JOBS):
            return sum(NPIECE - FIRST.get(n, 0) for n in names[:names.index(name)]) - FIRST.get(name, 0)

        PANELS = {"kv0": panA, "kv1": panB, "q": panA, "h": panB, "x": panB, "gu0": panB, "gu1": panA,
                  "d": panB}
        LN_STEPS = 10
        X_STEPS = LN_STEPS + 3
        FOLD_BANK = (0, 3)
        CNT = 5
        NFOLD = 4 * KC + 4
        FOLD_STORES = (NFOLD - 2 * KC) // 2
        PRES_BANK = (1, 2, 4, 5)
        EDGE_STEPS = 2 + (NT + 1) + 1 + 1 + len(PRES_BANK) + 1 + 4 + 4

        block = ctx.enter_context(nc.Block())

        def tiles(eng, first=0, last=NL):
            with eng.Fori(first, last) as i:
                for p in range(2):
                    yield 2 * i + p, p, i

        def pair_range(eng, t):
            at_t = rng[:].rearrange("a t c -> a (t c)")
            return (eng.value_load(at_t[0:1, bass.ds(2 * t, 1)], min_val=0, max_val=NPAIR - 1),
                    eng.value_load(at_t[0:1, bass.ds(2 * t + 1, 1)], min_val=1, max_val=NPAIR))

        def staggered(eng, front, back, extra=None):
            front(0, 0, 0)
            for t, p, i in tiles(eng, 0, NL - 1):
                front(t + 1, 1 - p, i + p)
                back(t, p, i)
                if extra:
                    extra(t, p)
            front(NT - 1, 1, NL - 1)
            back(NT - 2, 0, NL - 1)
            back(NT - 1, 1, NL - 1)

        @block.sync
        def _(sp):
            for s in (*tr_st, chi_st, clo_st):
                sp.sem_inc(s, 16)

            def load_act(source, t, u, p):
                sp.wait_ge(act_lo, u - 1)
                sp.dma_start(actF[:, p, :], source[t]).then_inc(act_in[p], 16)

            def load_bias(parts, v_before):
                if v_before:
                    sp.wait_ge(out_free, v_before + 2)
                n = D // len(parts)
                for k, part in enumerate(parts):
                    sp.dma_start(bias[:, k * n:(k + 1) * n], part.to_broadcast([P, n])).then_inc(bias_in, 16)

            mf = m_d.rearrange("h q k n -> h q (k n)")

            def load_pieces(name, first, second, start, stop):
                n0, half = before(name), NPIECE // 2
                for k in range(start, stop):
                    sp.wait_ge(pan_lo, n0 + max(k - 1, 0))
                    source = first if k < half else second
                    at = k % half * PIECE
                    sp.dma_start(stage[:, k % 2, :], source[:, at:at + PIECE]).then_inc(stg_sp[k % 2], 16)

            for p in range(2):
                sp.dma_start(tokA[:, p, :], x[p]).then_inc(in_x[p], 16)
            sp.dma_start(srcI[:], src).then_inc(in_edges, 16)
            sp.dma_start(dstI[:], dst).then_inc(in_edges, 16)
            sp.dma_start(wr[:], wr_t).then_inc(in_small, 16)
            sp.dma_start(tmp_t[:, 0:1], temp.to_broadcast([P, 1])).then_inc(in_small, 16)
            for t, p, i in tiles(sp, 0, NL - 1):
                sp.wait_ge(xn_ready, t + 1)
                sp.dma_start(tokA[:, p, :], x[t + 2]).then_inc(in_x[p], 16)
                sp.wait_ge(tp_out, 2 * t + 4)
                sp.dma_start(xnT_d[t], outT[:, p, :]).then_inc(tr_st[p], 16)
            for t in (NT - 2, NT - 1):
                sp.wait_ge(tp_out, 2 * t + 4)
                sp.dma_start(xnT_d[t], outT[:, t % 2, :]).then_inc(tr_st[t % 2], 16)
            for p in range(2):
                sp.wait_ge(tr_st[p], 16 * (1 + NL))
            sp.wait_ge(edge_step, EDGE_STEPS)
            for p in range(2):
                sp.dma_start(actF[:, p, :], xnT_d[p]).then_inc(act_in[p], 16)
            for p in range(2):
                sp.wait_ge(fold_st[p], 16 * FOLD_STORES)

            def store_counts(t):
                sp.wait_ge(chi_out, t + 1)
                sp.dma_start(chi_d[t], c0[:].bitcast(F32)).then_inc(chi_st, 16)
                sp.wait_ge(clo_out, t + 1)
                sp.dma_start(clo_d[t], c1[:].bitcast(F32)).then_inc(clo_st, 16)

            for hf in range(2):
                u0, vm = U[f"kv{hf}"], V[f"m{hf}"]
                load_bias([fbias_d[0:1, hf * W:(hf + 1) * W], bv[:, hf * W:(hf + 1) * W]], V["kv1"] if hf else 0)
                for t, p, i in tiles(sp, 0, NL - 1):
                    load_act(xnT_d, t + 2, t + u0 + 2, p)
                    if hf == 0:
                        store_counts(t)
                for t in range(2):
                    load_act(xnT_d, t, u0 + NT + t, t)
                    if hf == 0:
                        store_counts(NT - 2 + t)
                if hf == 0:
                    sp.wait_ge(chi_st, 16 * (1 + NT))
                    sp.wait_ge(clo_st, 16 * (1 + NT))
                for g in range(4 + 1):
                    if g < 4:
                        if g >= 2:
                            sp.wait_ge(out_ready, 2 * (vm + g - 1))
                        elif hf:
                            sp.wait_ge(out_ready, 2 * (V["m0"] + 4))
                        sp.dma_start(woP[:, g % 2, :], wo_t[4 * hf + g]).then_inc(wo_in[g % 2], 16)
                    if g >= 1:
                        k = g - 1
                        sp.wait_ge(out_free, vm + k + 3)
                        sp.dma_start(m_d[:, :, 4 * hf + k, :].rearrange("h q n -> q h n"),
                                     tokA[:, k % 2, :].rearrange("q (h n) -> q h n", h=2))\
                          .then_inc(m_st[k % 2], 16)

            load_bias([fbias_d[1:2, :]], V["q"])
            for t, p, i in tiles(sp, 0, NL - 1):
                load_act(xnT_d, t + 2, t + U["q"] + 2, p)
                sp.wait_ge(tp_out, 2 * t + T["q"] + 4)
                sp.dma_start(qT_d[t], outT[:, p, :]).then_inc(tr_st[p], 16)
            for t in range(2):
                load_act(xnT_d, t, U["h"] + t, t)
            for t in (NT - 2, NT - 1):
                sp.wait_ge(tp_out, 2 * t + T["q"] + 4)
                sp.dma_start(qT_d[t], outT[:, t % 2, :]).then_inc(tr_st[t % 2], 16)
            load_bias([bh], V["h"])
            for t, p, i in tiles(sp, 0, NL - 1):
                load_act(xnT_d, t + 2, t + U["h"] + 2, p)
            for p in range(2):
                sp.wait_ge(tr_st[p], 16 * (1 + 2 * NL))
            for t in range(2):
                load_act(qT_d, t, U["x"] + t, t)

            for p in range(2):
                sp.wait_ge(m_st[p], 16 * 4)
            load_pieces("x", mf[0], mf[1], 0, 2)
            load_bias([bo], V["x"])
            load_pieces("x", mf[0], mf[1], 2, NPIECE)
            sp.wait_ge(hlo_ready, NT)
            for p in range(2):
                sp.dma_start(tokA[:, p, :], x[p]).then_inc(xt_in[p], 16)
            sp.wait_ge(pan_lo, before("x") + NPIECE)

            def load_counts(t, p):
                sp.dma_start(cHi[:, p].bitcast(F32), chi_d[:, :, bass.ds(t * P, P)].rearrange("c q r -> q c r"))\
                  .then_inc(chi_in[p], 16)

            def load_rest(t):
                sp.dma_start(cLo[:].bitcast(F32), clo_d[:, :, bass.ds(t * P, P)].rearrange("c q r -> q c r"))\
                  .then_inc(clo_in, 16)

            load_counts(0, 0)
            load_rest(0)
            load_counts(1, 1)

            def store_x(t, p):
                sp.wait_ge(c_free, t + 2)
                sp.dma_start(x1_d[t], tokA[:, p, :]).then_inc(x1_st[p], 16)

            def store_x2(t):
                sp.wait_ge(tp_out, 2 * t + T["x"] + 4)
                sp.dma_start(x2T_d[t], outT[:, 1, :]).then_inc(tr_st[1], 16)

            for t, p, i in tiles(sp, 0, NL - 1):
                load_act(qT_d, t + 2, t + U["x"] + 2, p)
                sp.wait_ge(c_ready, 2 * t + 2)
                load_rest(t + 1)
                load_counts(t + 2, p)
                store_x(t, p)
                sp.wait_ge(x1_st[p], 16 * i + 16)
                sp.wait_ge(x2_ready, t + 1)
                sp.dma_start(tokA[:, p, :], x[t + 2]).then_inc(xt_in[p], 16)
                store_x2(t)
            for t in (NT - 2, NT - 1):
                p = t % 2
                if t < NT - 1:
                    sp.wait_ge(c_ready, 2 * t + 2)
                    load_rest(t + 1)
                sp.wait_ge(tr_st[1], 16 * (1 + 2 * NL + p + 1))
                load_act(x2T_d, p, U["gu0"] + p, p)
                if t < NT - 1:
                    store_x(t, p)
                    store_x2(t)
            sp.wait_ge(c_ready, 2 * NT)
            load_pieces("gu0", wgu_pan[0, 0], wgu_pan[0, 1], 0, 2)
            store_x(NT - 1, 1)
            load_pieces("gu0", wgu_pan[0, 0], wgu_pan[0, 1], 2, NPIECE)
            store_x2(NT - 1)

            for hf in range(2):
                name = f"gu{hf}"

                def store_h(t, p):
                    sp.wait_ge(tp_out, t + T[name] + 3)
                    sp.dma_start(hT_d[t][:, hf * W:(hf + 1) * W], outT[:, p, 0:W]).then_inc(tr_st[p], 16)

                if hf == 0:
                    sp.wait_ge(tr_st[1], 16 * (1 + 2 * NL + NT))
                for t, p, i in tiles(sp, 0, NL - 1):
                    load_act(x2T_d, t + 2, t + U[name] + 2, p)
                    store_h(t, p)
                for t in range(2):
                    if hf:
                        sp.wait_ge(tr_st[t], 16 * (1 + 2 * NL + (NT if t else 0) + NL + 1))
                    load_act(hT_d if hf else x2T_d, t, U[name] + NT + t, t)
                for t in (NT - 2, NT - 1):
                    store_h(t, t % 2)

            sp.wait_ge(out_free, V["d"] + 2)
            for p in range(2):
                sp.wait_ge(x1_st[p], 16 * NL)
                sp.wait_ge(tr_st[p], 16 * (1 + 4 * NL + (NT if p else 0)))
            for p in range(2):
                sp.dma_start(tokA[:, p, :], x1_d[p]).then_inc(x1b_in[p], 16)
            for t, p, i in tiles(sp, 0, NL - 1):
                load_act(hT_d, t + 2, t + U["d"] + 2, p)
                sp.wait_ge(out_free, t + V["d"] + 3)
                sp.dma_start(out[t], tokA[:, p, :]).then_inc(o_st[p], 16)
                sp.wait_ge(o_st[p], 16 * i + 16)
                sp.dma_start(tokA[:, p, :], x1_d[t + 2]).then_inc(x1b_in[p], 16)
            for t in (NT - 2, NT - 1):
                sp.wait_ge(out_free, t + V["d"] + 3)
                sp.dma_start(out[t], tokA[:, t % 2, :]).then_inc(o_st[t % 2], 16)
            for p in range(2):
                sp.wait_ge(o_st[p], 16 * NL)

        @block.gpsimd
        def _(pool):
            for m in (ident, id16, zero16, acc):
                pool.memset(m[:], 0.0).then_inc(consts, 1)
            for m in (ones16, ones):
                pool.memset(m[:], 1.0).then_inc(consts, 1)
            for m, pattern, base, channel in ((iota, [[1, NP]], 0, 0), (rowid, [[P, NT]], 0, 1),
                                              (up, [[0, NT], [1, NPAIR]], 1, 0),
                                              (down, [[0, NT], [-1, NPAIR]], NPAIR, 0)):
                pool.iota(m[:], pattern, base=base, channel_multiplier=channel,
                          allow_small_or_imprecise_dtypes=True).then_inc(consts, 1)
            pool.wait_ge(consts, 10)
            for m in (ident, id16):
                pool.affine_select(out=m[:], in_=m[:], compare_op=ALU.not_equal, fill=1.0, base=0,
                                   pattern=[[-1, P]], channel_multiplier=1).then_inc(consts, 1)

            def load_pair(name, first, second):
                n0, k0 = before(name), FIRST.get(name, 0)
                half = NPIECE // 2
                hi, lo = (m[:].rearrange("q a k n -> q (a k n)") for m in PANELS[name])

                def load(k, p):
                    source = first if k < half else second
                    at = k % half * PIECE
                    pool.dma_start(stage[:, p, :], source[:, at:at + PIECE]).then_inc(stg_in[p], 16)

                if n0 + k0:
                    pool.wait_ge(pan_lo, n0 + k0)
                for k in range(k0, k0 + 2):
                    load(k, k % 2)
                for k in range(k0, NPIECE):
                    p = k % 2
                    at = slice(k * PIECE, (k + 1) * PIECE)
                    pool.wait_ge(pan_hi, n0 + k + 1)
                    pool.tensor_tensor(lo[:, at], stage[:, p, :], hi[:, at].bitcast(F32),
                                       ALU.subtract).then_inc(pan_lo, 1)
                    if k + 2 < NPIECE:
                        pool.wait_ge(pan_lo, n0 + k + 1)
                        load(k + 2, p)

            def split_rest(name):
                n0 = before(name)
                hi, lo = (m[:].rearrange("q a k n -> q (a k n)") for m in PANELS[name])
                for k in range(NPIECE):
                    at = slice(k * PIECE, (k + 1) * PIECE)
                    pool.wait_ge(pan_hi, n0 + k + 1)
                    pool.tensor_tensor(lo[:, at], stage[:, k % 2, :], hi[:, at].bitcast(F32),
                                       ALU.subtract).then_inc(pan_lo, 1)

            qf = qfold_d.rearrange("h q k n -> h q (k n)")

            for n in range(2 * KC):
                pool.wait_ge(fold_out, n + 1)
                hi, lo = PANELS[f"kv{n // KC}"]
                pool.tensor_tensor(lo[:, 0, n % KC, :], fold[:, n % 2, :], hi[:, 0, n % KC, :].bitcast(F32),
                                   ALU.subtract).then_inc(fold_lo, 1)
            load_pair("kv0", None, wv_pan[0])
            pool.wait_ge(fold_out, 4 * KC)
            load_pair("kv1", None, wv_pan[1])
            pool.wait_ge(dg_max, 1)
            pool.partition_all_reduce(degi[:, 1:2], degi[:, 0:1], P, RMAX).then_inc(dg_max, 1)
            pool.wait_ge(out_ready, 2 * V["m0"])
            for p in range(2):
                pool.wait_ge(fold_st[p], 16 * FOLD_STORES)
            load_pair("q", qf[0], qf[1])
            pool.wait_ge(out_ready, 2 * V["m1"])
            load_pair("h", wh_pan[0], wh_pan[1])
            split_rest("x")
            split_rest("gu0")
            load_pair("gu1", wgu_pan[1, 0], wgu_pan[1, 1])
            pool.wait_ge(out_ready, 2 * V["gu1"])
            load_pair("d", wd_pan[0], wd_pan[1])

        @block.scalar
        def _(act):
            act.sem_inc(tp_out, 2)
            act.dma_start(pbd_s[:], pbd).then_inc(in_fold, 16)
            act.dma_start(bkq[:, 0:KC], bk_col).then_inc(in_fold, 16)
            act.dma_start(bkq[:, KC:2 * KC], bq_col).then_inc(in_fold, 16)
            for k, m in enumerate(w_s):
                act.dma_start(m[:], (wk_nat, wq_nat)[k // 2][:, k % 2 * 4:k % 2 * 4 + 4, :]).then_inc(in_w[k], 16)

            def to_outT(w, bank_no, p, col, k):
                act.wait_ge(tp_ready, w + 1)
                act.wait_ge(tr_st[p], 16 * k + 16)
                act.activation(outT[:, p, col:col + W], bank(6 + bank_no), ACT.Copy).then_inc(tp_out, 1)

            def fold_evac(n):
                act.wait_ge(fold_mm, n + 1)
                source = bank(FOLD_BANK[n % 2])
                if n < 2 * KC:
                    if n >= 2:
                        act.wait_ge(fold_lo, n - 1)
                    act.activation(fold[:, n % 2, :], source, ACT.Copy)
                    act.activation(PANELS[f"kv{n // KC}"][0][:, 0, n % KC, :], source, ACT.Copy)\
                       .then_inc(fold_out, 1)
                    return
                rows = P if n < 4 * KC else 1
                if n < 2 * KC + 2:
                    act.wait_ge(fold_lo, n - 1)
                else:
                    act.wait_ge(fold_st[n % 2], 16 * ((n - 2 * KC) // 2))
                act.activation(fold[0:rows, n % 2, :], source[0:rows, :], ACT.Copy).then_inc(fold_out, 1)
                act.wait_ge(fold_out, n + 1)
                if n < 4 * KC:
                    target = qfold_d[n // KC - 2, :, n % KC, :]
                else:
                    k = n - 4 * KC
                    target = fbias_d[k // 2:k // 2 + 1, k % 2 * W:(k % 2 + 1) * W]
                act.dma_start(target, fold[0:rows, n % 2, :]).then_inc(fold_st[n % 2], 16)

            def split(u, p, k):
                act.wait_ge(act_in[p], 16 * k + 16)
                act.wait_ge(act_used, u + 1)
                act.activation(actH[:, p, :], actF[:, p, :], ACT.Copy).then_inc(act_hi, 1)

            def split_next(name, t, p, i):
                split(t + U[name] + 1, 1 - p, i + U[name] // 2 + p)

            def piece(name, k, p):
                by_sp = name in SP_PAIRS
                n = before(name, SP_PAIRS if by_sp else POOL_PAIRS)
                hi = PANELS[name][0][:].rearrange("q a k n -> q (a k n)")
                act.wait_ge((stg_sp if by_sp else stg_in)[p], 8 * k + 8 * (1 - p) + 8 * n + 8)
                act.activation(hi[:, bass.ds(k * PIECE, PIECE)], stage[:, p, :], ACT.Copy).then_inc(pan_hi, 1)

            for t in range(NT):
                for k in range(4 * (t - 2), 4 * (t - 2) + 2):
                    if t >= 2:
                        fold_evac(k)
                act.wait_ge(ln_step, LN_STEPS * t + 5)
                act.activation(nrm[:, 1:2], nrm[:, 0:1], ACT.Sqrt).then_inc(ln_sqrt, 1)
                for k in range(4 * (t - 2) + 2, 4 * (t - 2) + 4):
                    if t >= 2:
                        fold_evac(k)
                for h in range(2):
                    to_outT(2 * t + h, h, t % 2, h * W, t // 2)
            for n in range(4 * KC, NFOLD):
                fold_evac(n)
            split(0, 0, 0)
            split_next("kv0", 0, 0, 0)
            for k in range(FIRST["kv0"], NPIECE):
                piece("kv0", k, k % 2)
            for p in range(2):
                act.wait_ge(tr_st[p], 16 * (1 + NL))

            def counts(t):
                act.wait_ge(cnt_ready, t + 1)
                act.wait_ge(chi_st, 16 * t + 16)
                act.activation(c0[:], ps[:, CNT * BANK:CNT * BANK + NP], ACT.Copy).then_inc(chi_out, 1)

            for hf in range(2):
                name, nxt = (f"kv{hf}", ("kv1", "q")[hf])

                def features(t, p):
                    act.wait_ge(kb_ready, t + hf * NT + 1)
                    act.activation(tokB[:, p, 0:W], tokA[:, p, 0:W], ACT.Relu,
                                   scale=vscale[:, bass.ds(t, 1)]).then_inc(k_ready, 1)

                def kv_tile(t, p, i, split_too=True):
                    if split_too:
                        split_next(name, t, p, i)
                    features(t, p)
                    if hf == 0:
                        counts(t)

                k0 = FIRST.get(nxt, 0)
                first = 0
                if hf == 0:
                    kv_tile(0, 0, 0, split_too=False)
                    piece(nxt, k0, 0)
                    kv_tile(1, 1, 0)
                    piece(nxt, k0 + 1, 1)
                    first = 1
                for t, p, i in tiles(act, first, (NPIECE - k0) // 2):
                    kv_tile(t, p, i)
                    piece(nxt, t + k0, p)
                for t, p, i in tiles(act, (NPIECE - k0) // 2, NL):
                    kv_tile(t, p, i)
                for g in range(4):
                    v, p = V[f"m{hf}"] + g, g % 2
                    if 2 * hf + g // 2:
                        act.wait_ge(m_st[p], 16 * (2 * hf + g // 2))
                    for h in range(2):
                        act.wait_ge(out_ready, 2 * v + h + 1)
                        last = act.activation(tokA[:, p, h * W:(h + 1) * W], bank(2 * p + h), ACT.Copy)
                    last.then_inc(out_free, 1)
                if hf == 0:
                    act.wait_ge(dg, 1)
                    act.activation(dtmp[:, 1, :], dtmp[:, 0, :], ACT.Sqrt).then_inc(dg_sqrt, 1)

            def q_tile(t, p, i):
                split_next("q", t, p, i)
                for h in range(2):
                    if h == 0:
                        act.wait_ge(qb_ready, t + 1)
                    else:
                        act.wait_ge(out_free, t + V["q"] + 3)
                    act.wait_ge(tp_ready, 2 * t + T["q"] - 3 + h)
                    act.activation(tokB[:, p, h * W:(h + 1) * W], tokA[:, p, h * W:(h + 1) * W], ACT.Relu,
                                   scale=1.0 / HD ** 0.5).then_inc(q_relu, 1)

            def q_transposed(t, p, i):
                for h in range(2):
                    to_outT(2 * t + T["q"] + h, h, p, h * W, i + NL)

            act.sem_inc(q_relu, 4)
            staggered(act, q_tile, q_transposed, lambda t, p: piece("h", t, p))

            hp_hi = hp[0][:].rearrange("q t n -> q (t n)")
            for t, p, i in tiles(act):
                split_next("h", t, p, i)
                act.wait_ge(out_free, t + V["h"] + 3)
                act.activation(hp_hi[:, bass.ds(t * D, D)], tokA[:, p, :], ACT.Copy,
                               scale=dis[:, bass.ds(t, 1)]).then_inc(hhi_ready, 1)
            def x_tile(t, p, i):
                split_next("x", t, p, i)

            def x_transposed(t, p, i):
                act.wait_ge(z_ready, t + 1)
                for h in range(2):
                    to_outT(2 * t + T["x"] + h, h, 1, h * W, t + 2 * NL)

            def x_sqrt(t):
                act.wait_ge(x1s, X_STEPS * t + 1 + 3 + 5)
                act.activation(nrm[:, 1:2], nrm[:, 0:1], ACT.Sqrt).then_inc(x1_sqrt, 1)

            x_tile(0, 0, 0)
            for k in range(NPIECE):
                piece("x", k, k % 2)
            x_sqrt(0)
            for t, p, i in tiles(act, 0, NL - 1):
                x_tile(t + 1, 1 - p, i + p)
                x_transposed(t, p, i)
                x_sqrt(t + 1)
            x_tile(NT - 1, 1, NL - 1)
            x_transposed(NT - 2, 0, NL - 1)
            x_sqrt(NT - 1)
            split_next("gu0", 0, 0, 0)
            for k in range(NPIECE):
                if k == NPIECE // 4:
                    x_transposed(NT - 1, 1, NL - 1)
                piece("gu0", k, k % 2)
            act.wait_ge(rt, 1)
            act.activation(r_inh, r_c, ACT.Exp, scale=-1.0).then_inc(rt_act, 1)
            act.wait_ge(rt, 6)
            act.activation(r_w, r_dist, ACT.Exp, scale=-1.0 / 0.1).then_inc(rt_act, 1)
            act.activation(r_fb, r_dist, ACT.Exp, scale=-1.0 / 0.3).then_inc(rt_act, 1)

            for p in range(2):
                act.wait_ge(x1_st[p], 16 * NL)
            for hf in range(2):
                name = f"gu{hf}"

                def gate(t, p, i, split_too=True):
                    if split_too:
                        split_next(name, t, p, i)
                    act.wait_ge(out_ready, 2 * t + 2 * V[name] + 1)
                    act.wait_ge(out_free, t + V[name] + 1)
                    act.activation(tokA[:, p, 0:W], bank(2 * p), ACT.Silu).then_inc(silu_ready, 1)

                def h_transposed(t, p, i):
                    to_outT(t + T[name], p, p, 0, i + (2 + hf) * NL + p * NT)

                gate(0, 0, 0, split_too=hf > 0)
                for t, p, i in tiles(act, 0, NL - 1):
                    gate(t + 1, 1 - p, i + p)
                    h_transposed(t, p, i)
                    piece(("gu1", "d")[hf], t, p)
                gate(NT - 1, 1, NL - 1)
                h_transposed(NT - 2, 0, NL - 1)
                h_transposed(NT - 1, 1, NL - 1)

            for t, p, i in tiles(act, 0, NL - 1):
                split_next("d", t, p, i)
            split_next("d", NT - 2, 0, NL - 1)

        @block.vector
        def _(dve):
            dve.sem_inc(out_free, 2)
            dve.sem_inc(cnt_free, 1)
            dve.sem_inc(c_free, 1)
            dve.sem_inc(z_read, 1)

            def split(u, p, k):
                dve.wait_ge(act_in[p], 16 * k + 16)
                dve.wait_ge(act_hi, u + 1)
                dve.tensor_tensor(actL[:, p, :], actF[:, p, :], actH[:, p, :].bitcast(F32), ALU.subtract)\
                   .then_inc(act_lo, 1)

            def split_next(name, t, p, i):
                split(t + U[name] + 1, 1 - p, i + U[name] // 2 + p)

            def refine(value, y, t, out_y, step, s):
                dve.tensor_tensor(t, y, y, ALU.mult).then_inc(step, 1)
                dve.wait_ge(step, s + 1)
                dve.tensor_tensor(t, t, value, ALU.mult).then_inc(step, 1)
                dve.wait_ge(step, s + 2)
                dve.tensor_scalar(t, t, -0.5, 1.5, ALU.mult, ALU.add).then_inc(step, 1)
                dve.wait_ge(step, s + 3)
                dve.tensor_tensor(out_y, y, t, ALU.mult).then_inc(step, 1)
                dve.wait_ge(step, s + 4)

            def layernorm(xin, target, step, s, root, n, done, before_second=None):
                dve.bn_stats(st6[:, 0:6], xin[:, 0:W]).then_inc(step, 1)
                if before_second:
                    before_second()
                dve.bn_stats(st6[:, 6:12], xin[:, W:D]).then_inc(step, 1)
                dve.wait_ge(step, s + 2)
                dve.sem_inc(step, 1)
                dve.bn_aggr(mv[:], st6[:]).then_inc(step, 1)
                dve.wait_ge(step, s + 4)
                dve.tensor_scalar(nrm[:, 0:1], mv[:, 1:2], EPS, None, ALU.add).then_inc(step, 1)
                dve.wait_ge(root, n)
                dve.reciprocal(nrm[:, 2:3], nrm[:, 1:2]).then_inc(step, 1)
                dve.wait_ge(step, s + 6)
                refine(nrm[:, 0:1], nrm[:, 2:3], nrm[:, 3:4], nrm[:, 4:5], step, s + 6)
                dve.tensor_scalar(target, xin, mv[:, 0:1], nrm[:, 4:5], ALU.subtract, ALU.mult).then_inc(done, 1)

            es = [0]

            def edge(ins):
                ins.then_inc(edge_step, 1)
                es[0] += 1
                dve.wait_ge(edge_step, es[0])

            def ln1(t, p, i):
                dve.wait_ge(in_x[p], 16 * i + 16)
                layernorm(tokA[:, p, :], tokB[:, p, :], ln_step, LN_STEPS * t, ln_sqrt, t + 1, xn_ready,
                          lambda: dve.wait_ge(tp_out, 2 * t + 1))

            ln1(0, 0, 0)
            ln1(1, 1, 0)
            dve.wait_ge(in_edges, 32)
            edge(dve.tensor_copy(srcF[:], srcI[:]))
            edge(dve.tensor_copy(dstF[:], dstI[:]))
            for t in range(NT + 1):
                edge(dve.tensor_scalar(ge[:, t, :], dstF[:], float(P * t), None, ALU.is_ge))
            dve.tensor_tensor(inT[:], ge[:, 0:NT, :], ge[:, 1:NT + 1, :], ALU.subtract).then_inc(edge_step, 1)
            es[0] += 1
            dve.wait_ge(consts, 12)
            edge(dve.tensor_scalar(vscale[:], rowid[:], float(N), 1.0 / HD ** 0.5, ALU.is_lt, ALU.mult))
            ln1(2, 0, 1)
            ln1(3, 1, 1)
            dve.wait_ge(pres_mm, 4)
            for k, b in enumerate(PRES_BANK):
                n = min(3, NT - 3 * k)
                cols = bank(b)[0:1, 0:n * NCH].rearrange("a (t c k) -> a t c k", t=n, k=2)
                edge(dve.tensor_reduce(pres[:, 3 * k:3 * k + n, :], cols, AX_X, ALU.max))
            edge(dve.tensor_scalar(pres[:], pres[:], 1.0, None, ALU.min))
            for col, weight in ((1, up), (0, down)):
                edge(dve.tensor_tensor(prod[:], pres[:], weight[:], ALU.mult))
                edge(dve.tensor_reduce(rngF[:, :, col], prod[:], AX_X, ALU.max))
            edge(dve.tensor_scalar(rngF[:, :, 0], rngF[:, :, 0], -1.0, float(NPAIR), ALU.mult, ALU.add))
            edge(dve.tensor_scalar(rngF[:, :, 0], rngF[:, :, 0], float(NPAIR - 1), None, ALU.min))
            edge(dve.scalar_tensor_tensor(out=rngF[:, :, 1], in0=rngF[:, :, 0], scalar=1.0, in1=rngF[:, :, 1],
                                          op0=ALU.add, op1=ALU.max))
            edge(dve.tensor_copy(rng[:], rngF[:]))
            assert es[0] == EDGE_STEPS

            for t, p, i in tiles(dve, 2, NL):
                ln1(t, p, i)
            for p in range(2):
                dve.wait_ge(fold_st[p], 16 * FOLD_STORES)
                dve.wait_ge(tr_st[p], 16 * (1 + NL))
            split(0, 0, 0)

            seen = dve.alloc_register("pairs_seen")
            dve.reg_mov(seen, 0)

            def one_hots(t):
                first, last = pair_range(dve, t)
                with dve.Fori(first, last) as j:
                    n = dve.snap(seen)
                    for k in range(2):
                        dve.wait_ge(hot_used, 2 * n + k + 1)
                        dve.tensor_scalar(srcHot[:, k, :], iota[:], srcF[:, bass.ds(2 * j + k, 1)], None,
                                          ALU.is_equal)
                        dve.tensor_scalar(dstHot[:, k, :], iota[:, bass.ds(P * t, P)],
                                          dstF[:, bass.ds(2 * j + k, 1)], None, ALU.is_equal)\
                           .then_inc(hot_ready, 1)
                    dve.reg_add(seen, seen, 1)

            def counts_rest(t):
                counts = ps[:, CNT * BANK:CNT * BANK + NP]
                dve.wait_ge(chi_out, t + 1)
                dve.wait_ge(clo_st, 16 * t + 16)
                dve.tensor_tensor(c1[:], counts, c0[:].bitcast(F32), ALU.subtract).then_inc(clo_out, 1)
                dve.wait_ge(cnt_free, t + 1)
                dve.tensor_tensor(acc[:], counts, acc[:], ALU.add).then_inc(cnt_free, 1)

            dve.memset(kvT[:], 0.0).then_inc(kvT_step, 1)
            for hf in range(2):
                name = f"kv{hf}"
                dve.wait_ge(bias_in, 32 * (hf + 1))
                if hf:
                    for p in range(2):
                        dve.wait_ge(m_st[p], 32)
                for t, p, i in tiles(dve):
                    split_next(name, t, p, i)
                    dve.wait_ge(kv_used, t + hf * NT + 1)
                    dve.wait_ge(out_ready, 2 * t + 2 * V[name] + 1)
                    dve.tensor_tensor(tokA[:, p, 0:W], bank(2 * p), bias[:, 0:W], ALU.add).then_inc(kb_ready, 1)
                    dve.wait_ge(out_ready, 2 * t + 2 * V[name] + 2)
                    dve.tensor_tensor(tokA[:, p, W:D], bank(2 * p + 1), bias[:, W:D], ALU.add)\
                       .then_inc(out_free, 1)
                    if hf == 0:
                        one_hots(t)
                        counts_rest(t)
                dve.wait_ge(kv_used, (hf + 1) * NT + 2)
                for k in range(2):
                    own = slice(k * HD, (k + 1) * HD)
                    dve.tensor_copy(kvT[own, :, own], bank(4).rearrange("q (g m) -> q g m", g=4)[own, :, own])\
                       .then_inc(kvT_step, 1)
                if hf == 0:
                    dve.wait_ge(deg_done, 1)
                    dve.tensor_copy(dtmp[:, 0, :], bank(CNT, NT)).then_inc(dg, 1)
                    dve.tensor_reduce(degi[:, 0:1], bank(CNT, NT), AX_X, ALU.max).then_inc(dg_max, 1)
                    dve.wait_ge(dg_sqrt, 1)
                    dve.reciprocal(dtmp[:, 2, :], dtmp[:, 1, :]).then_inc(dg, 1)
                    dve.wait_ge(dg, 2)
                    refine(dtmp[:, 0, :], dtmp[:, 2, :], dtmp[:, 3, :], dis[:], dg, 2)
                    dve.wait_ge(dg_max, 2)
                    dve.tensor_scalar(flag[:], degi[:, 1:2], float(EXACT_COUNT), None, ALU.is_gt)\
                       .then_inc(dg_max, 1)

            dve.wait_ge(bias_in, 80)
            for p in range(2):
                dve.wait_ge(m_st[p], 64)
            for t, p, i in tiles(dve):
                split_next("q", t, p, i)
                for h in range(2):
                    dve.wait_ge(q_relu, 2 * t + h + 1)
                    dve.wait_ge(out_ready, 2 * t + 2 * V["q"] + h + 1)
                    dve.tensor_tensor(tokA[:, p, h * W:(h + 1) * W], bank(2 * p + h),
                                      bias[:, h * W:(h + 1) * W], ALU.add)\
                       .then_inc(qb_ready if h == 0 else out_free, 1)

            dve.wait_ge(bias_in, 96)
            dve.wait_ge(q_relu, 2 * NT + 4)
            hp_hi, hp_lo = (m[:].rearrange("q t n -> q (t n)") for m in hp)
            for t, p, i in tiles(dve):
                split_next("h", t, p, i)
                for h in range(2):
                    dve.wait_ge(out_ready, 2 * t + 2 * V["h"] + h + 1)
                    last = dve.tensor_tensor(tokA[:, p, h * W:(h + 1) * W], bank(2 * p + h),
                                             bias[:, h * W:(h + 1) * W], ALU.add)
                last.then_inc(out_free, 1)
                dve.wait_ge(hhi_ready, t + 1)
                dve.scalar_tensor_tensor(out=hp_lo[:, bass.ds(t * D, D)], in0=tokA[:, p, :],
                                         scalar=dis[:, bass.ds(t, 1)],
                                         in1=hp_hi[:, bass.ds(t * D, D)].bitcast(F32),
                                         op0=ALU.mult, op1=ALU.subtract).then_inc(hlo_ready, 1)

            dve.wait_ge(bias_in, 112)

            def x_tile(t, p, i, between=None):
                xt, s, v = tokA[:, p, :], X_STEPS * t + 1, t + V["x"]
                split_next("x", t, p, i)
                dve.wait_ge(xt_in[p], 16 * i + 16)
                dve.tensor_tensor(xt, xt, bias[:], ALU.add).then_inc(x1s, 1)
                dve.wait_ge(x1s, s + 1)
                dve.wait_ge(out_ready, 2 * v + 1)
                dve.tensor_tensor(xt[:, 0:W], bank(2 * p), xt[:, 0:W], ALU.add).then_inc(x1s, 1)
                dve.wait_ge(out_ready, 2 * v + 2)
                dve.tensor_tensor(xt[:, W:D], bank(2 * p + 1), xt[:, W:D], ALU.add).then_inc(out_free, 1)
                if between:
                    between()
                dve.wait_ge(x1s, s + 2)
                dve.wait_ge(c_ready, 2 * t + 1)
                dve.scalar_tensor_tensor(out=xt[:, 0:W], in0=bank(4), scalar=dis[:, bass.ds(t, 1)],
                                         in1=xt[:, 0:W], op0=ALU.mult, op1=ALU.add).then_inc(x1s, 1)
                dve.wait_ge(out_free, v + 3)
                dve.wait_ge(c_ready, 2 * t + 2)
                dve.scalar_tensor_tensor(out=xt[:, W:D], in0=bank(5), scalar=dis[:, bass.ds(t, 1)],
                                         in1=xt[:, W:D], op0=ALU.mult, op1=ALU.add).then_inc(c_free, 1)
                dve.wait_ge(x1s, s + 3)

                def second_half():
                    dve.wait_ge(c_free, t + 2)
                    dve.wait_ge(tp_ready, 2 * t + T["x"])

                layernorm(xt, tokB[:, 0, :], x1s, s + 3, x1_sqrt, t + 1, x2_ready, second_half)

            def logits(t):
                dve.wait_ge(z_ready, t + 2)
                dve.tensor_scalar(zlog[:, bass.ds(NEXP * t, NEXP)], bank(7, NEXP), tmp_t[:, 1:2], None,
                                  ALU.mult).then_inc(z_read, 1)

            dve.wait_ge(in_small, 32)
            dve.reciprocal(tmp_t[:, 1:2], tmp_t[:, 0:1]).then_inc(x1s, 1)
            dve.wait_ge(x1s, 1)
            x_tile(0, 0, 0)
            x_tile(1, 1, 0)
            for t, p, i in tiles(dve, 1, NL):
                x_tile(t, p, i, lambda: logits(t - 2))
            split_next("gu0", 0, 0, 0)
            logits(NT - 2)
            logits(NT - 1)

            rs = [0]

            def route(ins):
                ins.then_inc(rt, 1)
                rs[0] += 1
                dve.wait_ge(rt, rs[0])

            def by_tile(m):
                return m.rearrange("q (t e) -> q t e", e=NEXP)

            def spread(m):
                return m.unsqueeze(2).to_broadcast([P, NT, NEXP])

            dve.wait_ge(c_ready, 2 * NT)
            dve.wait_ge(z_read, NT + 1)
            route(dve.tensor_scalar(r_c, zlog[:], LOGIT_MIN, None, ALU.max))
            dve.wait_ge(rt_act, 1)
            route(dve.tensor_scalar(r_inh, r_inh, 1.0, None, ALU.add))
            route(dve.reciprocal(r_inh, r_inh))
            route(dve.tensor_scalar(r_dist, r_inh, CENTER, None, ALU.subtract))
            route(dve.tensor_scalar(r_c, r_inh, -1.0, CENTER, ALU.mult, ALU.add))
            route(dve.tensor_tensor(r_dist, r_dist, r_c, ALU.max))
            route(dve.tensor_scalar(r_zone, zlog[:], ZONE_HIGH, None, ALU.is_le))
            route(dve.scalar_tensor_tensor(out=r_zone, in0=zlog[:], scalar=ZONE_LOW, in1=r_zone, op0=ALU.is_ge,
                                           op1=ALU.mult))
            dve.wait_ge(rt_act, 2)
            route(dve.tensor_tensor(r_w, r_w, r_zone, ALU.mult))
            route(dve.tensor_reduce(r_s, by_tile(r_w), AX_X, ALU.add))
            route(dve.tensor_scalar(r_none, r_s, 1e-8, None, ALU.is_lt))
            dve.wait_ge(rt_act, 3)
            route(dve.tensor_copy(r_c, r_fb))
            for e in range(NEXP):
                route(dve.memset(by_tile(r_rank)[:, :, e], float(NEXP - e)))
            for k in range(2):
                route(dve.tensor_reduce(r_s, by_tile(r_c), AX_X, ALU.max))
                route(dve.tensor_tensor(by_tile(r_eq), by_tile(r_c), spread(r_s), ALU.is_equal))
                route(dve.tensor_tensor(r_eq, r_eq, r_rank, ALU.mult))
                route(dve.tensor_reduce(r_s, by_tile(r_eq), AX_X, ALU.max))
                route(dve.tensor_tensor(by_tile(r_eq), by_tile(r_eq), spread(r_s), ALU.is_equal))
                if k == 0:
                    route(dve.tensor_copy(r_mask, r_eq))
                    route(dve.scalar_tensor_tensor(out=r_c, in0=r_eq, scalar=-2.0, in1=r_c, op0=ALU.mult,
                                                   op1=ALU.add))
            route(dve.tensor_tensor(r_mask, r_mask, r_eq, ALU.add))
            route(dve.tensor_tensor(r_fb, r_fb, r_mask, ALU.mult))

            def normalise(m):
                route(dve.tensor_reduce(r_s, by_tile(m), AX_X, ALU.add))
                route(dve.tensor_scalar(r_s, r_s, 1e-8, None, ALU.max))
                route(dve.reciprocal(r_s, r_s))
                route(dve.tensor_tensor(by_tile(m), by_tile(m), spread(r_s), ALU.mult))

            normalise(r_fb)
            route(dve.tensor_tensor(by_tile(r_fb), by_tile(r_fb), spread(r_none), ALU.mult))
            route(dve.tensor_scalar(r_none, r_none, -1.0, 1.0, ALU.mult, ALU.add))
            route(dve.tensor_tensor(by_tile(r_w), by_tile(r_w), spread(r_none), ALU.mult))
            route(dve.tensor_tensor(r_w, r_w, r_fb, ALU.add))
            normalise(r_w)
            route(dve.tensor_copy(wexp[:], r_w))

            for hf in range(2):
                name = f"gu{hf}"
                def hidden(t, p, i, split_too=True):
                    if split_too:
                        split_next(name, t, p, i)
                    dve.wait_ge(silu_ready, t + hf * NT + 1)
                    dve.wait_ge(out_ready, 2 * t + 2 * V[name] + 2)
                    dve.wait_ge(tp_ready, t + T[name] - 1)
                    for e in range(XH):
                        cols = slice(e * P, (e + 1) * P)
                        last = dve.scalar_tensor_tensor(
                            out=tokB[:, p, cols], in0=tokA[:, p, cols],
                            scalar=wexp[:, bass.ds(NEXP * t + hf * XH + e, 1)], in1=bank(2 * p + 1)[:, cols],
                            op0=ALU.mult, op1=ALU.mult)
                    last.then_inc(out_free, 1)

                if hf == 0:
                    hidden(0, 0, 0, split_too=False)
                    hidden(1, 1, 0)
                for t, p, i in tiles(dve, 1 - hf, NL):
                    hidden(t, p, i)

            def d_tile(t, p, i):
                dve.wait_ge(x1b_in[p], 16 * i + 16)
                for h in range(2):
                    dve.wait_ge(out_ready, 2 * t + 2 * V["d"] + h + 1)
                    cols = slice(h * W, (h + 1) * W)
                    last = dve.tensor_tensor(tokA[:, p, cols], bank(2 * p + h), tokA[:, p, cols], ALU.add)
                last.then_inc(out_free, 1)

            for t, p, i in tiles(dve, 0, NL - 1):
                split_next("d", t, p, i)
                d_tile(t, p, i)
            split_next("d", NT - 2, 0, NL - 1)
            d_tile(NT - 2, 0, NL - 1)
            d_tile(NT - 1, 1, NL - 1)

        @block.tensor
        def _(pe):
            pe.sem_inc(hot_used, 2)
            pe.sem_inc(act_used, 2)
            pe.sem_inc(kv_used, 2)
            pe.sem_inc(z_ready, 1)
            pe.wait_ge(consts, 12)

            def presence():
                pe.wait_ge(edge_step, 2 + NT + 1 + 1)
                for k, b in enumerate(PRES_BANK):
                    n = min(3, NT - 3 * k)
                    pe.matmul(bank(b)[0:1, 0:n * NCH], ones16[:, 0:1],
                              inT[:, 3 * k:3 * k + n, :].rearrange("q t c -> q (t c)"), start=True, stop=True)\
                      .then_inc(pres_mm, 1)

            def transposes(source, b):
                for k in range(4):
                    last = pe.transpose(bank(6 + b)[:, k * P:(k + 1) * P], source[:, k * P:(k + 1) * P], ident[:])
                last.then_inc(tp_ready, 1)

            def fold(n):
                target = bank(FOLD_BANK[n % 2])
                if n >= 2:
                    pe.wait_ge(fold_out, n - 1)
                if n < 4 * KC and n % KC == 0:
                    pe.wait_ge(in_w[n // KC], 16)
                for g in range(4):
                    if n < 4 * KC:
                        left = w_s[n // KC][:, g, n % KC * P:(n % KC + 1) * P]
                        right = pbd_s[:, n // KC % 2 * 4 + g, :]
                    else:
                        c = 4 * (n - 4 * KC) + g
                        left, right = bkq[:, c:c + 1], pbd_s[:, c % KC, :]
                    mm = pe.matmul(target[0:P if n < 4 * KC else 1, g * P:(g + 1) * P], left, right, start=True,
                                   stop=True)
                mm.then_inc(fold_mm, 1)

            for t in range(NT):
                if t == 2:
                    presence()
                    pe.wait_ge(in_fold, 16 * 3)
                if t >= 2:
                    for n in range(4 * (t - 2), 4 * (t - 2) + 4):
                        fold(n)
                pe.wait_ge(xn_ready, t + 1)
                for h in range(2):
                    pe.wait_ge(tp_out, 2 * t + h + 1)
                    transposes(tokB[:, t % 2, h * W:(h + 1) * W], h)
            for n in range(4 * KC, NFOLD):
                fold(n)

            seen = pe.alloc_register("pairs_counted")
            pe.reg_mov(seen, 0)

            def count(t):
                counts = ps[:, CNT * BANK:CNT * BANK + NP]
                blocks = [(slice(c, min(c + BANK, NP)), counts[:, c:min(c + BANK, NP)])
                          for c in range(0, NP, BANK)]
                pe.wait_ge(cnt_free, t + 1)
                for cols, target in blocks:
                    pe.matmul(target, zero16[:], iota[:, cols], start=True, stop=False)
                pe.matmul(counts[:, bass.ds(P * t, P)], id16[:], id16[:], start=False, stop=False)
                first, last = pair_range(pe, t)
                with pe.Fori(first, last):
                    n = pe.snap(seen)
                    for k in range(2):
                        pe.wait_ge(hot_ready, 2 * n + k + 1)
                        for cols, target in blocks:
                            mm = pe.matmul(target, dstHot[:, k, :], srcHot[:, k, cols], start=False, stop=False)
                        mm.then_inc(hot_used, 1)
                    pe.reg_add(seen, seen, 1)
                for cols, target in blocks:
                    mm = pe.matmul(target, zero16[:], iota[:, cols], start=False, stop=True)
                mm.then_inc(cnt_ready, 1)

            def gemm(name, t, p):
                u, v = t + U[name], t + V[name]
                hi, lo = PANELS[name]
                pe.wait_ge(act_hi, u + 1)
                pe.wait_ge(act_lo, u + 1)
                pe.wait_ge(out_free, v + 1)
                for h in range(2):
                    target = bank(2 * p + h)
                    for kc in range(KC):
                        ah = actH[:, p, kc * P:(kc + 1) * P]
                        al = actL[:, p, kc * P:(kc + 1) * P]
                        pe.matmul(target, ah, hi[:, h, kc, :], start=(kc == 0), stop=False)
                        mm = pe.matmul(target, ah, lo[:, h, kc, :], start=False, stop=False)
                        if h == 1 and kc == KC - 1:
                            mm.then_inc(act_used, 1)
                        mm = pe.matmul(target, al, hi[:, h, kc, :], start=False, stop=(kc == KC - 1))
                    mm.then_inc(out_ready, 1)

            def panels(name):
                pe.wait_ge(pan_lo, before(name) + NPIECE)
                pe.wait_ge(pan_hi, before(name) + NPIECE)

            def gemm_first(name, h, first=0, last=KC):
                u, v = U[name], V[name]
                hi, lo = PANELS[name]
                for kc in range(first, last):
                    piece = before(name) + (h * KC + kc) // 2
                    if kc % 2 == 0 and (h or name not in FIRST):
                        pe.wait_ge(pan_lo, piece + 1)
                        pe.wait_ge(pan_hi, piece + 1)
                    for p in range(2):
                        if kc == 0 and h == 0:
                            pe.wait_ge(act_hi, u + p + 1)
                            pe.wait_ge(act_lo, u + p + 1)
                            pe.wait_ge(out_free, v + p + 1)
                        target = bank(2 * p + h)
                        ah = actH[:, p, kc * P:(kc + 1) * P]
                        al = actL[:, p, kc * P:(kc + 1) * P]
                        pe.matmul(target, ah, hi[:, h, kc, :], start=(kc == 0), stop=False)
                        mm = pe.matmul(target, ah, lo[:, h, kc, :], start=False, stop=False)
                        if h == 1 and kc == KC - 1:
                            mm.then_inc(act_used, 1)
                        mm = pe.matmul(target, al, hi[:, h, kc, :], start=False, stop=(kc == KC - 1))
                        if kc == KC - 1 and (h, p) != (0, 1):
                            mm.then_inc(out_ready, 1 + (h == 1 and p == 1))

            for hf in range(2):
                name = f"kv{hf}"

                def kv(t, p, first=False, last=False):
                    pe.wait_ge(k_ready, t + hf * NT + 1)
                    pe.wait_ge(out_free, t + V[name] + 3)
                    for g in range(4):
                        mm = pe.matmul(bank(4)[:, g * P:(g + 1) * P], tokA[:, p, W + g * P:W + (g + 1) * P],
                                       tokB[:, p, g * P:(g + 1) * P], start=first and g == 0,
                                       stop=last and g == 3)
                    mm.then_inc(kv_used, 1)

                def counted(t):
                    if hf == 0:
                        count(t)

                if hf == 0:
                    pe.wait_ge(fold_out, KC)
                    pe.wait_ge(fold_lo, KC)
                    gemm_first(name, 0)
                    gemm_first(name, 1)
                    pe.wait_ge(edge_step, EDGE_STEPS)
                else:
                    panels(name)
                    gemm(name, 0, 0)
                    gemm(name, 1, 1)
                counted(0)
                kv(0, 0, first=True)
                with pe.Fori(0, NL - 1) as i:
                    for p in (1, 0):
                        t = 2 * i + 2 - p
                        counted(t)
                        gemm(name, t + 1, 1 - p)
                        kv(t, p)
                counted(NT - 1)
                kv(NT - 1, 1, last=True)
                pe.wait_ge(kvT_step, 1 + 2 * (hf + 1))
                for g in range(4):
                    v, p = V[f"m{hf}"] + g, g % 2
                    pe.wait_ge(wo_in[p], 16 * (2 * hf + g // 2 + 1))
                    pe.wait_ge(out_free, v + 1)
                    for h in range(2):
                        pe.matmul(bank(2 * p + h), kvT[:, g, :], woP[:, p, h * W:(h + 1) * W], start=True,
                                  stop=True).then_inc(out_ready, 1)
                if hf == 0:
                    pe.wait_ge(cnt_free, NT + 1)
                    for c in range(NT):
                        mm = pe.matmul(bank(CNT)[:, c:c + 1], acc[:, c * P:(c + 1) * P], ones[:], start=True,
                                       stop=True)
                    mm.then_inc(deg_done, 1)

            def q_transposes(t, p, i):
                for h in range(2):
                    pe.wait_ge(q_relu, 4 + 2 * t + h + 1)
                    pe.wait_ge(tp_out, 2 * t + T["q"] + h + 1)
                    transposes(tokB[:, p, h * W:(h + 1) * W], h)

            panels("q")
            staggered(pe, lambda t, p, i: gemm("q", t, p), q_transposes)

            panels("h")
            for t, p, i in tiles(pe):
                gemm("h", t, p)

            for h in range(2):
                gemm_first("x", h)
            pe.wait_ge(hlo_ready, NT)
            pe.wait_ge(dg_max, 3)
            pe.wait_ge(in_small, 32)
            big = pe.value_load(flag[0:1, 0:1], min_val=0, max_val=1)

            def aggregate(t, p, i):
                pe.wait_ge(chi_in[p], 16 * i + 16)
                pe.wait_ge(clo_in, 16 * t + 16)
                pe.wait_ge(c_free, t + 1)
                for h in range(2):
                    cols = slice(h * W, (h + 1) * W)
                    for c in range(NT):
                        pe.matmul(bank(4 + h), cHi[:, p, c, :], hp[0][:, c, cols], start=(c == 0), stop=False)
                    with pe.If(big != 0):
                        for c in range(NT):
                            pe.matmul(bank(4 + h), cLo[:, c, :], hp[0][:, c, cols], start=False, stop=False)
                    for c in range(NT):
                        mm = pe.matmul(bank(4 + h), cHi[:, p, c, :], hp[1][:, c, cols], start=False,
                                       stop=(c == NT - 1))
                    mm.then_inc(c_ready, 1)

            def x_transposes(t):
                pe.wait_ge(x2_ready, t + 1)
                pe.wait_ge(z_read, t + 1)
                for h in range(2):
                    pe.wait_ge(tp_out, 2 * t + T["x"] + h + 1)
                    transposes(tokB[:, 0, h * W:(h + 1) * W], h)

            def router(t):
                pe.wait_ge(tp_out, 2 * t + T["x"] + 4)
                for kc in range(KC):
                    mm = pe.matmul(bank(7, NEXP), outT[:, 1, kc * P:(kc + 1) * P],
                                   wr[:, kc * NEXP:(kc + 1) * NEXP], start=(kc == 0), stop=(kc == KC - 1))
                mm.then_inc(z_ready, 1)

            aggregate(0, 0, 0)
            aggregate(1, 1, 0)
            x_transposes(0)
            for t, p, i in tiles(pe, 1, NL):
                gemm("x", t, p)
                router(t - 2)
                aggregate(t, p, i)
                x_transposes(t - 1)
            router(NT - 2)
            gemm_first("gu0", 0, 0, KC // 2)
            x_transposes(NT - 1)
            gemm_first("gu0", 0, KC // 2, KC)
            router(NT - 1)
            gemm_first("gu0", 1)

            for hf in range(2):
                name = f"gu{hf}"

                def h_transposes(t, p, i):
                    pe.wait_ge(out_free, t + V[name] + 3)
                    pe.wait_ge(tp_out, t + T[name] + 1)
                    transposes(tokB[:, p, 0:W], p)

                if hf == 0:
                    h_transposes(0, 0, 0)
                    with pe.Fori(0, NL - 1) as i:
                        for p in range(2):
                            gemm(name, 2 * i + p + 2, p)
                            h_transposes(2 * i + p + 1, 1 - p, i + p)
                    h_transposes(NT - 1, 1, NL - 1)
                else:
                    panels(name)
                    staggered(pe, lambda t, p, i: gemm(name, t, p), h_transposes)

            panels("d")
            for t, p, i in tiles(pe):
                gemm("d", t, p)


def _panels(w, np):
    return w.reshape(KC, P, 2, W).transpose(2, 1, 0, 3).reshape(2, P, KC * W)


def _layouts(np, x, src, dst, L0_gnn_W, L0_gnn_b, L0_mix_Wq, L0_mix_bq, L0_mix_Wk, L0_mix_bk, L0_mix_Wv, L0_mix_bv,
             L0_mix_Wo, L0_mix_bo, L0_mix_P, L0_ffn_Wg, L0_ffn_Wu, L0_ffn_Wd, L0_ffn_Wr, L0_ffn_temperature):
    def rows(w):
        return w.reshape(KC, P, -1).transpose(1, 0, 2)

    def edges(e):
        full = np.full(NCH * P, -1, dtype=e.dtype)
        full[:E_EDGES] = e
        return full.reshape(NCH, P).T

    xp = np.zeros((NP, D), dtype=x.dtype)
    xp[:N] = x
    pbd = np.zeros((P, KC, P), dtype=L0_mix_P.dtype)
    for h in range(2 * KC):
        k = h % 2 * HD
        pbd[k:k + HD, h // 2, k:k + HD] = L0_mix_P[h].T
    gate_up = np.stack([_panels(w.transpose(1, 0, 2).reshape(D, D), np) for w in (L0_ffn_Wg, L0_ffn_Wu)], axis=1)
    return [xp.reshape(NT, P, D), edges(src), edges(dst), rows(L0_mix_Wk), rows(L0_mix_Wq), pbd,
            L0_mix_bk.reshape(KC, P).T, L0_mix_bq.reshape(KC, P).T, _panels(L0_mix_Wv.T, np),
            L0_mix_bv.reshape(1, D), _panels(L0_gnn_W.T, np), L0_gnn_b.reshape(1, D),
            L0_mix_Wo.T.reshape(KC, P, D), L0_mix_bo.reshape(1, D), gate_up,
            _panels(L0_ffn_Wd.reshape(D, D), np), rows(L0_ffn_Wr).reshape(P, KC * NEXP),
            L0_ffn_temperature.reshape(1, 1)]


def kernel(**inputs):
    import numpy as np
    import concourse.bacc as bacc
    from concourse.bass_utils import run_bass_kernel_spmd

    nc = bacc.Bacc("TRN2", target_bir_lowering=False, num_devices=1)
    arrays, args = {}, []
    for k, a in enumerate(_layouts(np, **{name: np.asarray(a) for name, a in inputs.items()})):
        a = np.ascontiguousarray(a)
        arrays[f"in_{k}"] = a
        args.append(nc.dram_tensor(f"in_{k}", a.shape, mybir.dt.from_np(a.dtype), kind="ExternalInput").ap())
    args.append(nc.dram_tensor("out", (NT, P, D), F32, kind="ExternalOutput").ap())
    gps_layer(nc, *args)
    r = run_bass_kernel_spmd(nc, [arrays], core_ids=[0])
    return r.results[0]["out"].reshape(NP, D)[:N]
```

```python
from contextlib import ExitStack

import concourse.bass as bass
import numpy as np
from concourse import mybir

F32 = mybir.dt.float32
F32R = mybir.dt.float32r
F16 = mybir.dt.float16
I32 = mybir.dt.int32
ALU = mybir.AluOpType
ACT = mybir.ActivationFunctionType
AX_X = mybir.AxisListType.X
RMAX = bass.bass_isa.ReduceOp.max

P = 128
N = 1250
D = 1024
NT = (N + P - 1) // P
NP = NT * P
NL = NT // 2
KC = D // P
W = D // 2
BANK = 512
HD = 64
E_EDGES = 20000
GROUP = 4
NGRP = (E_EDGES + GROUP * P - 1) // (GROUP * P)
NCH = GROUP * NGRP
NEXP = 8
XH = NEXP // 2
EPS = 1e-5
PIECE = 1024
NPIECE = 2 * KC * W // PIECE
EXACT_COUNT = 4096
ZONE_LOW = -1.31100973754
ZONE_HIGH = 1.1e-7
LOGIT_MIN = -80.0
CENTER = 0.36787944117144233

KB = 1024
BASE = 16512
OFF_A = BASE
OFF_B = OFF_A + 80 * KB
OFF_E = OFF_A + 64 * KB
OFF_AF = OFF_B + 64 * KB
OFF_AH = OFF_AF + 8 * KB
OFF_AL = OFF_AH + 8 * KB
OFF_TA = OFF_AL + 8 * KB
OFF_TB = OFF_TA + 8 * KB
OFF_OT = OFF_TB + 8 * KB
OFF_BIAS = OFF_OT + 8 * KB
OFF_STG = OFF_BIAS + 4 * KB
OFF_SM = OFF_STG + 10 * KB


def gps_layer(nc, x, src, dst, wk_nat, wq_nat, pbd, bk_col, bq_col, wv_pan, bv, wh_pan, bh, wo_t, bo,
              wgu_pan, wd_pan, wr_t, temp, out):
    ctx = ExitStack()
    with ctx:
        def at(name, shape, dt, off):
            return nc.alloc_sbuf_tensor_at(name, shape, dt, offset=off)

        def sem(name):
            return ctx.enter_context(nc.semaphore(name))

        def dram(name, shape, dt=F32):
            return nc.dram_tensor(name, shape, dt, kind="Internal").ap()

        xnT_d = dram("xnT_d", [NT, P, D])
        qT_d = dram("qT_d", [NT, P, D])
        x1_d = dram("x1_d", [NT, P, D])
        x2T_d = dram("x2T_d", [NT, P, D])
        hT_d = dram("hT_d", [NT, P, D])
        qfold_d = dram("qfold_d", [2, P, KC, W])
        m_d = dram("m_d", [2, P, KC, W])
        fbias_d = dram("fbias_d", [2, D])
        chi_d = dram("chi_d", [NT, P, NP])
        clo_d = dram("clo_d", [NT, P, NP])

        panA = [at("panA_hi", [P, 2, KC, W], F32R, OFF_A), at("panA_lo", [P, 2, KC, W], F32R, OFF_A + 32 * KB)]
        panB = [at("panB_hi", [P, 2, KC, W], F32R, OFF_B), at("panB_lo", [P, 2, KC, W], F32R, OFF_B + 32 * KB)]
        hp = [at("hp_hi", [P, NT, D], F32R, OFF_A), at("hp_lo", [P, NT, D], F32R, OFF_A + 40 * KB)]
        actF = at("actF", [P, 2, D], F32, OFF_AF)
        actH = at("actH", [P, 2, D], F32R, OFF_AH)
        actL = at("actL", [P, 2, D], F32R, OFF_AL)
        tokA = at("tokA", [P, 2, D], F32, OFF_TA)
        tokB = at("tokB", [P, 2, D], F32, OFF_TB)
        outT = at("outT", [P, 2, D], F32, OFF_OT)
        woP = at("woP", [P, 2, D], F32, OFF_OT)
        bias = at("bias", [P, D], F32, OFF_BIAS)
        stage = at("stage", [P, 2, PIECE], F32, OFF_STG)
        cHi = at("cHi", [P, 2, NT, P], F32R, OFF_STG)
        cLo = at("cLo", [P, NT, P], F32R, OFF_TB + 4 * KB)
        small = [OFF_SM]

        def sm(name, cols, dt=F32, size=4):
            off = small[0]
            small[0] += (cols * size + 31) // 32 * 32
            return at(name, [P, cols], dt, off)

        ident = sm("ident", P)
        wr = sm("wr", KC * NEXP)
        zlog = sm("zlog", NT * NEXP)
        wexp = sm("wexp", NT * NEXP)
        dis = sm("dis", NT)
        vscale = sm("vscale", NT)
        tmp_t = sm("tmp_t", 2)
        st6 = sm("st6", 12)
        mv = sm("mv", 2)
        nrm = sm("nrm", 8)
        degi = sm("degi", 2)
        flag = sm("flag", 1, I32)
        ones = sm("ones", 1)
        assert small[0] <= 229368

        kvT = at("kvT", [P, 4, P], F32, OFF_TB + 2 * KB)
        w_s = [at(f"w_s{k}", [P, 4, D], F32, (OFF_A, OFF_B)[k // 2] + (16 + 32 * (k % 2)) * KB) for k in range(4)]
        xin = at("xin", [P, 4, D], F32, OFF_AL)
        pbd_s = at("pbd_s", [P, KC, P], F32, OFF_BIAS)
        size = {F32: 4, I32: 4, F16: 2}

        def lay_out(items, start, stop):
            tensors = []
            for name, shape, dt in items:
                tensors.append(at(name, shape, dt, start))
                start += (int(np.prod(shape[1:])) * size[dt] + 31) // 32 * 32
            assert start <= stop
            return tensors

        srcI, dstI, ge, inT, ones16, pres, up, down, prod, rngF = lay_out((
            ("srcI", [P, NCH], I32), ("dstI", [P, NCH], I32), ("ge", [P, NT + 1, NCH], F16),
            ("inT", [P, NT, NCH], F16), ("ones16", [P, 2], F16), ("pres", [1, NT, NGRP], F16),
            ("up", [1, NT, NGRP], F16), ("down", [1, NT, NGRP], F16), ("prod", [1, NT, NGRP], F16),
            ("rngF", [1, NT, 2], F32)), OFF_AF, OFF_AL)
        qfold = at("qfold", [P, 4, W], F32, OFF_AH)
        dstHot, iota, srcF, dstF, id16, zero16, acc, rowid, rng, bkq, dtmp, fold, lnw = lay_out((
            ("dstHot", [P, GROUP, P], F16), ("iota", [P, NP], F16),
            ("srcF", [P, NCH], F32), ("dstF", [P, NCH], F32), ("id16", [P, P], F16), ("zero16", [P, P], F16),
            ("acc", [P, NP], F32), ("rowid", [P, NT], F32), ("rng", [1, NT, 2], I32), ("bkq", [P, 2 * KC], F32),
            ("dtmp", [P, 4, NT], F32), ("fold", [P, 2, W], F32), ("lnw", [P, 2, 20], F32)), OFF_E, OFF_B)
        c0 = at("c0", [P, NP], F32R, OFF_B + 16 * KB)
        c1 = at("c1", [P, NP], F32R, OFF_B + 21 * KB)
        srcHot = at("srcHot", [P, GROUP, NP], F16, OFF_B + 48 * KB)
        late = at("late", [P, 4, PIECE], F32, OFF_E)
        route_t = at("route_t", [P, 9, NT * NEXP], F32, OFF_TB + 4 * KB)
        r_inh, r_dist, r_zone, r_w, r_fb, r_c, r_eq, r_rank, r_mask = (route_t[:, k, :] for k in range(9))
        route_s = at("route_s", [P, 2, NT], F32, OFF_TB + 7 * KB)
        r_s, r_none = (route_s[:, k, :] for k in range(2))

        ps = nc.alloc_psum_tensor("ps", [P, 8 * BANK], F32)

        def bank(b, n=BANK):
            return ps[:, b * BANK:b * BANK + n]

        in_x = [sem(f"in_x{k}") for k in range(4)]
        in_fold = sem("in_fold")
        in_edges = sem("in_edges")
        in_small = sem("in_small")
        consts = sem("consts")
        fold_mm = sem("fold_mm")
        fold_out = sem("fold_out")
        fold_lo = sem("fold_lo")
        fb_st = [sem(f"fb_st{p}") for p in range(2)]
        fold_st = [sem(f"fold_st{k}") for k in range(4)]
        ln_step = sem("ln_step")
        ln_sqrt = sem("ln_sqrt")
        xn_ready = sem("xn_ready")
        tp_ready = sem("tp_ready")
        tp_out = sem("tp_out")
        tr_st = [sem(f"tr_st{p}") for p in range(2)]
        in_w = [sem(f"in_w{k}") for k in range(4)]
        edge_step = sem("edge_step")
        pres_mm = sem("pres_mm")
        hot_ready = sem("hot_ready")
        hot_used = sem("hot_used")
        cnt_ready = sem("cnt_ready")
        cnt_free = sem("cnt_free")
        deg_done = sem("deg_done")
        chi_out = sem("chi_out")
        clo_out = sem("clo_out")
        chi_st = sem("chi_st")
        clo_st = sem("clo_st")
        dg = sem("dg")
        dg_sqrt = sem("dg_sqrt")
        dg_max = sem("dg_max")
        act_in = [sem(f"act_in{p}") for p in range(2)]
        act_hi = sem("act_hi")
        act_lo = sem("act_lo")
        act_used = sem("act_used")
        stg_in = [sem(f"stg_in{p}") for p in range(2)]
        stg_sp = [sem(f"stg_sp{k}") for k in range(NPIECE)]
        pan_hi = sem("pan_hi")
        pan_lo = sem("pan_lo")
        bias_in = sem("bias_in")
        out_ready = sem("out_ready")
        out_free = sem("out_free")
        kb_ready = sem("kb_ready")
        k_ready = sem("k_ready")
        kv_used = sem("kv_used")
        kvT_step = sem("kvT_step")
        wo_in = [sem(f"wo_in{p}") for p in range(2)]
        m_st = [sem(f"m_st{p}") for p in range(2)]
        qb_ready = sem("qb_ready")
        q_relu = sem("q_relu")
        hhi_ready = sem("hhi_ready")
        hlo_ready = sem("hlo_ready")
        xt_in = [sem(f"xt_in{p}") for p in range(2)]
        chi_in = [sem(f"chi_in{p}") for p in range(2)]
        clo_in = sem("clo_in")
        c_ready = sem("c_ready")
        c_free = sem("c_free")
        x1s = sem("x1s")
        x1_sqrt = sem("x1_sqrt")
        x1_st = [sem(f"x1_st{p}") for p in range(2)]
        x2_ready = sem("x2_ready")
        z_ready = sem("z_ready")
        z_read = sem("z_read")
        rt = sem("rt")
        rt_act = sem("rt_act")
        silu_ready = sem("silu_ready")
        x1b_in = [sem(f"x1b_in{p}") for p in range(2)]
        o_st = [sem(f"o_st{p}") for p in range(2)]

        U = {"kv0": 0, "kv1": NT, "q": 2 * NT, "h": 3 * NT, "x": 4 * NT, "gu0": 5 * NT, "gu1": 6 * NT,
             "d": 7 * NT}
        V = {"kv0": 0, "m0": NT, "kv1": NT + 4, "m1": 2 * NT + 4, "q": 2 * NT + 8, "h": 3 * NT + 8,
             "x": 4 * NT + 8, "gu0": 5 * NT + 8, "gu1": 6 * NT + 8, "d": 7 * NT + 8}
        T = {"ln": 0, "q": 2 * NT, "x": 4 * NT, "gu0": 6 * NT, "gu1": 7 * NT}
        FIRST = {"kv0": NPIECE // 2, "kv1": NPIECE // 2}
        JOBS = ("kv0", "kv1", "q", "h", "x", "gu0", "gu1", "d")
        SP_PAIRS = ("x", "gu0")
        POOL_PAIRS = ("kv0", "kv1", "q", "h", "gu1", "d")

        def staged(name, k):
            if name == "x" and k % 4 >= 2:
                return outT[:, k % 4 - 2, :]
            if name == "gu0" and 2 <= k < 6:
                return late[:, k - 2, :]
            return stage[:, k % 2, :]

        def before(name, names=JOBS):
            return sum(NPIECE - FIRST.get(n, 0) for n in names[:names.index(name)]) - FIRST.get(name, 0)

        PANELS = {"kv0": panA, "kv1": panB, "q": panA, "h": panB, "x": panB, "gu0": panB, "gu1": panA,
                  "d": panB}
        LN_STEPS = 10
        X_STEPS = LN_STEPS + 3
        FOLD_BANK = (0, 3)
        CNT = 5
        NFOLD = 4 * KC + 4
        FOLD_START = (0, 0, 0, 5, 10, 15, 20, 26, 31, 36, 36)
        PRES_BANK = (1, 2, 4, 5)
        EDGE_STEPS = 2 + (NT + 1) + 1 + 1 + len(PRES_BANK) + 1 + 4 + 4

        block = ctx.enter_context(nc.Block())

        def tiles(eng, first=0, last=NL):
            with eng.Fori(first, last) as i:
                for p in range(2):
                    yield 2 * i + p, p, i

        def group_range(eng, t):
            at_t = rng[:].rearrange("a t c -> a (t c)")
            return (eng.value_load(at_t[0:1, bass.ds(2 * t, 1)], min_val=0, max_val=NGRP - 1),
                    eng.value_load(at_t[0:1, bass.ds(2 * t + 1, 1)], min_val=1, max_val=NGRP))

        def staggered(eng, front, back, extra=None):
            front(0, 0, 0)
            for t, p, i in tiles(eng, 0, NL - 1):
                front(t + 1, 1 - p, i + p)
                back(t, p, i)
                if extra:
                    extra(t, p)
            front(NT - 1, 1, NL - 1)
            back(NT - 2, 0, NL - 1)
            back(NT - 1, 1, NL - 1)

        @block.sync
        def _(sp):
            for s in (*tr_st, chi_st, clo_st):
                sp.sem_inc(s, 16)

            def load_act(source, t, u, p):
                sp.wait_ge(act_lo, u - 1)
                sp.dma_start(actF[:, p, :], source[t]).then_inc(act_in[p], 16)

            def load_bias(parts, v_before):
                if v_before:
                    sp.wait_ge(out_free, v_before + 2)
                n = D // len(parts)
                for k, part in enumerate(parts):
                    sp.dma_start(bias[:, k * n:(k + 1) * n], part.to_broadcast([P, n])).then_inc(bias_in, 16)

            mf = m_d.rearrange("h q k n -> h q (k n)")

            def load_pieces(name, first, second, start, stop, ahead):
                n0, half = before(name), NPIECE // 2
                for k in range(start, stop):
                    sp.wait_ge(pan_lo, n0 + max(k - ahead + 1, 0))
                    source = first if k < half else second
                    at = k % half * PIECE
                    sp.dma_start(staged(name, k), source[:, at:at + PIECE]).then_inc(stg_sp[k], 16)

            for t in range(4):
                sp.dma_start(xin[:, t, :], x[t]).then_inc(in_x[t], 16)
            sp.dma_start(wr[:], wr_t).then_inc(in_small, 16)
            sp.dma_start(tmp_t[:, 0:1], temp.to_broadcast([P, 1])).then_inc(in_small, 16)
            for t in range(NT):
                if t + 4 < NT:
                    sp.wait_ge(xn_ready, t + 1)
                    sp.dma_start(xin[:, t % 4, :], x[t + 4]).then_inc(in_x[t % 4], 16)
                if t == NT - 2:
                    sp.wait_ge(edge_step, EDGE_STEPS)
                    for p in range(2):
                        sp.wait_ge(tr_st[p], 16 * 2)
                        sp.dma_start(actF[:, p, :], xnT_d[p]).then_inc(act_in[p], 16)
                sp.wait_ge(tp_out, 2 * t + 4)
                sp.dma_start(xnT_d[t], outT[:, t % 2, :]).then_inc(tr_st[t % 2], 16)
            for p in range(2):
                sp.wait_ge(tr_st[p], 16 * (1 + NL))
            for p in range(2):
                sp.wait_ge(fb_st[p], 16 * 2)
            sp.wait_ge(fold_mm, NFOLD)

            def store_counts(t):
                sp.wait_ge(chi_out, t + 1)
                sp.dma_start(chi_d[t], c0[:].bitcast(F32)).then_inc(chi_st, 16)
                sp.wait_ge(clo_out, t + 1)
                sp.dma_start(clo_d[t], c1[:].bitcast(F32)).then_inc(clo_st, 16)

            for hf in range(2):
                u0, vm = U[f"kv{hf}"], V[f"m{hf}"]
                load_bias([fbias_d[0:1, hf * W:(hf + 1) * W], bv[:, hf * W:(hf + 1) * W]], V["kv1"] if hf else 0)
                if hf == 0:
                    for g in range(2):
                        sp.dma_start(woP[:, g, :], wo_t[g]).then_inc(wo_in[g], 16)
                for t, p, i in tiles(sp, 0, NL - 1):
                    load_act(xnT_d, t + 2, t + u0 + 2, p)
                    if hf == 0:
                        store_counts(t)
                for t in range(2):
                    load_act(xnT_d, t, u0 + NT + t, t)
                    if hf == 0:
                        store_counts(NT - 2 + t)
                for g in range(4 + 1):
                    if 2 * (1 - hf) <= g < 4:
                        if g >= 2:
                            sp.wait_ge(out_ready, 2 * (vm + g - 1))
                        elif hf:
                            sp.wait_ge(out_ready, 2 * (V["m0"] + 4))
                        sp.dma_start(woP[:, g % 2, :], wo_t[4 * hf + g]).then_inc(wo_in[g % 2], 16)
                    if g >= 1:
                        k = g - 1
                        sp.wait_ge(out_free, vm + k + 3)
                        sp.dma_start(m_d[:, :, 4 * hf + k, :].rearrange("h q n -> q h n"),
                                     tokA[:, k % 2, :].rearrange("q (h n) -> q h n", h=2))\
                          .then_inc(m_st[k % 2], 16)

            load_bias([fbias_d[1:2, :]], V["q"])
            for t, p, i in tiles(sp, 0, NL - 1):
                load_act(xnT_d, t + 2, t + U["q"] + 2, p)
                sp.wait_ge(tp_out, 2 * t + T["q"] + 4)
                sp.dma_start(qT_d[t], outT[:, p, :]).then_inc(tr_st[p], 16)
            for t in range(2):
                load_act(xnT_d, t, U["h"] + t, t)
            for t in (NT - 2, NT - 1):
                sp.wait_ge(tp_out, 2 * t + T["q"] + 4)
                sp.dma_start(qT_d[t], outT[:, t % 2, :]).then_inc(tr_st[t % 2], 16)
            load_bias([bh], V["h"])
            for t, p, i in tiles(sp, 0, NL - 1):
                load_act(xnT_d, t + 2, t + U["h"] + 2, p)
            for p in range(2):
                sp.wait_ge(tr_st[p], 16 * (1 + 2 * NL))
            for t in range(2):
                load_act(qT_d, t, U["x"] + t, t)

            for p in range(2):
                sp.wait_ge(m_st[p], 16 * 4)
            load_pieces("x", mf[0], mf[1], 0, 4, 4)
            load_bias([bo], V["x"])
            load_pieces("x", mf[0], mf[1], 4, NPIECE, 4)
            sp.wait_ge(hlo_ready, NT)
            for p in range(2):
                sp.dma_start(tokA[:, p, :], x[p]).then_inc(xt_in[p], 16)
            sp.wait_ge(pan_lo, before("x") + NPIECE)

            def load_counts(t, p):
                sp.dma_start(cHi[:, p].bitcast(F32), chi_d[:, :, bass.ds(t * P, P)].rearrange("c q r -> q c r"))\
                  .then_inc(chi_in[p], 16)

            def load_rest(t):
                sp.dma_start(cLo[:].bitcast(F32), clo_d[:, :, bass.ds(t * P, P)].rearrange("c q r -> q c r"))\
                  .then_inc(clo_in, 16)

            load_counts(0, 0)
            load_counts(1, 1)
            load_rest(0)

            def store_x(t, p):
                sp.wait_ge(c_free, t + 2)
                sp.dma_start(x1_d[t], tokA[:, p, :]).then_inc(x1_st[p], 16)

            def store_x2(t):
                sp.wait_ge(tp_out, 2 * t + T["x"] + 4)
                sp.dma_start(x2T_d[t], outT[:, 1, :]).then_inc(tr_st[1], 16)

            for t, p, i in tiles(sp, 0, NL - 1):
                load_act(qT_d, t + 2, t + U["x"] + 2, p)
                sp.wait_ge(c_ready, 2 * t + 2)
                load_counts(t + 2, p)
                load_rest(t + 1)
                store_x(t, p)
                sp.wait_ge(x1_st[p], 16 * i + 16)
                sp.wait_ge(x2_ready, t + 1)
                sp.dma_start(tokA[:, p, :], x[t + 2]).then_inc(xt_in[p], 16)
                store_x2(t)
            for t in (NT - 2, NT - 1):
                p = t % 2
                if t < NT - 1:
                    sp.wait_ge(c_ready, 2 * t + 2)
                    load_rest(t + 1)
                    load_pieces("gu0", wgu_pan[0, 0], wgu_pan[0, 1], 0, 1, 6)
                    for k in range(2):
                        sp.wait_ge(tr_st[1], 16 * (1 + 2 * NL + k + 1))
                        load_act(x2T_d, k, U["gu0"] + k, k)
                if t < NT - 1:
                    store_x(t, p)
                    store_x2(t)
            sp.wait_ge(c_ready, 2 * NT)
            load_pieces("gu0", wgu_pan[0, 0], wgu_pan[0, 1], 1, 6, 6)
            store_x(NT - 1, 1)
            load_pieces("gu0", wgu_pan[0, 0], wgu_pan[0, 1], 6, NPIECE, 6)
            store_x2(NT - 1)

            for hf in range(2):
                name = f"gu{hf}"

                def store_h(t, p):
                    sp.wait_ge(tp_out, t + T[name] + 3)
                    sp.dma_start(hT_d[t][:, hf * W:(hf + 1) * W], outT[:, p, 0:W]).then_inc(tr_st[p], 16)

                if hf == 0:
                    sp.wait_ge(tr_st[1], 16 * (1 + 2 * NL + NT))
                for t, p, i in tiles(sp, 0, NL - 1):
                    load_act(x2T_d, t + 2, t + U[name] + 2, p)
                    store_h(t, p)
                for t in range(2):
                    if hf:
                        sp.wait_ge(tr_st[t], 16 * (1 + 2 * NL + (NT if t else 0) + NL + 1))
                    load_act(hT_d if hf else x2T_d, t, U[name] + NT + t, t)
                for t in (NT - 2, NT - 1):
                    store_h(t, t % 2)

            sp.wait_ge(out_free, V["d"] + 2)
            for p in range(2):
                sp.wait_ge(x1_st[p], 16 * NL)
                sp.wait_ge(tr_st[p], 16 * (1 + 4 * NL + (NT if p else 0)))
            for p in range(2):
                sp.dma_start(tokA[:, p, :], x1_d[p]).then_inc(x1b_in[p], 16)
            for t, p, i in tiles(sp, 0, NL - 1):
                load_act(hT_d, t + 2, t + U["d"] + 2, p)
                sp.wait_ge(out_free, t + V["d"] + 3)
                sp.dma_start(out[t], tokA[:, p, :]).then_inc(o_st[p], 16)
                sp.wait_ge(o_st[p], 16 * i + 16)
                sp.dma_start(tokA[:, p, :], x1_d[t + 2]).then_inc(x1b_in[p], 16)
            for t in (NT - 2, NT - 1):
                sp.wait_ge(out_free, t + V["d"] + 3)
                sp.dma_start(out[t], tokA[:, t % 2, :]).then_inc(o_st[t % 2], 16)
            for p in range(2):
                sp.wait_ge(o_st[p], 16 * NL)

        @block.gpsimd
        def _(pool):
            for m in (ident, id16, zero16, acc):
                pool.memset(m[:], 0.0).then_inc(consts, 1)
            for m in (ones16, ones):
                pool.memset(m[:], 1.0).then_inc(consts, 1)
            for m, pattern, base, channel in ((iota, [[1, NP]], 0, 0), (rowid, [[P, NT]], 0, 1),
                                              (up, [[0, NT], [1, NGRP]], 1, 0),
                                              (down, [[0, NT], [-1, NGRP]], NGRP, 0)):
                pool.iota(m[:], pattern, base=base, channel_multiplier=channel,
                          allow_small_or_imprecise_dtypes=True).then_inc(consts, 1)
            pool.wait_ge(consts, 10)
            for m in (ident, id16):
                pool.affine_select(out=m[:], in_=m[:], compare_op=ALU.not_equal, fill=1.0, base=0,
                                   pattern=[[-1, P]], channel_multiplier=1).then_inc(consts, 1)

            def load_pair(name, first, second):
                n0, k0 = before(name), FIRST.get(name, 0)
                half = NPIECE // 2
                hi, lo = (m[:].rearrange("q a k n -> q (a k n)") for m in PANELS[name])

                def load(k, p):
                    source = first if k < half else second
                    at = k % half * PIECE
                    pool.dma_start(stage[:, p, :], source[:, at:at + PIECE]).then_inc(stg_in[p], 16)

                if n0 + k0:
                    pool.wait_ge(pan_lo, n0 + k0)
                for k in range(k0, k0 + 2):
                    load(k, k % 2)
                for k in range(k0, NPIECE):
                    p = k % 2
                    at = slice(k * PIECE, (k + 1) * PIECE)
                    pool.wait_ge(pan_hi, n0 + k + 1)
                    pool.tensor_tensor(lo[:, at], stage[:, p, :], hi[:, at].bitcast(F32),
                                       ALU.subtract).then_inc(pan_lo, 1)
                    if k + 2 < NPIECE:
                        pool.wait_ge(pan_lo, n0 + k + 1)
                        load(k + 2, p)

            def split_rest(name):
                n0 = before(name)
                hi, lo = (m[:].rearrange("q a k n -> q (a k n)") for m in PANELS[name])
                for k in range(NPIECE):
                    at = slice(k * PIECE, (k + 1) * PIECE)
                    pool.wait_ge(pan_hi, n0 + k + 1)
                    pool.tensor_tensor(lo[:, at], staged(name, k), hi[:, at].bitcast(F32),
                                       ALU.subtract).then_inc(pan_lo, 1)

            qf = qfold_d.rearrange("h q k n -> h q (k n)")

            for n in range(2 * KC):
                pool.wait_ge(fold_out, n + 1)
                hi, lo = PANELS[f"kv{n // KC}"]
                pool.tensor_tensor(lo[:, 0, n % KC, :], fold[:, n % 2, :], hi[:, 0, n % KC, :].bitcast(F32),
                                   ALU.subtract).then_inc(fold_lo, 1)
            load_pair("kv0", None, wv_pan[0])
            pool.wait_ge(cnt_free, NT + 1)
            pool.wait_ge(chi_st, 16 * (1 + NT))
            pool.wait_ge(clo_st, 16 * (1 + NT))
            load_pair("kv1", None, wv_pan[1])
            pool.wait_ge(dg_max, 1)
            pool.partition_all_reduce(degi[:, 1:2], degi[:, 0:1], P, RMAX).then_inc(dg_max, 1)
            pool.wait_ge(out_ready, 2 * V["m0"])
            for k in range(4):
                pool.wait_ge(fold_st[k], 16 * 4)
            load_pair("q", qf[0], qf[1])
            pool.wait_ge(out_ready, 2 * V["m1"])
            load_pair("h", wh_pan[0], wh_pan[1])
            split_rest("x")
            split_rest("gu0")
            load_pair("gu1", wgu_pan[1, 0], wgu_pan[1, 1])
            pool.wait_ge(out_ready, 2 * V["gu1"])
            load_pair("d", wd_pan[0], wd_pan[1])

        @block.scalar
        def _(act):
            act.sem_inc(tp_out, 2)
            act.dma_start(srcI[:], src).then_inc(in_edges, 16)
            act.dma_start(dstI[:], dst).then_inc(in_edges, 16)
            act.dma_start(pbd_s[:], pbd).then_inc(in_fold, 16)
            act.dma_start(bkq[:, 0:KC], bk_col).then_inc(in_fold, 16)
            act.dma_start(bkq[:, KC:2 * KC], bq_col).then_inc(in_fold, 16)

            def load_weights(k):
                act.dma_start(w_s[k][:], (wk_nat, wq_nat)[k // 2][:, k % 2 * 4:k % 2 * 4 + 4, :])\
                   .then_inc(in_w[k], 16)

            act.wait_ge(in_x[0], 16)
            load_weights(0)

            def to_outT(w, bank_no, p, col, k):
                act.wait_ge(tp_ready, w + 1)
                act.wait_ge(tr_st[p], 16 * k + 16)
                act.activation(outT[:, p, col:col + W], bank(6 + bank_no), ACT.Copy).then_inc(tp_out, 1)

            def fold_evac(n):
                act.wait_ge(fold_mm, n + 1)
                source = bank(FOLD_BANK[n % 2])
                if n < 2 * KC:
                    if n >= 2:
                        act.wait_ge(fold_lo, n - 1)
                    act.activation(fold[:, n % 2, :], source, ACT.Copy)
                    act.activation(PANELS[f"kv{n // KC}"][0][:, 0, n % KC, :], source, ACT.Copy)\
                       .then_inc(fold_out, 1)
                    return
                k, m = n - 2 * KC, n - 2 * KC - 4
                if k < 4:
                    if k < 2:
                        act.wait_ge(fold_lo, n - 1)
                    else:
                        act.wait_ge(fb_st[k % 2], 16)
                    row = fold[0:1, k % 2, :]
                    act.activation(row, source[0:1, :], ACT.Copy).then_inc(fold_out, 1)
                    act.wait_ge(fold_out, n + 1)
                    act.dma_start(fbias_d[k // 2:k // 2 + 1, k % 2 * W:(k % 2 + 1) * W], row)\
                       .then_inc(fb_st[k % 2], 16)
                else:
                    if m == 0:
                        act.wait_ge(edge_step, EDGE_STEPS)
                    if m >= 4:
                        act.wait_ge(fold_st[m % 4], 16 * (m // 4))
                    act.activation(qfold[:, m % 4, :], source, ACT.Copy).then_inc(fold_out, 1)
                    act.wait_ge(fold_out, n + 1)
                    act.dma_start(qfold_d[m // KC, :, m % KC, :], qfold[:, m % 4, :]).then_inc(fold_st[m % 4], 16)

            def split(u, p, k):
                act.wait_ge(act_in[p], 16 * k + 16)
                act.wait_ge(act_used, u + 1)
                act.activation(actH[:, p, :], actF[:, p, :], ACT.Copy).then_inc(act_hi, 1)

            def split_next(name, t, p, i):
                split(t + U[name] + 1, 1 - p, i + U[name] // 2 + p)

            def piece(name, k, p):
                hi = PANELS[name][0][:].rearrange("q a k n -> q (a k n)")
                if name in SP_PAIRS:
                    act.wait_ge(stg_sp[k], 16 * (SP_PAIRS.index(name) + 1))
                    act.activation(hi[:, k * PIECE:(k + 1) * PIECE], staged(name, k), ACT.Copy).then_inc(pan_hi, 1)
                    return
                n = before(name, POOL_PAIRS)
                act.wait_ge(stg_in[p], 8 * k + 8 * (1 - p) + 8 * n + 8)
                act.activation(hi[:, bass.ds(k * PIECE, PIECE)], stage[:, p, :], ACT.Copy).then_inc(pan_hi, 1)

            def ln1_sqrt(t):
                act.wait_ge(ln_step, LN_STEPS * t if t else LN_STEPS // 2)
                act.activation(lnw[:, t % 2, 15:16], lnw[:, t % 2, 14:15], ACT.Sqrt).then_inc(ln_sqrt, 1)

            ln1_sqrt(0)
            for t in range(NT):
                if t + 1 < NT:
                    ln1_sqrt(t + 1)
                if t in (1, 2, 4):
                    load_weights({1: 1, 2: 2, 4: 3}[t])
                for n in range(FOLD_START[t], FOLD_START[t + 1]):
                    fold_evac(n)
                for h in range(2):
                    to_outT(2 * t + h, h, t % 2, h * W, t // 2)
            for k in range(4):
                act.wait_ge(fold_st[k], 16 * 4)
            split(0, 0, 0)
            split_next("kv0", 0, 0, 0)
            for k in range(FIRST["kv0"], NPIECE):
                piece("kv0", k, k % 2)

            def counts(t):
                act.wait_ge(cnt_ready, t + 1)
                act.wait_ge(chi_st, 16 * t + 16)
                act.activation(c0[:], ps[:, CNT * BANK:CNT * BANK + NP], ACT.Copy).then_inc(chi_out, 1)

            for hf in range(2):
                name, nxt = (f"kv{hf}", ("kv1", "q")[hf])

                def features(t, p):
                    act.wait_ge(kb_ready, t + hf * NT + 1)
                    act.activation(tokB[:, p, 0:W], tokA[:, p, 0:W], ACT.Relu,
                                   scale=vscale[:, bass.ds(t, 1)]).then_inc(k_ready, 1)

                if hf == 0:
                    for t, p, i in tiles(act):
                        features(t, p)
                        counts(t)
                        split(t + 2, p, i + 1)
                else:
                    features(0, 0)
                    piece(nxt, 0, 0)
                    split_next(name, 1, 1, 0)
                    features(1, 1)
                    piece(nxt, 1, 1)
                    for t, p, i in tiles(act, 1, NL - 1):
                        split_next(name, t, p, i)
                        features(t, p)
                        piece(nxt, t, p)
                    for t in (NT - 2, NT - 1):
                        split_next(name, t, t % 2, t // 2)
                        features(t, t % 2)
                for g in range(4):
                    v, p = V[f"m{hf}"] + g, g % 2
                    if 2 * hf + g // 2:
                        act.wait_ge(m_st[p], 16 * (2 * hf + g // 2))
                    for h in range(2):
                        act.wait_ge(out_ready, 2 * v + h + 1)
                        last = act.activation(tokA[:, p, h * W:(h + 1) * W], bank(2 * p + h), ACT.Copy)
                    last.then_inc(out_free, 1)
                if hf == 0:
                    for k in range(FIRST["kv1"], NPIECE):
                        piece("kv1", k, k % 2)
                    act.wait_ge(dg, 1)
                    act.activation(dtmp[:, 1, :], dtmp[:, 0, :], ACT.Sqrt).then_inc(dg_sqrt, 1)

            def q_tile(t, p, i):
                split_next("q", t, p, i)
                for h in range(2):
                    if h == 0:
                        act.wait_ge(qb_ready, t + 1)
                    else:
                        act.wait_ge(out_free, t + V["q"] + 3)
                    act.wait_ge(tp_ready, 2 * t + T["q"] - 3 + h)
                    act.activation(tokB[:, p, h * W:(h + 1) * W], tokA[:, p, h * W:(h + 1) * W], ACT.Relu,
                                   scale=1.0 / HD ** 0.5).then_inc(q_relu, 1)

            def q_transposed(t, p, i):
                for h in range(2):
                    to_outT(2 * t + T["q"] + h, h, p, h * W, i + NL)

            act.sem_inc(q_relu, 4)
            staggered(act, q_tile, q_transposed, lambda t, p: piece("h", t, p))

            hp_hi = hp[0][:].rearrange("q t n -> q (t n)")

            def h_hi(t, p):
                act.wait_ge(out_free, t + V["h"] + 3)
                act.activation(hp_hi[:, bass.ds(t * D, D)], tokA[:, p, :], ACT.Copy,
                               scale=dis[:, bass.ds(t, 1)]).then_inc(hhi_ready, 1)

            for t, p, i in tiles(act, 0, NL - 1):
                split_next("h", t, p, i)
                h_hi(t, p)
            split_next("h", NT - 2, 0, NL - 1)
            h_hi(NT - 2, 0)
            split_next("h", NT - 1, 1, NL - 1)
            act.wait_ge(out_ready, 2 * V["x"] - 1)
            for k in range(2):
                piece("x", k, k)
            split_next("x", 0, 0, 0)
            h_hi(NT - 1, 1)

            def x_tile(t, p, i):
                split_next("x", t, p, i)

            def x_transposed(t, p, i):
                act.wait_ge(z_ready, t + 1)
                for h in range(2):
                    to_outT(2 * t + T["x"] + h, h, 1, h * W, t + 2 * NL)

            def x_sqrt(t):
                act.wait_ge(x1s, X_STEPS * t + 1 + 3 + 5)
                act.activation(nrm[:, 1:2], nrm[:, 0:1], ACT.Sqrt).then_inc(x1_sqrt, 1)

            for k in range(2, NPIECE):
                piece("x", k, k % 2)
            x_sqrt(0)
            for t, p, i in tiles(act, 0, NL - 1):
                x_tile(t + 1, 1 - p, i + p)
                x_transposed(t, p, i)
                x_sqrt(t + 1)
            x_tile(NT - 1, 1, NL - 1)
            split_next("gu0", 0, 0, 0)
            act.wait_ge(out_ready, 2 * V["gu0"])
            piece("gu0", 0, 0)
            x_transposed(NT - 2, 0, NL - 1)
            x_sqrt(NT - 1)
            for k in range(1, NPIECE):
                if k == 3:
                    x_transposed(NT - 1, 1, NL - 1)
                if k == 5:
                    act.wait_ge(rt, 1)
                    act.activation(r_inh, r_c, ACT.Exp, scale=-1.0).then_inc(rt_act, 1)
                if k == 6:
                    act.wait_ge(rt, 6)
                    act.activation(r_w, r_dist, ACT.Exp, scale=-1.0 / 0.1).then_inc(rt_act, 1)
                    act.activation(r_fb, r_dist, ACT.Exp, scale=-1.0 / 0.3).then_inc(rt_act, 1)
                piece("gu0", k, k % 2)

            for p in range(2):
                act.wait_ge(x1_st[p], 16 * NL)
            for hf in range(2):
                name = f"gu{hf}"

                def gate(t, p, i, split_too=True):
                    if split_too:
                        split_next(name, t, p, i)
                    act.wait_ge(out_ready, 2 * t + 2 * V[name] + 1)
                    act.wait_ge(out_free, t + V[name] + 1)
                    act.activation(tokA[:, p, 0:W], bank(2 * p), ACT.Silu).then_inc(silu_ready, 1)

                def h_transposed(t, p, i):
                    to_outT(t + T[name], p, p, 0, i + (2 + hf) * NL + p * NT)

                gate(0, 0, 0, split_too=hf > 0)
                for t, p, i in tiles(act, 0, NL - 1):
                    gate(t + 1, 1 - p, i + p)
                    h_transposed(t, p, i)
                    piece(("gu1", "d")[hf], t, p)
                gate(NT - 1, 1, NL - 1)
                h_transposed(NT - 2, 0, NL - 1)
                h_transposed(NT - 1, 1, NL - 1)

            for t, p, i in tiles(act, 0, NL - 1):
                split_next("d", t, p, i)
            split_next("d", NT - 2, 0, NL - 1)

        @block.vector
        def _(dve):
            dve.sem_inc(out_free, 2)
            dve.sem_inc(cnt_free, 1)
            dve.sem_inc(c_free, 1)
            dve.sem_inc(z_read, 1)

            def split(u, p, k):
                dve.wait_ge(act_in[p], 16 * k + 16)
                dve.wait_ge(act_hi, u + 1)
                dve.tensor_tensor(actL[:, p, :], actF[:, p, :], actH[:, p, :].bitcast(F32), ALU.subtract)\
                   .then_inc(act_lo, 1)

            def split_next(name, t, p, i):
                split(t + U[name] + 1, 1 - p, i + U[name] // 2 + p)

            def refine(value, y, t, out_y, step, s):
                dve.tensor_tensor(t, y, y, ALU.mult).then_inc(step, 1)
                dve.wait_ge(step, s + 1)
                dve.tensor_tensor(t, t, value, ALU.mult).then_inc(step, 1)
                dve.wait_ge(step, s + 2)
                dve.tensor_scalar(t, t, -0.5, 1.5, ALU.mult, ALU.add).then_inc(step, 1)
                dve.wait_ge(step, s + 3)
                dve.tensor_tensor(out_y, y, t, ALU.mult).then_inc(step, 1)
                dve.wait_ge(step, s + 4)

            def layernorm(xin, target, step, s, root, n, done, before_second=None):
                dve.bn_stats(st6[:, 0:6], xin[:, 0:W]).then_inc(step, 1)
                if before_second:
                    before_second()
                dve.bn_stats(st6[:, 6:12], xin[:, W:D]).then_inc(step, 1)
                dve.wait_ge(step, s + 2)
                dve.sem_inc(step, 1)
                dve.bn_aggr(mv[:], st6[:]).then_inc(step, 1)
                dve.wait_ge(step, s + 4)
                dve.tensor_scalar(nrm[:, 0:1], mv[:, 1:2], EPS, None, ALU.add).then_inc(step, 1)
                dve.wait_ge(root, n)
                dve.reciprocal(nrm[:, 2:3], nrm[:, 1:2]).then_inc(step, 1)
                dve.wait_ge(step, s + 6)
                refine(nrm[:, 0:1], nrm[:, 2:3], nrm[:, 3:4], nrm[:, 4:5], step, s + 6)
                dve.tensor_scalar(target, xin, mv[:, 0:1], nrm[:, 4:5], ALU.subtract, ALU.mult).then_inc(done, 1)

            es = [0]

            def edge(ins):
                ins.then_inc(edge_step, 1)
                es[0] += 1
                dve.wait_ge(edge_step, es[0])

            def ln1_stats(t):
                xt, st, s = xin[:, t % 4, :], lnw[:, t % 2, :], LN_STEPS * t - 5 if t else 0
                dve.wait_ge(in_x[t % 4], 16 * (t // 4 + 1))
                dve.bn_stats(st[:, 0:6], xt[:, 0:W]).then_inc(ln_step, 1)
                dve.bn_stats(st[:, 6:12], xt[:, W:D]).then_inc(ln_step, 1)
                dve.wait_ge(ln_step, s + 2)
                dve.bn_aggr(st[:, 12:14], st[:, 0:12]).then_inc(ln_step, 2)
                dve.wait_ge(ln_step, s + 4)
                dve.tensor_scalar(st[:, 14:15], st[:, 13:14], EPS, None, ALU.add).then_inc(ln_step, 1)

            def ln1_normalise(t):
                xt, st, s = xin[:, t % 4, :], lnw[:, t % 2, :], LN_STEPS * (t + 1) - (5 if t == NT - 1 else 0)
                dve.wait_ge(ln_sqrt, t + 1)
                dve.reciprocal(st[:, 16:17], st[:, 15:16]).then_inc(ln_step, 1)
                dve.wait_ge(ln_step, s + 1)
                refine(st[:, 14:15], st[:, 16:17], st[:, 17:18], st[:, 18:19], ln_step, s + 1)
                if t >= 2:
                    dve.wait_ge(tp_out, 2 * t)
                dve.tensor_scalar(tokB[:, t % 2, :], xt, st[:, 12:13], st[:, 18:19], ALU.subtract, ALU.mult)\
                   .then_inc(xn_ready, 1)

            def ln1(t):
                if t + 1 < NT:
                    ln1_stats(t + 1)
                ln1_normalise(t)

            ln1_stats(0)
            for t in range(4):
                ln1(t)
            dve.wait_ge(in_edges, 32)
            edge(dve.tensor_copy(srcF[:], srcI[:]))
            edge(dve.tensor_copy(dstF[:], dstI[:]))
            for t in range(NT + 1):
                edge(dve.tensor_scalar(ge[:, t, :], dstF[:], float(P * t), None, ALU.is_ge))
            dve.tensor_tensor(inT[:], ge[:, 0:NT, :], ge[:, 1:NT + 1, :], ALU.subtract).then_inc(edge_step, 1)
            es[0] += 1
            dve.wait_ge(consts, 12)
            edge(dve.tensor_scalar(vscale[:], rowid[:], float(N), 1.0 / HD ** 0.5, ALU.is_lt, ALU.mult))
            ln1(4)
            ln1(5)
            dve.wait_ge(pres_mm, 4)
            for k, b in enumerate(PRES_BANK):
                n = min(3, NT - 3 * k)
                cols = bank(b)[0:1, 0:n * NCH].rearrange("a (t c k) -> a t c k", t=n, k=GROUP)
                edge(dve.tensor_reduce(pres[:, 3 * k:3 * k + n, :], cols, AX_X, ALU.max))
            edge(dve.tensor_scalar(pres[:], pres[:], 1.0, None, ALU.min))
            for col, weight in ((1, up), (0, down)):
                edge(dve.tensor_tensor(prod[:], pres[:], weight[:], ALU.mult))
                edge(dve.tensor_reduce(rngF[:, :, col], prod[:], AX_X, ALU.max))
            edge(dve.tensor_scalar(rngF[:, :, 0], rngF[:, :, 0], -1.0, float(NGRP), ALU.mult, ALU.add))
            edge(dve.tensor_scalar(rngF[:, :, 0], rngF[:, :, 0], float(NGRP - 1), None, ALU.min))
            edge(dve.scalar_tensor_tensor(out=rngF[:, :, 1], in0=rngF[:, :, 0], scalar=1.0, in1=rngF[:, :, 1],
                                          op0=ALU.add, op1=ALU.max))
            edge(dve.tensor_copy(rng[:], rngF[:]))
            assert es[0] == EDGE_STEPS

            for t in range(6, NT):
                ln1(t)
            dve.wait_ge(xn_ready, NT)
            split(0, 0, 0)
            split(1, 1, 0)

            seen = dve.alloc_register("groups_seen")
            dve.reg_mov(seen, 0)

            def one_hots(t):
                first, last = group_range(dve, t)
                with dve.Fori(first, last) as j:
                    n = dve.snap(seen)
                    for k in range(GROUP):
                        dve.wait_ge(hot_used, GROUP * n + k + 1)
                        dve.tensor_scalar(srcHot[:, k, :], iota[:],
                                          srcF[:, bass.ds(GROUP * j + k, 1)], None, ALU.is_equal)
                        dve.tensor_scalar(dstHot[:, k, :], iota[:, bass.ds(P * t, P)],
                                          dstF[:, bass.ds(GROUP * j + k, 1)], None, ALU.is_equal)\
                           .then_inc(hot_ready, 1)
                    dve.reg_add(seen, seen, 1)

            def counts_rest(t):
                counts = ps[:, CNT * BANK:CNT * BANK + NP]
                dve.wait_ge(chi_out, t + 1)
                dve.wait_ge(clo_st, 16 * t + 16)
                dve.tensor_tensor(c1[:], counts, c0[:].bitcast(F32), ALU.subtract).then_inc(clo_out, 1)
                dve.wait_ge(cnt_free, t + 1)
                dve.tensor_tensor(acc[:], counts, acc[:], ALU.add).then_inc(cnt_free, 1)

            dve.memset(kvT[:], 0.0).then_inc(kvT_step, 1)
            one_hots(0)
            for hf in range(2):
                name = f"kv{hf}"
                dve.wait_ge(bias_in, 32 * (hf + 1))
                if hf:
                    for p in range(2):
                        dve.wait_ge(m_st[p], 32)

                def kv_tile(t, p, i, split_too=True):
                    if split_too:
                        split_next(name, t, p, i)
                    dve.wait_ge(kv_used, t + hf * NT + 1)
                    dve.wait_ge(out_ready, 2 * t + 2 * V[name] + 1)
                    dve.tensor_tensor(tokA[:, p, 0:W], bank(2 * p), bias[:, 0:W], ALU.add).then_inc(kb_ready, 1)
                    dve.wait_ge(out_ready, 2 * t + 2 * V[name] + 2)
                    dve.tensor_tensor(tokA[:, p, W:D], bank(2 * p + 1), bias[:, W:D], ALU.add)\
                       .then_inc(out_free, 1)

                if hf == 0:
                    def counting_tile(t, p, i):
                        kv_tile(t, p, i, split_too=False)
                        counts_rest(t)
                        split(t + 2, p, i + 1)

                    for t, p, i in tiles(dve, 0, NL - 1):
                        counting_tile(t, p, i)
                        one_hots(t + 1)
                    counting_tile(NT - 2, 0, NL - 1)
                    one_hots(NT - 1)
                    kv_tile(NT - 1, 1, NL - 1, split_too=False)
                else:
                    kv_tile(0, 0, 0, split_too=False)
                    kv_tile(1, 1, 0)
                    for t, p, i in tiles(dve, 1, NL):
                        kv_tile(t, p, i)
                dve.wait_ge(kv_used, (hf + 1) * NT + 2)
                for k in range(2):
                    own = slice(k * HD, (k + 1) * HD)
                    dve.tensor_copy(kvT[own, :, own], bank(4).rearrange("q (g m) -> q g m", g=4)[own, :, own])\
                       .then_inc(kvT_step, 1)
                if hf == 0:
                    counts_rest(NT - 1)
                    split(NT + 1, 1, NL)
                    dve.wait_ge(deg_done, 1)
                    dve.tensor_copy(dtmp[:, 0, :], bank(CNT, NT)).then_inc(dg, 1)
                    dve.tensor_reduce(degi[:, 0:1], bank(CNT, NT), AX_X, ALU.max).then_inc(dg_max, 1)
                    dve.wait_ge(dg_sqrt, 1)
                    dve.reciprocal(dtmp[:, 2, :], dtmp[:, 1, :]).then_inc(dg, 1)
                    dve.wait_ge(dg, 2)
                    refine(dtmp[:, 0, :], dtmp[:, 2, :], dtmp[:, 3, :], dis[:], dg, 2)
                    dve.wait_ge(dg_max, 2)
                    dve.tensor_scalar(flag[:], degi[:, 1:2], float(EXACT_COUNT), None, ALU.is_gt)\
                       .then_inc(dg_max, 1)

            dve.wait_ge(bias_in, 80)
            for p in range(2):
                dve.wait_ge(m_st[p], 64)
            for t, p, i in tiles(dve):
                split_next("q", t, p, i)
                for h in range(2):
                    dve.wait_ge(q_relu, 2 * t + h + 1)
                    dve.wait_ge(out_ready, 2 * t + 2 * V["q"] + h + 1)
                    dve.tensor_tensor(tokA[:, p, h * W:(h + 1) * W], bank(2 * p + h),
                                      bias[:, h * W:(h + 1) * W], ALU.add)\
                       .then_inc(qb_ready if h == 0 else out_free, 1)

            dve.wait_ge(bias_in, 96)
            dve.wait_ge(q_relu, 2 * NT + 4)
            hp_hi, hp_lo = (m[:].rearrange("q t n -> q (t n)") for m in hp)

            def h_bias(t, p, i):
                split_next("h", t, p, i)
                for h in range(2):
                    dve.wait_ge(out_ready, 2 * t + 2 * V["h"] + h + 1)
                    last = dve.tensor_tensor(tokA[:, p, h * W:(h + 1) * W], bank(2 * p + h),
                                             bias[:, h * W:(h + 1) * W], ALU.add)
                last.then_inc(out_free, 1)

            def h_lo(t, p):
                dve.wait_ge(hhi_ready, t + 1)
                dve.scalar_tensor_tensor(out=hp_lo[:, bass.ds(t * D, D)], in0=tokA[:, p, :],
                                         scalar=dis[:, bass.ds(t, 1)],
                                         in1=hp_hi[:, bass.ds(t * D, D)].bitcast(F32),
                                         op0=ALU.mult, op1=ALU.subtract).then_inc(hlo_ready, 1)

            for t, p, i in tiles(dve, 0, NL - 1):
                h_bias(t, p, i)
                h_lo(t, p)
            h_bias(NT - 2, 0, NL - 1)
            h_lo(NT - 2, 0)
            h_bias(NT - 1, 1, NL - 1)
            split_next("x", 0, 0, 0)
            h_lo(NT - 1, 1)

            dve.wait_ge(bias_in, 112)

            def x_tile(t, p, i, between=None, split_too=True):
                xt, s, v = tokA[:, p, :], X_STEPS * t + 1, t + V["x"]
                if split_too:
                    split_next("x", t, p, i)
                dve.wait_ge(xt_in[p], 16 * i + 16)
                dve.tensor_tensor(xt, xt, bias[:], ALU.add).then_inc(x1s, 1)
                dve.wait_ge(x1s, s + 1)
                dve.wait_ge(out_ready, 2 * v + 1)
                dve.tensor_tensor(xt[:, 0:W], bank(2 * p), xt[:, 0:W], ALU.add).then_inc(x1s, 1)
                dve.wait_ge(out_ready, 2 * v + 2)
                dve.tensor_tensor(xt[:, W:D], bank(2 * p + 1), xt[:, W:D], ALU.add).then_inc(out_free, 1)
                if between:
                    between()
                dve.wait_ge(x1s, s + 2)
                dve.wait_ge(c_ready, 2 * t + 1)
                dve.scalar_tensor_tensor(out=xt[:, 0:W], in0=bank(4), scalar=dis[:, bass.ds(t, 1)],
                                         in1=xt[:, 0:W], op0=ALU.mult, op1=ALU.add).then_inc(x1s, 1)
                dve.wait_ge(out_free, v + 3)
                dve.wait_ge(c_ready, 2 * t + 2)
                dve.scalar_tensor_tensor(out=xt[:, W:D], in0=bank(5), scalar=dis[:, bass.ds(t, 1)],
                                         in1=xt[:, W:D], op0=ALU.mult, op1=ALU.add).then_inc(c_free, 1)
                dve.wait_ge(x1s, s + 3)

                def second_half():
                    dve.wait_ge(c_free, t + 2)
                    dve.wait_ge(tp_ready, 2 * t + T["x"])

                layernorm(xt, tokB[:, 0, :], x1s, s + 3, x1_sqrt, t + 1, x2_ready, second_half)

            def logits(t):
                dve.wait_ge(z_ready, t + 2)
                dve.tensor_scalar(zlog[:, bass.ds(NEXP * t, NEXP)], bank(7, NEXP), tmp_t[:, 1:2], None,
                                  ALU.mult).then_inc(z_read, 1)

            dve.wait_ge(in_small, 32)
            dve.reciprocal(tmp_t[:, 1:2], tmp_t[:, 0:1]).then_inc(x1s, 1)
            dve.wait_ge(x1s, 1)
            x_tile(0, 0, 0, split_too=False)
            x_tile(1, 1, 0)
            for t, p, i in tiles(dve, 1, NL - 1):
                x_tile(t, p, i, lambda: logits(t - 2))
            x_tile(NT - 2, 0, NL - 1, lambda: logits(NT - 4))

            def before_last():
                logits(NT - 3)
                split_next("gu0", 0, 0, 0)

            x_tile(NT - 1, 1, NL - 1, before_last)
            logits(NT - 2)
            logits(NT - 1)

            rs = [0]

            def route(ins):
                ins.then_inc(rt, 1)
                rs[0] += 1
                dve.wait_ge(rt, rs[0])

            def by_tile(m):
                return m.rearrange("q (t e) -> q t e", e=NEXP)

            def spread(m):
                return m.unsqueeze(2).to_broadcast([P, NT, NEXP])

            dve.wait_ge(c_ready, 2 * NT)
            dve.wait_ge(z_read, NT + 1)
            route(dve.tensor_scalar(r_c, zlog[:], LOGIT_MIN, None, ALU.max))
            dve.wait_ge(rt_act, 1)
            route(dve.tensor_scalar(r_inh, r_inh, 1.0, None, ALU.add))
            route(dve.reciprocal(r_inh, r_inh))
            route(dve.tensor_scalar(r_dist, r_inh, CENTER, None, ALU.subtract))
            route(dve.tensor_scalar(r_c, r_inh, -1.0, CENTER, ALU.mult, ALU.add))
            route(dve.tensor_tensor(r_dist, r_dist, r_c, ALU.max))
            route(dve.tensor_scalar(r_zone, zlog[:], ZONE_HIGH, None, ALU.is_le))
            route(dve.scalar_tensor_tensor(out=r_zone, in0=zlog[:], scalar=ZONE_LOW, in1=r_zone, op0=ALU.is_ge,
                                           op1=ALU.mult))
            dve.wait_ge(rt_act, 2)
            route(dve.tensor_tensor(r_w, r_w, r_zone, ALU.mult))
            route(dve.tensor_reduce(r_s, by_tile(r_w), AX_X, ALU.add))
            route(dve.tensor_scalar(r_none, r_s, 1e-8, None, ALU.is_lt))
            dve.wait_ge(rt_act, 3)
            route(dve.tensor_copy(r_c, r_fb))
            for e in range(NEXP):
                route(dve.memset(by_tile(r_rank)[:, :, e], float(NEXP - e)))
            for k in range(2):
                route(dve.tensor_reduce(r_s, by_tile(r_c), AX_X, ALU.max))
                route(dve.tensor_tensor(by_tile(r_eq), by_tile(r_c), spread(r_s), ALU.is_equal))
                route(dve.tensor_tensor(r_eq, r_eq, r_rank, ALU.mult))
                route(dve.tensor_reduce(r_s, by_tile(r_eq), AX_X, ALU.max))
                route(dve.tensor_tensor(by_tile(r_eq), by_tile(r_eq), spread(r_s), ALU.is_equal))
                if k == 0:
                    route(dve.tensor_copy(r_mask, r_eq))
                    route(dve.scalar_tensor_tensor(out=r_c, in0=r_eq, scalar=-2.0, in1=r_c, op0=ALU.mult,
                                                   op1=ALU.add))
            route(dve.tensor_tensor(r_mask, r_mask, r_eq, ALU.add))
            route(dve.tensor_tensor(r_fb, r_fb, r_mask, ALU.mult))

            def normalise(m):
                route(dve.tensor_reduce(r_s, by_tile(m), AX_X, ALU.add))
                route(dve.tensor_scalar(r_s, r_s, 1e-8, None, ALU.max))
                route(dve.reciprocal(r_s, r_s))
                route(dve.tensor_tensor(by_tile(m), by_tile(m), spread(r_s), ALU.mult))

            normalise(r_fb)
            route(dve.tensor_tensor(by_tile(r_fb), by_tile(r_fb), spread(r_none), ALU.mult))
            route(dve.tensor_scalar(r_none, r_none, -1.0, 1.0, ALU.mult, ALU.add))
            route(dve.tensor_tensor(by_tile(r_w), by_tile(r_w), spread(r_none), ALU.mult))
            route(dve.tensor_tensor(r_w, r_w, r_fb, ALU.add))
            normalise(r_w)
            route(dve.tensor_copy(wexp[:], r_w))

            for hf in range(2):
                name = f"gu{hf}"
                def hidden(t, p, i, split_too=True):
                    if split_too:
                        split_next(name, t, p, i)
                    dve.wait_ge(silu_ready, t + hf * NT + 1)
                    dve.wait_ge(out_ready, 2 * t + 2 * V[name] + 2)
                    dve.wait_ge(tp_ready, t + T[name] - 1)
                    for e in range(XH):
                        cols = slice(e * P, (e + 1) * P)
                        last = dve.scalar_tensor_tensor(
                            out=tokB[:, p, cols], in0=tokA[:, p, cols],
                            scalar=wexp[:, bass.ds(NEXP * t + hf * XH + e, 1)], in1=bank(2 * p + 1)[:, cols],
                            op0=ALU.mult, op1=ALU.mult)
                    last.then_inc(out_free, 1)

                if hf == 0:
                    hidden(0, 0, 0, split_too=False)
                    hidden(1, 1, 0)
                for t, p, i in tiles(dve, 1 - hf, NL):
                    hidden(t, p, i)

            def d_tile(t, p, i):
                dve.wait_ge(x1b_in[p], 16 * i + 16)
                for h in range(2):
                    dve.wait_ge(out_ready, 2 * t + 2 * V["d"] + h + 1)
                    cols = slice(h * W, (h + 1) * W)
                    last = dve.tensor_tensor(tokA[:, p, cols], bank(2 * p + h), tokA[:, p, cols], ALU.add)
                last.then_inc(out_free, 1)

            for t, p, i in tiles(dve, 0, NL - 1):
                split_next("d", t, p, i)
                d_tile(t, p, i)
            split_next("d", NT - 2, 0, NL - 1)
            d_tile(NT - 2, 0, NL - 1)
            d_tile(NT - 1, 1, NL - 1)

        @block.tensor
        def _(pe):
            pe.sem_inc(hot_used, GROUP)
            pe.sem_inc(act_used, 2)
            pe.sem_inc(kv_used, 2)
            pe.sem_inc(z_ready, 1)
            pe.wait_ge(consts, 12)

            def presence():
                pe.wait_ge(edge_step, 2 + NT + 1 + 1)
                for k, b in enumerate(PRES_BANK):
                    n = min(3, NT - 3 * k)
                    pe.matmul(bank(b)[0:1, 0:n * NCH], ones16[:, 0:1],
                              inT[:, 3 * k:3 * k + n, :].rearrange("q t c -> q (t c)"), start=True, stop=True)\
                      .then_inc(pres_mm, 1)

            def transposes(source, b):
                for k in range(4):
                    last = pe.transpose(bank(6 + b)[:, k * P:(k + 1) * P], source[:, k * P:(k + 1) * P], ident[:])
                last.then_inc(tp_ready, 1)

            def fold(n):
                target = bank(FOLD_BANK[n % 2])
                if n >= 2:
                    pe.wait_ge(fold_out, n - 1)
                biases = 2 * KC <= n < 2 * KC + 4
                m = n if n < 2 * KC else n - 4
                if not biases and m % KC == 0:
                    pe.wait_ge(in_w[m // KC], 16)
                for g in range(4):
                    if biases:
                        c = 4 * (n - 2 * KC) + g
                        left, right = bkq[:, c:c + 1], pbd_s[:, c % KC, :]
                    else:
                        left = w_s[m // KC][:, g, m % KC * P:(m % KC + 1) * P]
                        right = pbd_s[:, m // KC % 2 * 4 + g, :]
                    mm = pe.matmul(target[0:1 if biases else P, g * P:(g + 1) * P], left, right, start=True,
                                   stop=True)
                mm.then_inc(fold_mm, 1)

            for t in range(NT):
                if t == 2:
                    pe.wait_ge(in_fold, 16 * 3)
                if t == 5:
                    presence()
                for n in range(FOLD_START[t], FOLD_START[t + 1]):
                    fold(n)
                pe.wait_ge(xn_ready, t + 1)
                for h in range(2):
                    pe.wait_ge(tp_out, 2 * t + h + 1)
                    transposes(tokB[:, t % 2, h * W:(h + 1) * W], h)

            seen = pe.alloc_register("groups_counted")
            pe.reg_mov(seen, 0)

            def count(t):
                counts = ps[:, CNT * BANK:CNT * BANK + NP]
                blocks = [(slice(c, min(c + BANK, NP)), counts[:, c:min(c + BANK, NP)])
                          for c in range(0, NP, BANK)]
                pe.wait_ge(cnt_free, t + 1)
                for cols, target in blocks:
                    pe.matmul(target, zero16[:], iota[:, cols], start=True, stop=False)
                pe.matmul(counts[:, bass.ds(P * t, P)], id16[:], id16[:], start=False, stop=False)
                first, last = group_range(pe, t)
                with pe.Fori(first, last):
                    n = pe.snap(seen)
                    for k in range(GROUP):
                        pe.wait_ge(hot_ready, GROUP * n + k + 1)
                        for cols, target in blocks:
                            mm = pe.matmul(target, dstHot[:, k, :],
                                           srcHot[:, k, cols],
                                           start=False, stop=False)
                        mm.then_inc(hot_used, 1)
                    pe.reg_add(seen, seen, 1)
                for cols, target in blocks:
                    mm = pe.matmul(target[:, 0:16], zero16[:], iota[:, 0:16], start=False, stop=True)
                mm.then_inc(cnt_ready, 1)

            def gemm(name, t, p):
                u, v = t + U[name], t + V[name]
                hi, lo = PANELS[name]
                pe.wait_ge(act_hi, u + 1)
                pe.wait_ge(act_lo, u + 1)
                pe.wait_ge(out_free, v + 1)
                for h in range(2):
                    target = bank(2 * p + h)
                    for kc in range(KC):
                        ah = actH[:, p, kc * P:(kc + 1) * P]
                        al = actL[:, p, kc * P:(kc + 1) * P]
                        pe.matmul(target, ah, hi[:, h, kc, :], start=(kc == 0), stop=False)
                        mm = pe.matmul(target, ah, lo[:, h, kc, :], start=False, stop=False)
                        if h == 1 and kc == KC - 1:
                            mm.then_inc(act_used, 1)
                        mm = pe.matmul(target, al, hi[:, h, kc, :], start=False, stop=(kc == KC - 1))
                    mm.then_inc(out_ready, 1)

            def panels(name):
                pe.wait_ge(pan_lo, before(name) + NPIECE)
                pe.wait_ge(pan_hi, before(name) + NPIECE)

            def gemm_first(name, h, first=0, last=KC):
                u, v = U[name], V[name]
                hi, lo = PANELS[name]
                for kc in range(first, last):
                    piece = before(name) + (h * KC + kc) // 2
                    if kc % 2 == 0 and (h or name not in FIRST):
                        pe.wait_ge(pan_lo, piece + 1)
                        pe.wait_ge(pan_hi, piece + 1)
                    for p in range(2):
                        if kc == 0 and h == 0:
                            pe.wait_ge(act_hi, u + p + 1)
                            pe.wait_ge(act_lo, u + p + 1)
                            pe.wait_ge(out_free, v + p + 1)
                        target = bank(2 * p + h)
                        ah = actH[:, p, kc * P:(kc + 1) * P]
                        al = actL[:, p, kc * P:(kc + 1) * P]
                        pe.matmul(target, ah, hi[:, h, kc, :], start=(kc == 0), stop=False)
                        mm = pe.matmul(target, ah, lo[:, h, kc, :], start=False, stop=False)
                        if h == 1 and kc == KC - 1:
                            mm.then_inc(act_used, 1)
                        mm = pe.matmul(target, al, hi[:, h, kc, :], start=False, stop=(kc == KC - 1))
                        if kc == KC - 1 and (h, p) != (0, 1):
                            mm.then_inc(out_ready, 1 + (h == 1 and p == 1))

            for hf in range(2):
                name = f"kv{hf}"

                def kv(t, p, first=False, last=False):
                    pe.wait_ge(k_ready, t + hf * NT + 1)
                    pe.wait_ge(out_free, t + V[name] + 3)
                    for g in range(4):
                        mm = pe.matmul(bank(4)[:, g * P:(g + 1) * P], tokA[:, p, W + g * P:W + (g + 1) * P],
                                       tokB[:, p, g * P:(g + 1) * P], start=first and g == 0,
                                       stop=last and g == 3)
                    mm.then_inc(kv_used, 1)

                def counted(t):
                    if hf == 0:
                        count(t)

                if hf == 0:
                    pe.wait_ge(fold_out, KC)
                    pe.wait_ge(fold_lo, KC)
                    gemm_first(name, 0)
                    gemm_first(name, 1)
                    pe.wait_ge(edge_step, EDGE_STEPS)
                else:
                    gemm_first(name, 0)
                    gemm_first(name, 1)
                counted(0)
                kv(0, 0, first=True)
                with pe.Fori(0, NL - 1) as i:
                    for p in (1, 0):
                        t = 2 * i + 2 - p
                        counted(t)
                        gemm(name, t + 1, 1 - p)
                        kv(t, p)
                counted(NT - 1)
                kv(NT - 1, 1, last=True)
                pe.wait_ge(kvT_step, 1 + 2 * (hf + 1))
                for g in range(4):
                    v, p = V[f"m{hf}"] + g, g % 2
                    pe.wait_ge(wo_in[p], 16 * (2 * hf + g // 2 + 1))
                    pe.wait_ge(out_free, v + 1)
                    for h in range(2):
                        pe.matmul(bank(2 * p + h), kvT[:, g, :], woP[:, p, h * W:(h + 1) * W], start=True,
                                  stop=True).then_inc(out_ready, 1)
                if hf == 0:
                    pe.wait_ge(cnt_free, NT + 1)
                    for c in range(NT):
                        mm = pe.matmul(bank(CNT)[:, c:c + 1], acc[:, c * P:(c + 1) * P], ones[:], start=True,
                                       stop=True)
                    mm.then_inc(deg_done, 1)

            def q_transposes(t, p, i):
                for h in range(2):
                    pe.wait_ge(q_relu, 4 + 2 * t + h + 1)
                    pe.wait_ge(tp_out, 2 * t + T["q"] + h + 1)
                    transposes(tokB[:, p, h * W:(h + 1) * W], h)

            panels("q")
            staggered(pe, lambda t, p, i: gemm("q", t, p), q_transposes)

            panels("h")
            for t, p, i in tiles(pe):
                gemm("h", t, p)

            for h in range(2):
                gemm_first("x", h)
            pe.wait_ge(hlo_ready, NT)
            pe.wait_ge(dg_max, 3)
            pe.wait_ge(in_small, 32)
            big = pe.value_load(flag[0:1, 0:1], min_val=0, max_val=1)

            def aggregate(t, p, i):
                pe.wait_ge(chi_in[p], 16 * i + 16)
                pe.wait_ge(c_free, t + 1)
                for h in range(2):
                    cols = slice(h * W, (h + 1) * W)
                    for c in range(NT):
                        pe.matmul(bank(4 + h), cHi[:, p, c, :], hp[0][:, c, cols], start=(c == 0), stop=False)
                    pe.wait_ge(clo_in, 16 * t + 16)
                    with pe.If(big != 0):
                        for c in range(NT):
                            pe.matmul(bank(4 + h), cLo[:, c, :], hp[0][:, c, cols], start=False, stop=False)
                    for c in range(NT):
                        mm = pe.matmul(bank(4 + h), cHi[:, p, c, :], hp[1][:, c, cols], start=False,
                                       stop=(c == NT - 1))
                    mm.then_inc(c_ready, 1)

            def x_transposes(t):
                pe.wait_ge(x2_ready, t + 1)
                pe.wait_ge(z_read, t + 1)
                for h in range(2):
                    pe.wait_ge(tp_out, 2 * t + T["x"] + h + 1)
                    transposes(tokB[:, 0, h * W:(h + 1) * W], h)

            def router(t):
                pe.wait_ge(tp_out, 2 * t + T["x"] + 4)
                for kc in range(KC):
                    mm = pe.matmul(bank(7, NEXP), outT[:, 1, kc * P:(kc + 1) * P],
                                   wr[:, kc * NEXP:(kc + 1) * NEXP], start=(kc == 0), stop=(kc == KC - 1))
                mm.then_inc(z_ready, 1)

            aggregate(0, 0, 0)
            aggregate(1, 1, 0)
            x_transposes(0)
            for t, p, i in tiles(pe, 1, NL):
                gemm("x", t, p)
                router(t - 2)
                aggregate(t, p, i)
                x_transposes(t - 1)
            router(NT - 2)
            gemm_first("gu0", 0, 0, 4)
            x_transposes(NT - 1)
            gemm_first("gu0", 0, 4, 6)
            router(NT - 1)
            gemm_first("gu0", 0, 6, KC)
            gemm_first("gu0", 1)

            for hf in range(2):
                name = f"gu{hf}"

                def h_transposes(t, p, i):
                    pe.wait_ge(out_free, t + V[name] + 3)
                    pe.wait_ge(tp_out, t + T[name] + 1)
                    transposes(tokB[:, p, 0:W], p)

                if hf == 0:
                    h_transposes(0, 0, 0)
                    with pe.Fori(0, NL - 1) as i:
                        for p in range(2):
                            gemm(name, 2 * i + p + 2, p)
                            h_transposes(2 * i + p + 1, 1 - p, i + p)
                    h_transposes(NT - 1, 1, NL - 1)
                else:
                    panels(name)
                    staggered(pe, lambda t, p, i: gemm(name, t, p), h_transposes)

            panels("d")
            for t, p, i in tiles(pe):
                gemm("d", t, p)


def _panels(w, np):
    return w.reshape(KC, P, 2, W).transpose(2, 1, 0, 3).reshape(2, P, KC * W)


def _layouts(np, x, src, dst, L0_gnn_W, L0_gnn_b, L0_mix_Wq, L0_mix_bq, L0_mix_Wk, L0_mix_bk, L0_mix_Wv, L0_mix_bv,
             L0_mix_Wo, L0_mix_bo, L0_mix_P, L0_ffn_Wg, L0_ffn_Wu, L0_ffn_Wd, L0_ffn_Wr, L0_ffn_temperature):
    def rows(w):
        return w.reshape(KC, P, -1).transpose(1, 0, 2)

    def edges(e):
        full = np.full(NCH * P, -1, dtype=e.dtype)
        full[:E_EDGES] = e
        return full.reshape(NCH, P).T

    xp = np.zeros((NP, D), dtype=x.dtype)
    xp[:N] = x
    pbd = np.zeros((P, KC, P), dtype=L0_mix_P.dtype)
    for h in range(2 * KC):
        k = h % 2 * HD
        pbd[k:k + HD, h // 2, k:k + HD] = L0_mix_P[h].T
    gate_up = np.stack([_panels(w.transpose(1, 0, 2).reshape(D, D), np) for w in (L0_ffn_Wg, L0_ffn_Wu)], axis=1)
    return [xp.reshape(NT, P, D), edges(src), edges(dst), rows(L0_mix_Wk), rows(L0_mix_Wq), pbd,
            L0_mix_bk.reshape(KC, P).T, L0_mix_bq.reshape(KC, P).T, _panels(L0_mix_Wv.T, np),
            L0_mix_bv.reshape(1, D), _panels(L0_gnn_W.T, np), L0_gnn_b.reshape(1, D),
            L0_mix_Wo.T.reshape(KC, P, D), L0_mix_bo.reshape(1, D), gate_up,
            _panels(L0_ffn_Wd.reshape(D, D), np), rows(L0_ffn_Wr).reshape(P, KC * NEXP),
            L0_ffn_temperature.reshape(1, 1)]


def kernel(**inputs):
    import numpy as np
    import concourse.bacc as bacc
    from concourse.bass_utils import run_bass_kernel_spmd

    nc = bacc.Bacc("TRN2", target_bir_lowering=False, num_devices=1)
    arrays, args = {}, []
    for k, a in enumerate(_layouts(np, **{name: np.asarray(a) for name, a in inputs.items()})):
        a = np.ascontiguousarray(a)
        arrays[f"in_{k}"] = a
        args.append(nc.dram_tensor(f"in_{k}", a.shape, mybir.dt.from_np(a.dtype), kind="ExternalInput").ap())
    args.append(nc.dram_tensor("out", (NT, P, D), F32, kind="ExternalOutput").ap())
    gps_layer(nc, *args)
    r = run_bass_kernel_spmd(nc, [arrays], core_ids=[0])
    return r.results[0]["out"].reshape(NP, D)[:N]
```
